# Optimizing a Trainium2 kernel written in Bass

```python
import numpy as np
import jax
import jax.numpy as jnp

def _softmax(x, axis=-1):
    return jax.nn.softmax(x, axis=axis)

def _gelu(x):
    return jax.nn.gelu(x, approximate=True)

def _silu(x):
    return jax.nn.silu(x)

def _sigmoid(x):
    return jax.nn.sigmoid(x)

def _layernorm(x, axis=-1, eps=1e-05):
    m = jnp.mean(x, axis=axis, keepdims=True)
    v = jnp.var(x, axis=axis, keepdims=True)
    return (x - m) / jnp.sqrt(v + eps)

def _scatter_add(tgt, idx, src, axis=0):
    return tgt.at[idx].add(src)

def _segment_sum(src, seg, n):
    return jax.ops.segment_sum(src, seg, n)
kernel_name = 'mk_xattn_ffn_d2_seqx_r8_4f112a'

def setup_inputs(seed: int=0):
    np.random.seed(seed)
    _w = jnp.asarray

    def _rec_inputs():
        import jax
        import jax.numpy as jnp
        _rk = jax.random.key(seed)
        x = -0.0002928 + 1 * jax.random.normal(jax.random.fold_in(_rk, 1), (32, 128, 128), jnp.float32)
        _lenS = 128 - jax.random.randint(jax.random.fold_in(_rk, 7), (32,), 0, max(1, 128 // 4) + 1, jnp.int32)
        _lenS2 = 120 - jax.random.randint(jax.random.fold_in(_rk, 8), (32,), 0, max(1, 120 // 4) + 1, jnp.int32)
        _ctx_1024P = jax.random.normal(jax.random.fold_in(_rk, 11), (32, 16, 128), jnp.float32)
        _ctx_1024c = jax.random.dirichlet(jax.random.fold_in(_rk, 511), 0.3 * jnp.ones((16,), jnp.float32), (32, 120))
        _ctx_1024t = jnp.einsum('bsk,bkd->bsd', _ctx_1024c, _ctx_1024P)
        _ctx_1024t = _ctx_1024t * jax.lax.rsqrt(jnp.mean(jnp.square(_ctx_1024t)) + 1e-12) * 0.953939
        ctx_1024 = -1.39393e-06 + 0.999914 * (_ctx_1024t + 0.3 * jax.random.normal(jax.random.fold_in(_rk, 611), (32, 120, 128), jnp.float32))
        return (x, ctx_1024)
    x, ctx_1024 = _rec_inputs()

    def _L0_xattn_setup():
        import jax, jax.numpy as jnp
        import numpy as np
        INPUT_DIM = 128
        HIDDEN_DIM = 128
        NUM_HEADS = 16
        HEAD_DIM = HIDDEN_DIM // NUM_HEADS

        def _layernorm(x, gamma, beta, eps=1e-05):
            mu = jnp.mean(x, axis=-1, keepdims=True)
            var = jnp.var(x, axis=-1, keepdims=True)
            return (x - mu) * jax.lax.rsqrt(var + eps) * gamma + beta
        key = jax.random.key(seed)
        ks = jax.random.split(key, 12)
        s = 1.0 / np.sqrt(INPUT_DIM)
        so = 1.0 / np.sqrt(HIDDEN_DIM)
        return {'x1': jax.random.normal(ks[0], (2, 256, INPUT_DIM), dtype=jnp.float32), 'x2': jax.random.normal(ks[1], (2, 256, INPUT_DIM), dtype=jnp.float32), 'Wq': jax.random.uniform(ks[2], (INPUT_DIM, HIDDEN_DIM), minval=-s, maxval=s, dtype=jnp.float32), 'bq': jnp.zeros((HIDDEN_DIM,), jnp.float32), 'Wk': jax.random.uniform(ks[3], (INPUT_DIM, HIDDEN_DIM), minval=-s, maxval=s, dtype=jnp.float32), 'bk': jnp.zeros((HIDDEN_DIM,), jnp.float32), 'Wv': jax.random.uniform(ks[4], (INPUT_DIM, HIDDEN_DIM), minval=-s, maxval=s, dtype=jnp.float32), 'bv': jnp.zeros((HIDDEN_DIM,), jnp.float32), 'gq': jnp.ones((HIDDEN_DIM,), jnp.float32), 'betq': jnp.zeros((HIDDEN_DIM,), jnp.float32), 'gk': jnp.ones((HIDDEN_DIM,), jnp.float32), 'betk': jnp.zeros((HIDDEN_DIM,), jnp.float32), 'gv': jnp.ones((HIDDEN_DIM,), jnp.float32), 'betv': jnp.zeros((HIDDEN_DIM,), jnp.float32), 'Wo': jax.random.uniform(ks[5], (HIDDEN_DIM, INPUT_DIM), minval=-so, maxval=so, dtype=jnp.float32), 'bo': jnp.zeros((INPUT_DIM,), jnp.float32)}
    _L0_xattn_all = _L0_xattn_setup()
    _L0_xattn_in = {k: v for k, v in _L0_xattn_all.items() if k in ('Wq', 'bq', 'Wk', 'bk', 'Wv', 'bv', 'gq', 'betq', 'gk', 'betk', 'gv', 'betv', 'Wo', 'bo')}
    del _L0_xattn_all

    def _L0_ffn_setup():
        import jax, jax.numpy as jnp
        import numpy as np
        B, S, D, F, E, K = (4, 256, 128, 512, 8, 2)
        key = jax.random.key(seed)
        ks = jax.random.split(key, 8)
        x = jax.random.normal(ks[0], (B, S, D), dtype=jnp.float32)
        router_w = jax.random.normal(ks[1], (E, D), dtype=jnp.float32) * 0.02
        w1_w = jax.random.normal(ks[2], (E, F, D), dtype=jnp.float32) * 0.02
        w1_b = jax.random.normal(ks[3], (E, F), dtype=jnp.float32) * 0.02
        w2_w = jax.random.normal(ks[4], (E, D, F), dtype=jnp.float32) * 0.02
        w2_b = jax.random.normal(ks[5], (E, D), dtype=jnp.float32) * 0.02
        wg_w = jax.random.normal(ks[6], (E, F, D), dtype=jnp.float32) * 0.02
        wg_b = jax.random.normal(ks[7], (E, F), dtype=jnp.float32) * 0.02
        return {'x': x, 'router_w': router_w, 'w1_w': w1_w, 'w1_b': w1_b, 'w2_w': w2_w, 'w2_b': w2_b, 'wg_w': wg_w, 'wg_b': wg_b}
    _L0_ffn_all = _L0_ffn_setup()
    _L0_ffn_in = {k: v for k, v in _L0_ffn_all.items() if k in ('router_w', 'w1_w', 'w1_b', 'w2_w', 'w2_b', 'wg_w', 'wg_b')}
    del _L0_ffn_all

    def _L1_xattn_setup():
        import jax, jax.numpy as jnp
        import numpy as np
        C = 128
        B, SQ, SKV = (4, 256, 256)
        key = jax.random.key(seed)
        ks = jax.random.split(key, 10)
        s = 1.0 / np.sqrt(C)
        return {'x': jax.random.normal(ks[0], (B, SQ, C), jnp.float32), 'content_embeddings': jax.random.normal(ks[1], (B, SKV, C), jnp.float32), 'Wq': jax.random.normal(ks[2], (C, C), jnp.float32) * s, 'bq': jnp.zeros((C,), jnp.float32), 'Wk': jax.random.normal(ks[3], (C, C), jnp.float32) * s, 'bk': jnp.zeros((C,), jnp.float32), 'Wv': jax.random.normal(ks[4], (C, C), jnp.float32) * s, 'bv': jnp.zeros((C,), jnp.float32), 'Wo': jax.random.normal(ks[5], (C, C), jnp.float32) * s, 'bo': jnp.zeros((C,), jnp.float32)}
    _L1_xattn_all = _L1_xattn_setup()
    _L1_xattn_in = {k: v for k, v in _L1_xattn_all.items() if k in ('Wq', 'bq', 'Wk', 'bk', 'Wv', 'bv', 'Wo', 'bo')}
    del _L1_xattn_all

    def _L1_ffn_setup():
        import jax, jax.numpy as jnp
        import numpy as np
        TOP_K = 8
        key = jax.random.key(seed)
        ks = jax.random.split(key, 6)
        B, S, D, F, E = (2, 128, 128, 64, 64)
        x = jax.random.normal(ks[0], (B, S, D), dtype=jnp.float32)
        centroids = jax.random.normal(ks[1], (E, D), dtype=jnp.float32) * 0.05
        expert_biases = jnp.zeros((E,), dtype=jnp.float32)
        Ws_up = jax.random.normal(ks[2], (D, F), dtype=jnp.float32) / np.sqrt(D)
        Ws_down = jax.random.normal(ks[3], (F, D), dtype=jnp.float32) / np.sqrt(F)
        W_up = jax.random.normal(ks[4], (E, D, F), dtype=jnp.float32) / np.sqrt(D)
        W_down = jax.random.normal(ks[5], (E, F, D), dtype=jnp.float32) / np.sqrt(F)
        return {'x': x, 'centroids': centroids, 'expert_biases': expert_biases, 'Ws_up': Ws_up, 'Ws_down': Ws_down, 'W_up': W_up, 'W_down': W_down}
    _L1_ffn_all = _L1_ffn_setup()
    _L1_ffn_in = {k: v for k, v in _L1_ffn_all.items() if k in ('centroids', 'expert_biases', 'Ws_up', 'Ws_down', 'W_up', 'W_down')}
    del _L1_ffn_all
    return {'x': x, 'ctx_1024': ctx_1024, 'L0_xattn_Wq': _L0_xattn_in['Wq'], 'L0_xattn_bq': _L0_xattn_in['bq'], 'L0_xattn_Wk': _L0_xattn_in['Wk'], 'L0_xattn_bk': _L0_xattn_in['bk'], 'L0_xattn_Wv': _L0_xattn_in['Wv'], 'L0_xattn_bv': _L0_xattn_in['bv'], 'L0_xattn_gq': _L0_xattn_in['gq'], 'L0_xattn_betq': _L0_xattn_in['betq'], 'L0_xattn_gk': _L0_xattn_in['gk'], 'L0_xattn_betk': _L0_xattn_in['betk'], 'L0_xattn_gv': _L0_xattn_in['gv'], 'L0_xattn_betv': _L0_xattn_in['betv'], 'L0_xattn_Wo': _L0_xattn_in['Wo'], 'L0_xattn_bo': _L0_xattn_in['bo'], 'L0_ffn_router_w': _L0_ffn_in['router_w'], 'L0_ffn_w1_w': _L0_ffn_in['w1_w'], 'L0_ffn_w1_b': _L0_ffn_in['w1_b'], 'L0_ffn_w2_w': _L0_ffn_in['w2_w'], 'L0_ffn_w2_b': _L0_ffn_in['w2_b'], 'L0_ffn_wg_w': _L0_ffn_in['wg_w'], 'L0_ffn_wg_b': _L0_ffn_in['wg_b'], 'L1_xattn_Wq': _L1_xattn_in['Wq'], 'L1_xattn_bq': _L1_xattn_in['bq'], 'L1_xattn_Wk': _L1_xattn_in['Wk'], 'L1_xattn_bk': _L1_xattn_in['bk'], 'L1_xattn_Wv': _L1_xattn_in['Wv'], 'L1_xattn_bv': _L1_xattn_in['bv'], 'L1_xattn_Wo': _L1_xattn_in['Wo'], 'L1_xattn_bo': _L1_xattn_in['bo'], 'L1_ffn_centroids': _L1_ffn_in['centroids'], 'L1_ffn_expert_biases': _L1_ffn_in['expert_biases'], 'L1_ffn_Ws_up': _L1_ffn_in['Ws_up'], 'L1_ffn_Ws_down': _L1_ffn_in['Ws_down'], 'L1_ffn_W_up': _L1_ffn_in['W_up'], 'L1_ffn_W_down': _L1_ffn_in['W_down']}

def reference(x, ctx_1024, L0_xattn_Wq, L0_xattn_bq, L0_xattn_Wk, L0_xattn_bk, L0_xattn_Wv, L0_xattn_bv, L0_xattn_gq, L0_xattn_betq, L0_xattn_gk, L0_xattn_betk, L0_xattn_gv, L0_xattn_betv, L0_xattn_Wo, L0_xattn_bo, L0_ffn_router_w, L0_ffn_w1_w, L0_ffn_w1_b, L0_ffn_w2_w, L0_ffn_w2_b, L0_ffn_wg_w, L0_ffn_wg_b, L1_xattn_Wq, L1_xattn_bq, L1_xattn_Wk, L1_xattn_bk, L1_xattn_Wv, L1_xattn_bv, L1_xattn_Wo, L1_xattn_bo, L1_ffn_centroids, L1_ffn_expert_biases, L1_ffn_Ws_up, L1_ffn_Ws_down, L1_ffn_W_up, L1_ffn_W_down):
    import jax
    import jax.numpy as jnp

    def _L0_xattn_ref(x1, x2, Wq, bq, Wk, bk, Wv, bv, gq, betq, gk, betk, gv, betv, Wo, bo):
        import jax, jax.numpy as jnp
        import numpy as np
        INPUT_DIM = 128
        HIDDEN_DIM = 128
        NUM_HEADS = 16
        HEAD_DIM = HIDDEN_DIM // NUM_HEADS

        def _layernorm(x, gamma, beta, eps=1e-05):
            mu = jnp.mean(x, axis=-1, keepdims=True)
            var = jnp.var(x, axis=-1, keepdims=True)
            return (x - mu) * jax.lax.rsqrt(var + eps) * gamma + beta
        B, S1, _ = x1.shape
        S2 = x2.shape[1]
        q = _layernorm(x1 @ Wq + bq, gq, betq)
        k = _layernorm(x2 @ Wk + bk, gk, betk)
        v = _layernorm(x2 @ Wv + bv, gv, betv)
        q = q.reshape(B, S1, NUM_HEADS, HEAD_DIM)
        k = k.reshape(B, S2, NUM_HEADS, HEAD_DIM)
        v = v.reshape(B, S2, NUM_HEADS, HEAD_DIM)
        scores = jnp.einsum('bqhd,bkhd->bhqk', q, k) / np.sqrt(HEAD_DIM).astype(np.float32)
        attn = jax.nn.softmax(scores, axis=-1)
        out = jnp.einsum('bhqk,bkhd->bqhd', attn, v).reshape(B, S1, NUM_HEADS * HEAD_DIM)
        return out @ Wo + bo

    def _L0_ffn_ref(x, router_w, w1_w, w1_b, w2_w, w2_b, wg_w, wg_b):
        import jax, jax.numpy as jnp
        import numpy as np
        B, S, D, F, E, K = (4, 256, 128, 512, 8, 2)
        probs = jax.nn.softmax(jnp.einsum('bsd,ed->bse', x, router_w), axis=-1)
        token_probs, probs_idx = jax.lax.top_k(probs, K)
        gates = jnp.sum(token_probs[..., None] * jax.nn.one_hot(probs_idx, E, dtype=x.dtype), axis=-2)
        gates_e = jnp.moveaxis(gates, -1, 0)

        def body(acc, params):
            w1w, w1b, w2w, w2b, wgw, wgb, g = params
            y = jax.nn.gelu(jnp.einsum('bsd,fd->bsf', x, wgw) + wgb, approximate=False)
            h = y * (jnp.einsum('bsd,fd->bsf', x, w1w) + w1b)
            out = jnp.einsum('bsf,df->bsd', h, w2w) + w2b
            return (acc + out * g[..., None], None)
        acc0 = jnp.zeros_like(x)
        out, _ = jax.lax.scan(body, acc0, (w1_w, w1_b, w2_w, w2_b, wg_w, wg_b, gates_e))
        return out

    def _L1_xattn_ref(x, content_embeddings, Wq, bq, Wk, bk, Wv, bv, Wo, bo):
        import jax, jax.numpy as jnp
        import numpy as np
        C = 128
        B, SQ, SKV = (4, 256, 256)
        queries = x @ Wq.T + bq
        keys = content_embeddings @ Wk.T + bk
        values = content_embeddings @ Wv.T + bv
        scale = 1.0 / jnp.sqrt(jnp.asarray(C, x.dtype))
        scores = jnp.einsum('bqc,bkc->bqk', queries, keys) * scale
        attn = jax.nn.softmax(scores, axis=-1)
        attended = jnp.einsum('bqk,bkc->bqc', attn, values)
        out = x + attended
        return out @ Wo.T + bo

    def _L1_ffn_ref(x, centroids, expert_biases, Ws_up, Ws_down, W_up, W_down):
        import jax, jax.numpy as jnp
        import numpy as np
        TOP_K = 8
        B, S, D = x.shape
        E = centroids.shape[0]
        T = B * S
        xf = x.reshape(T, D)
        shared = jax.nn.silu(xf @ Ws_up) @ Ws_down
        aff = xf @ centroids.T
        biased = aff + expert_biases
        _, idx = jax.lax.top_k(biased, TOP_K)
        sel = jnp.take_along_axis(aff, idx, axis=1)
        w = jax.nn.sigmoid(sel)
        w = w / (jnp.sum(w, axis=-1, keepdims=True) + 1e-08)
        cw = jnp.zeros((T, E), dtype=x.dtype).at[jnp.arange(T)[:, None], idx].add(w)
        h = jax.nn.silu(jnp.einsum('td,edf->etf', xf, W_up))
        y = jnp.einsum('etf,efd->etd', h, W_down)
        routed = jnp.einsum('etd,te->td', y, cw)
        return (shared + routed).reshape(B, S, D)
    x = x + _L0_xattn_ref(_layernorm(x, axis=-1), ctx_1024, L0_xattn_Wq, L0_xattn_bq, L0_xattn_Wk, L0_xattn_bk, L0_xattn_Wv, L0_xattn_bv, L0_xattn_gq, L0_xattn_betq, L0_xattn_gk, L0_xattn_betk, L0_xattn_gv, L0_xattn_betv, L0_xattn_Wo, L0_xattn_bo)
    x = x + _L0_ffn_ref(_layernorm(x, axis=-1), L0_ffn_router_w, L0_ffn_w1_w, L0_ffn_w1_b, L0_ffn_w2_w, L0_ffn_w2_b, L0_ffn_wg_w, L0_ffn_wg_b)
    x = x + _L1_xattn_ref(_layernorm(x, axis=-1), ctx_1024, L1_xattn_Wq, L1_xattn_bq, L1_xattn_Wk, L1_xattn_bk, L1_xattn_Wv, L1_xattn_bv, L1_xattn_Wo, L1_xattn_bo)
    x = x + _L1_ffn_ref(_layernorm(x, axis=-1), L1_ffn_centroids, L1_ffn_expert_biases, L1_ffn_Ws_up, L1_ffn_Ws_down, L1_ffn_W_up, L1_ffn_W_down)
    return x

_drawn_inputs = setup_inputs


def setup_inputs(seed=0):
    import zlib

    import numpy as np

    out = dict(_drawn_inputs(seed))
    spreads = {'L0_xattn_bq': (0.0, 0.1),
     'L0_xattn_bk': (0.0, 0.768),
     'L0_xattn_bv': (0.0, 0.1),
     'L0_xattn_gq': (1.0, 0.2),
     'L0_xattn_betq': (0.0, 0.427),
     'L0_xattn_gk': (1.0, 0.2),
     'L0_xattn_betk': (0.0, 2.0),
     'L0_xattn_gv': (1.0, 0.2),
     'L0_xattn_betv': (0.0, 0.1),
     'L0_xattn_bo': (0.0, 0.1),
     'L1_xattn_bq': (0.0, 1.402),
     'L1_xattn_bk': (0.0, 2.0),
     'L1_xattn_bv': (0.0, 0.343),
     'L1_xattn_bo': (0.0, 0.347),
     'L1_ffn_expert_biases': (0.0, 0.372)}
    factors = {'L0_ffn_router_w': 5.571,
     'L0_ffn_w1_w': 8.0,
     'L0_ffn_w1_b': 8.0,
     'L0_ffn_w2_w': 8.0,
     'L0_ffn_w2_b': 21.992,
     'L0_ffn_wg_w': 8.0,
     'L0_ffn_wg_b': 8.0}
    for name, (base, spread) in spreads.items():
        noise = np.random.default_rng([zlib.crc32(name.encode()), seed]).standard_normal(out[name].shape)
        drawn = base * np.exp(spread * noise) if base else spread * noise
        out[name] = jnp.asarray(drawn.astype(out[name].dtype))
    for name, factor in factors.items():
        out[name] = (out[name] * factor).astype(out[name].dtype)
    return out
```

```python
import concourse.bass as bass
from concourse import mybir
from contextlib import ExitStack

F32 = mybir.dt.float32
F16 = mybir.dt.float16
I32 = mybir.dt.int32
ALU = mybir.AluOpType
ACT = mybir.ActivationFunctionType
AX = mybir.AxisListType.X
ds = bass.ds

P = 128
NB = 32
NK = 120
H = 16
HD = P // H
HG = 4
E0, F0 = 8, 512
FC = F0 // P
E1, F1 = 64, 64
NFT = E1 * F1 // P
EPS = 1e-5
REGION = NB * P + P
NT = 2 * NB + E0
ZERO_ROW = E0 * REGION
LOTS = 4
NG = NB // LOTS

C_ID, C_TRI, C_ONE, C_MASK, C_LT, C_K, C_RUN, C_P, C_J, C_END = 0, 128, 256, 384, 388, 452, 468, 476, 477, 477 + NT
GQ, BQN, GK, BKN, GV, BVN, BQ1, BK1, N_COL = 0, 1, 2, 3, 4, 5, 6, 7, 8
R_QKV, R_BO0, R_EB, R_BO1, R_END = 0, 512, 640, 704, 832


class Shared:
    pass


def bcast(ap, *shape):
    return ap.to_broadcast(list(shape))


class Steps:

    def __init__(self, eng, sem, per, b):
        self.eng, self.sem, self.first, self.done = eng, sem, b * per, 0

    def __call__(self, instruction):
        instruction.then_inc(self.sem, 1)
        self.done += 1

    def wait(self):
        self.eng.wait_ge(self.sem, self.first + self.done)

    def wait_apart(self, g):
        wait_apart(g, self.eng, self.sem, self.first + self.done)


def wait_apart(g, eng, sem, value):
    eng.wait_ge(sem, value)
    if not isinstance(value, int):
        eng.sem_inc(g.apart[eng], 1)


def wait_free(eng, sem, b, back, per=1, apart=None):
    if isinstance(b, int) and b < back:
        return
    if apart is None:
        eng.wait_ge(sem, (b - back) * per + per)
    else:
        wait_apart(apart, eng, sem, (b - back) * per + per)


def pipeline(eng, stages, n, lead):
    def step(half, parity):
        for k, stage in reversed(list(enumerate(stages))):
            if stage is None:
                continue
            h, p = half + (parity - k) // 2, (parity - k) % 2
            if isinstance(half, int) and not 0 <= 2 * h + p < n:
                continue
            stage(h, p)
    for t in range(lead):
        step(t // 2, t % 2)
    with eng.Fori(lead // 2, n // 2) as half:
        for parity in range(2):
            step(half, parity)
    for t in range(n, n + len(stages) - 1):
        step(t // 2, t % 2)


def load(nc, g):
    with ExitStack() as ctx:
        zeroed = ctx.enter_context(nc.semaphore("zeroed"))
        loaded = ctx.enter_context(nc.semaphore("loaded"))
        consts_in = ctx.enter_context(nc.semaphore("consts_in"))
        block = ctx.enter_context(nc.Block())

        @block.gpsimd
        def _(pool):
            nc.gpsimd.memset(g.zeros[:, :], 0.0).then_inc(zeroed, 1)
            nc.gpsimd.memset(g.cstage[:, :, :], 0.0).then_inc(zeroed, 1)
            nc.gpsimd.memset(g.vaug[:, :, :, :], 1.0).then_inc(zeroed, 1)
            nc.gpsimd.memset(g.mhalf[:, :], -0.5).then_inc(zeroed, 1)
            pool.wait_ge(zeroed, 4)

        @block.sync
        def _(sp):
            n = 0
            sp.dma_start(g.consts[:, :], g.d_consts).then_inc(consts_in, 16)
            for to, of in ((g.cols[:, :], g.d_cols), (g.w_ctx[:, :], g.d_w_ctx),
                           (g.rows[:, :], g.d_rows.partition_broadcast(P)), (g.w_small[:, :], g.d_w_small)):
                sp.dma_start(to, of).then_inc(loaded, 16)
                n += 16
            for i in range(4):
                sp.dma_start(g.X[:, 8 * i:8 * i + 8, :], g.d_x[8 * i:8 * i + 8].rearrange("b p d -> p b d")).then_inc(loaded, 16)
                n += 16
            sp.wait_ge(zeroed, 1)
            sp.dma_start(g.xs[ZERO_ROW:ZERO_ROW + P, :], g.zeros[:, :]).then_inc(loaded, 16)
            sp.wait_ge(loaded, n + 16)
            sp.wait_ge(consts_in, 16)

        @block.vector
        def _(dve):
            dve.wait_ge(consts_in, 16)
            nc.vector.tensor_copy(g.run[:, :], g.consts[:, C_RUN:C_RUN + E0])


def attention0(nc, g):
    with ExitStack() as ctx:
        def sb(name, shape, dt=F32):
            return ctx.enter_context(nc.sbuf_tensor(name, shape, dt))

        def sem(name):
            return ctx.enter_context(nc.semaphore(name))

        st6, mv, ve, rstd = sb("st6", [P, 2, 6]), sb("mv", [P, 2, 2]), sb("ve", [P, 2, 1]), sb("rstd", [P, 2, 1])
        xn, xcT = sb("xn", [P, 2, P]), sb("xcT", [P, 2, 2 * P])
        qkv = sb("qkv", [P, 2, 4 * P])
        st18, mv3, ve3, rstd3 = sb("st18", [P, 2, 3, 6]), sb("mv3", [P, 2, 3, 2]), sb("ve3", [P, 2, 3]), sb("rstd3", [P, 2, 3])
        qkn = sb("qkn", [P, 2, 2 * P])
        qT, kT, kbd = sb("qT", [P, 2, P]), sb("kT", [P, 2, NK]), sb("kbd", [P, 2, HG * NK])
        mx, prob, pT = sb("mx", [P, 2, H]), sb("prob", [P, 2, H * NK]), sb("pT", [P, 2, H * P])
        rs, o, oT = sb("rs", [P, 2, H]), sb("o", [P, 2, P]), sb("oT", [P, 2, P])
        st1, mv1, ve1, rstd1 = sb("st1", [P, 2, 6]), sb("mv1", [P, 2, 2]), sb("ve1", [P, 2, 1]), sb("rstd1", [P, 2, 1])
        xn1, xn1T = sb("xn1", [P, 2, P]), sb("xn1T", [P, 2, P])
        lmax, lg, ex, esum, erec, pr = (sb("lmax", [P, 2, 1]), sb("lg", [P, 2, E0]), sb("ex", [P, 2, E0]), sb("esum", [P, 2, 1]),
                                        sb("erec", [P, 2, 1]), sb("pr", [P, 2, E0]))
        gt, eq, rank = sb("gt", [P, 2, E0 * E0]), sb("eq", [P, 2, E0 * E0]), sb("rank", [P, 2, E0])
        chosen, picked = sb("chosen", [P, 2, 2 * E0]), sb("picked", [P, 2, E0])
        place, tmp, slotf, slot = (sb("place", [P, 2, E0]), sb("tmp", [P, 2, 2 * E0]), sb("slotf", [P, 2, 2]), sb("slot", [P, 2, 2], I32))
        tmp2 = sb("tmp2", [P, 2, 2 * E0])

        psA, psB = g.bank[0], g.bank[1]
        psS = g.psum[:, 2:6, :]
        psT = g.psum[:, 6:8, :]

        ctx_in = [sem("ctx_in_even"), sem("ctx_in_odd")]
        scattered = [sem("scattered_even"), sem("scattered_odd")]
        x_stats, x_var, x_rstd, xn_ready = sem("x_stats"), sem("x_var"), sem("x_rstd"), sem("xn_ready")
        xc_turned, xcT_ready, ctxT_kept, projected = sem("xc_turned"), sem("xcT_ready"), sem("ctxT_kept"), sem("projected")
        qkv_ready, qkv_stats, qkv_var, qkv_rstd, v1_kept = sem("qkv_ready"), sem("qkv_stats"), sem("qkv_var"), sem("qkv_rstd"), sem("v1_kept")
        qkn_ready, qk_turned, kT_ready, kbd_ready = sem("qkn_ready"), sem("qk_turned"), sem("kT_ready"), sem("kbd_ready")
        scores_ready, max_ready, shifted, exp_ready = sem("scores_ready"), sem("max_ready"), sem("shifted"), sem("exp_ready")
        p_turned, pT_act, pT_dve, pv_ready = sem("p_turned"), sem("pT_act"), sem("pT_dve"), sem("pv_ready")
        rs_ready, o_ready, o_turned, oT_ready, y_ready = sem("rs_ready"), sem("o_ready"), sem("o_turned"), sem("oT_ready"), sem("y_ready")
        bo_added, x1_ready, x1_stats, x1_var, x1_rstd = sem("bo_added"), sem("x1_ready"), sem("x1_stats"), sem("x1_var"), sem("x1_rstd")
        xn1_ready, xn1_turned, xn1T_ready, logits_ready = sem("xn1_ready"), sem("xn1_turned"), sem("xn1T_ready"), sem("logits_ready")
        shift_steps, lg_exp, rank_steps, picked_ready = sem("shift_steps"), sem("lg_exp"), sem("rank_steps"), sem("picked_ready")
        counted, place_steps, routed = sem("counted"), sem("place_steps"), sem("routed")

        block = ctx.enter_context(nc.Block())

        @block.sync
        def _(sp):
            def load_ctx(h, p):
                wait_free(sp, xc_turned, 2 * h + p, 2)
                sp.dma_start(g.cstage[0:NK, p, :], g.d_ctx[ds(2 * h + p, 1), :, :].rearrange("b k d -> (b k) d")).then_inc(ctx_in[p], 16)
            pipeline(sp, [load_ctx], NB, 2)

        @block.gpsimd
        def _(pool):
            def power(out, var_eps, var, n):
                return var_eps, var, out, n

            def rstd_of(var, var_eps, out, n, b, steps, sem_ready):
                st = Steps(pool, steps, 1, b)
                st(nc.gpsimd.tensor_scalar(var_eps, var, EPS, None, ALU.add))
                st.wait()
                nc.gpsimd.tensor_tensor(out, var_eps, g.mhalf[:, 0:n], ALU.pow).then_inc(sem_ready, 1)

            def stage_x(h, p):
                b = 2 * h + p
                wait_apart(g, pool, x_stats, 2 * b + 2)
                wait_free(pool, xn_ready, b, 2, apart=g)
                rstd_of(mv[:, p, 1:2], ve[:, p, :], rstd[:, p, :], 1, b, x_var, x_rstd)

            def stage_q(h, p):
                b = 2 * h + p
                pool.wait_ge(xcT_ready, b + 1)
                nc.gpsimd.tensor_copy(g.ctxT[:, ds(b, 1), :].rearrange("p a k -> p (a k)"), xcT[:, p, P:P + NK]).then_inc(ctxT_kept, 1)
                wait_apart(g, pool, qkv_stats, 6 * b + 6)
                wait_free(pool, qkn_ready, b, 2, 3, apart=g)
                rstd_of(mv3[:, p, :, 1:2].rearrange("p a c -> p (a c)"), ve3[:, p, :], rstd3[:, p, :], 3, b, qkv_var, qkv_rstd)
                nc.gpsimd.tensor_copy(g.V1[:, ds(b, 1), :].rearrange("p a k -> p (a k)"), qkv[:, p, 3 * P:4 * P]).then_inc(v1_kept, 1)
                pool.wait_ge(kT_ready, 2 * b + 2)
                wait_free(pool, scores_ready, b, 2)
                nc.gpsimd.tensor_tensor(kbd[:, p, :].rearrange("p (j k) -> p j k", j=HG),
                                        bcast(kT[:, p, :].unsqueeze(1), P, HG, NK),
                                        bcast(g.consts[:, C_MASK:C_MASK + HG].unsqueeze(2), P, HG, NK), ALU.mult).then_inc(kbd_ready, 1)

            def stage_bo(h, p):
                b = 2 * h + p
                pool.wait_ge(xn_ready, b + 1)
                xb = g.X[:, ds(b, 1), :].rearrange("p a d -> p (a d)")
                nc.gpsimd.tensor_tensor(xb, xb, g.rows[:, R_BO0:R_BO0 + P], ALU.add).then_inc(bo_added, 1)

            def stage_x1(h, p):
                b = 2 * h + p
                wait_apart(g, pool, x1_stats, 2 * b + 2)
                wait_free(pool, xn1_ready, b, 2, apart=g)
                rstd_of(mv1[:, p, 1:2], ve1[:, p, :], rstd1[:, p, :], 1, b, x1_var, x1_rstd)

            def stage_scatter(h, p):
                b = 2 * h + p
                wait_apart(g, pool, routed, b + 1)
                for c in range(2):
                    nc.gpsimd.indirect_dma_start(g.xs[:, :], bass.IndirectOffsetOnAxis(slot[:, p, c:c + 1], 0),
                                                 xn1[:, p, :], None).then_inc(scattered[p], 16)

            pipeline(pool, [stage_x, stage_q, stage_bo, stage_x1, stage_scatter], NB, 6)
            for p in range(2):
                pool.wait_ge(scattered[p], 32 * (NB // 2))

        @block.vector
        def _(dve):
            V = nc.vector

            def stage_stats(h, p):
                b = 2 * h + p
                wait_free(dve, xn_ready, b, 2, apart=g)
                wait_free(dve, x_rstd, b, 2, apart=g)
                st = Steps(dve, x_stats, 2, b)
                st(V.bn_stats(st6[:, p, :], g.X[:, ds(b, 1), :].rearrange("p a d -> p (a d)")))
                st.wait_apart(g)
                st(V.bn_aggr(mv[:, p, :], st6[:, p, :]))

            def stage_norm(h, p):
                b = 2 * h + p
                dve.wait_ge(x_rstd, b + 1)
                wait_free(dve, xc_turned, b, 2)
                V.tensor_scalar(xn[:, p, :], g.X[:, ds(b, 1), :].rearrange("p a d -> p (a d)"), mv[:, p, 0:1], rstd[:, p, :],
                                ALU.subtract, ALU.mult).then_inc(xn_ready, 1)

            def stage_q(h, p):
                b = 2 * h + p
                dve.wait_ge(projected, b + 1)
                wait_free(dve, qkn_ready, b, 2, 3)
                wait_free(dve, v1_kept, b, 2)
                V.tensor_tensor(qkv[:, p, :], psA[:, 0:4 * P], g.rows[:, R_QKV:R_QKV + 4 * P], ALU.add).then_inc(qkv_ready, 1)
                wait_free(dve, qkv_rstd, b, 2, apart=g)
                wait_apart(g, dve, qkv_ready, b + 1)
                st = Steps(dve, qkv_stats, 6, b)
                for i in range(3):
                    st(V.bn_stats(st18[:, p, i, :], qkv[:, p, P * i:P * i + P]))
                st.wait_apart(g)
                for i in range(3):
                    st(V.bn_aggr(mv3[:, p, i, :], st18[:, p, i, :]))
                dve.wait_ge(qkv_rstd, b + 1)
                st.wait()
                wait_free(dve, qk_turned, b, 2)
                for i in range(2):
                    V.tensor_scalar(qkn[:, p, P * i:P * i + P], qkv[:, p, P * i:P * i + P], mv3[:, p, i, 0:1], rstd3[:, p, i:i + 1],
                                    ALU.subtract, ALU.mult).then_inc(qkn_ready, 1)
                wait_free(dve, pv_ready, b, 2)
                V.tensor_scalar(g.vaug[:, p, :, 0:HD], qkv[:, p, 2 * P:3 * P].rearrange("p (h i) -> p h i", h=H),
                                mv3[:, p, 2, 0:1], rstd3[:, p, 2:3], ALU.subtract, ALU.mult).then_inc(qkn_ready, 1)

            def stage_soft(h, p):
                b = 2 * h + p
                dve.wait_ge(scores_ready, b + 1)
                s = psS[:, :, 0:HG * NK].rearrange("p g (j k) -> p g j k", j=HG)
                V.tensor_reduce(mx[:, p, :].rearrange("p (g j) -> p g j", g=HG), s, AX, ALU.max).then_inc(max_ready, 1)
                dve.wait_ge(max_ready, b + 1)
                wait_free(dve, p_turned, b, 2, 4)
                V.tensor_tensor(prob[:, p, :].rearrange("p (g j k) -> p g j k", g=HG, j=HG), s,
                                bcast(mx[:, p, :].rearrange("p (g j) -> p g j", g=HG).unsqueeze(3), P, HG, HG, NK),
                                ALU.subtract).then_inc(shifted, 1)

            def stage_out(h, p):
                b = 2 * h + p
                for i in range(2):
                    c = 2 * i + 1
                    dve.wait_ge(p_turned, 4 * b + c + 1)
                    wait_free(dve, pv_ready, b, 2)
                    V.tensor_copy(pT[0:NK, p, 4 * P * c:4 * P * c + 4 * P], psT[0:NK, 1, :]).then_inc(pT_dve, 1)
                dve.wait_ge(pv_ready, b + 1)
                av = psB[:, 0:H * (HD + 1)].rearrange("p (h i) -> p h i", h=H)
                V.reciprocal(rs[:, p, :], av[:, :, HD:HD + 1].rearrange("p h i -> p (h i)")).then_inc(rs_ready, 1)
                dve.wait_ge(rs_ready, b + 1)
                wait_free(dve, o_turned, b, 2)
                V.tensor_tensor(o[:, p, :].rearrange("p (h i) -> p h i", h=H), av[:, :, 0:HD],
                                bcast(rs[:, p, :].unsqueeze(2), P, H, HD), ALU.mult).then_inc(o_ready, 1)
                dve.wait_ge(y_ready, b + 1)
                dve.wait_ge(bo_added, b + 1)
                xb = g.X[:, ds(b, 1), :].rearrange("p a d -> p (a d)")
                V.tensor_tensor(xb, psB[:, 3 * P:4 * P], xb, ALU.add).then_inc(x1_ready, 1)
                wait_apart(g, dve, x1_ready, b + 1)
                wait_free(dve, x1_rstd, b, 2, apart=g)
                st = Steps(dve, x1_stats, 2, b)
                st(V.bn_stats(st1[:, p, :], xb))
                st.wait_apart(g)
                st(V.bn_aggr(mv1[:, p, :], st1[:, p, :]))
                dve.wait_ge(x1_rstd, b + 1)
                st.wait()
                half_done = h if p == 0 else h
                if not (isinstance(b, int) and b < 2):
                    dve.wait_ge(scattered[p], 32 * half_done)
                V.tensor_scalar(xn1[:, p, :], xb, mv1[:, p, 0:1], rstd1[:, p, :], ALU.subtract, ALU.mult).then_inc(xn1_ready, 1)

            def stage_route(h, p):
                b = 2 * h + p
                dve.wait_ge(logits_ready, b + 1)
                st = Steps(dve, shift_steps, 2, b)
                st(V.tensor_reduce(lmax[:, p, :], psB[:, 0:E0], AX, ALU.max))
                st.wait()
                st(V.tensor_scalar(lg[:, p, :], psB[:, 0:E0], lmax[:, p, :], None, ALU.subtract))
                dve.wait_ge(lg_exp, b + 1)
                st = Steps(dve, rank_steps, 9, b)
                st(V.reciprocal(erec[:, p, :], esum[:, p, :]))
                st.wait()
                st(V.tensor_scalar(pr[:, p, :], ex[:, p, :], erec[:, p, :], None, ALU.mult))
                st.wait()
                other = bcast(pr[:, p, :].unsqueeze(1), P, E0, E0)
                own = bcast(pr[:, p, :].unsqueeze(2), P, E0, E0)
                gtv, eqv = (x[:, p, :].rearrange("p (e f) -> p e f", e=E0) for x in (gt, eq))
                st(V.tensor_tensor(gtv, other, own, ALU.is_gt))
                st(V.tensor_tensor(eqv, other, own, ALU.is_equal))
                st.wait()
                st(V.tensor_tensor(eq[:, p, :], eq[:, p, :], g.consts[:, C_LT:C_LT + E0 * E0], ALU.mult))
                st.wait()
                st(V.tensor_tensor(gt[:, p, :], gt[:, p, :], eq[:, p, :], ALU.add))
                st.wait()
                st(V.tensor_reduce(rank[:, p, :], gtv, AX, ALU.add))
                st.wait()
                st(V.tensor_tensor(chosen[:, p, :].rearrange("p (c e) -> p c e", c=2), bcast(rank[:, p, :].unsqueeze(1), P, 2, E0),
                                   g.consts[:, C_K:C_K + 2 * E0].rearrange("p (c e) -> p c e", c=2), ALU.is_equal))
                wait_free(dve, counted, b, 2)
                st(V.tensor_scalar(picked[:, p, :], rank[:, p, :], 1.5, None, ALU.is_lt))
                dve.wait_ge(counted, b + 1)
                st.wait()
                st = Steps(dve, place_steps, 6, b)
                st(V.tensor_tensor(place[:, p, :], psB[:, 8:8 + E0], g.run[:, :], ALU.add))
                st.wait()
                st(V.tensor_tensor(g.run[:, :], psB[:, 16:16 + E0], g.run[:, :], ALU.add))
                ch = chosen[:, p, :].rearrange("p (c e) -> p c e", c=2)
                st(V.tensor_tensor(tmp[:, p, :].rearrange("p (c e) -> p c e", c=2), ch, bcast(place[:, p, :].unsqueeze(1), P, 2, E0), ALU.mult))
                st(V.tensor_tensor(tmp2[:, p, :].rearrange("p (c e) -> p c e", c=2), ch, bcast(pr[:, p, :].unsqueeze(1), P, 2, E0), ALU.mult))
                st.wait()
                st(V.tensor_reduce(slotf[:, p, :], tmp[:, p, :].rearrange("p (c e) -> p c e", c=2), AX, ALU.add))
                st(V.tensor_reduce(g.gate[:, ds(b, 1), :].rearrange("p a c -> p (a c)"), tmp2[:, p, :].rearrange("p (c e) -> p c e", c=2), AX, ALU.add))
                st.wait()
                if not (isinstance(b, int) and b < 2):
                    dve.wait_ge(scattered[p], 32 * h)
                V.tensor_copy(g.slotf[:, ds(b, 1), :].rearrange("p a c -> p (a c)"), slotf[:, p, :])
                V.tensor_copy(slot[:, p, :], slotf[:, p, :]).then_inc(routed, 1)

            pipeline(dve, [lambda h, p: (stage_stats(h, p), stage_norm(h, p)), stage_q, stage_soft,
                           lambda h, p: (stage_out(h, p), stage_route(h, p))], NB, 6)

        @block.scalar
        def _(act):
            A = nc.scalar

            def stage_q(h, p):
                b = 2 * h + p
                act.wait_ge(xc_turned, b + 1)
                wait_free(act, projected, b, 2)
                wait_free(act, ctxT_kept, b, 2)
                A.activation(xcT[:, p, :], psA[:, 0:2 * P], ACT.Copy).then_inc(xcT_ready, 1)
                act.wait_ge(qk_turned, b + 1)
                wait_free(act, scores_ready, b, 2)
                wait_free(act, kbd_ready, b, 2)
                A.activation(qT[:, p, :], psA[:, 0:P], ACT.Identity, bias=g.cols[:, BQN:BQN + 1], scale=g.cols[:, GQ:GQ + 1]).then_inc(kT_ready, 1)
                A.activation(kT[:, p, :], psA[:, P:P + NK], ACT.Identity, bias=g.cols[:, BKN:BKN + 1], scale=g.cols[:, GK:GK + 1]).then_inc(kT_ready, 1)

            def stage_soft(h, p):
                b = 2 * h + p
                act.wait_ge(shifted, b + 1)
                A.activation(prob[:, p, :], prob[:, p, :], ACT.Exp, scale=float(HD) ** -0.5).then_inc(exp_ready, 1)

            def stage_out(h, p):
                b = 2 * h + p
                for i in range(2):
                    c = 2 * i
                    act.wait_ge(p_turned, 4 * b + c + 1)
                    wait_free(act, pv_ready, b, 2)
                    A.activation(pT[0:NK, p, 4 * P * c:4 * P * c + 4 * P], psT[0:NK, 0, :], ACT.Copy).then_inc(pT_act, 1)
                act.wait_ge(o_turned, b + 1)
                wait_free(act, y_ready, b, 2)
                A.activation(oT[:, p, :], psB[:, 2 * P:3 * P], ACT.Identity, bias=g.cols[:, BVN:BVN + 1], scale=g.cols[:, GV:GV + 1]).then_inc(oT_ready, 1)
                act.wait_ge(xn1_turned, b + 1)
                wait_free(act, logits_ready, b, 2)
                A.activation(xn1T[:, p, :], psB[:, P:2 * P], ACT.Copy).then_inc(xn1T_ready, 1)
                act.wait_ge(shift_steps, 2 * b + 2)
                wait_free(act, rank_steps, b, 2, 9)
                A.activation(ex[:, p, :], lg[:, p, :], ACT.Exp, accum_out=esum[:, p, :]).then_inc(lg_exp, 1)

            pipeline(act, [None, stage_q, stage_soft, stage_out], NB, 6)

        @block.tensor
        def _(pe):
            T = nc.tensor
            ident = g.consts[:, C_ID:C_ID + P]

            def stage_q(h, p):
                b = 2 * h + p
                wait_free(pe, kT_ready, b, 1, 2)
                pe.wait_ge(xn_ready, b + 1)
                pe.wait_ge(ctx_in[p], 16 * h + 16)
                T.transpose(psA[:, 0:P], xn[:, p, :], ident)
                T.transpose(psA[:, P:2 * P], g.cstage[:, p, :], ident).then_inc(xc_turned, 1)
                pe.wait_ge(xcT_ready, b + 1)
                T.matmul(psA[:, 0:P], xcT[:, p, 0:P], g.w_ctx[:, 0:P], start=True, stop=True)
                T.matmul(psA[:, P:4 * P], xcT[:, p, P:2 * P], g.w_ctx[:, P:4 * P], start=True, stop=True).then_inc(projected, 1)
                pe.wait_ge(qkn_ready, 3 * b + 2)
                T.transpose(psA[:, 0:P], qkn[:, p, 0:P], ident)
                T.transpose(psA[:, P:2 * P], qkn[:, p, P:2 * P], ident).then_inc(qk_turned, 1)

            def stage_soft(h, p):
                b = 2 * h + p
                pe.wait_ge(kbd_ready, b + 1)
                pe.wait_ge(kT_ready, 2 * b + 2)
                wait_free(pe, shifted, b, 1)
                for i in range(HG):
                    last = T.matmul(psS[:, i, 0:HG * NK], qT[32 * i:32 * i + 32, p, :], kbd[32 * i:32 * i + 32, p, :], start=True, stop=True)
                last.then_inc(scores_ready, 1)

            def stage_out(h, p):
                b = 2 * h + p
                pe.wait_ge(exp_ready, b + 1)
                for c in range(4):
                    evacuated = pT_dve if c % 2 else pT_act
                    if not (isinstance(b, int) and 2 * b + c // 2 < 1):
                        pe.wait_ge(evacuated, 2 * b + c // 2)
                    for i in range(4):
                        k = 4 * c + i
                        last = T.transpose(psT[0:NK, c % 2, P * i:P * i + P], prob[:, p, NK * k:NK * k + NK], ident)
                    last.then_inc(p_turned, 1)
                pe.wait_ge(pT_act, 2 * b + 2)
                pe.wait_ge(pT_dve, 2 * b + 2)
                pe.wait_ge(qkn_ready, 3 * b + 3)
                wait_free(pe, place_steps, b, 1, 6)
                for k in range(H):
                    last = T.matmul(psB[:, (HD + 1) * k:(HD + 1) * (k + 1)], pT[0:NK, p, P * k:P * k + P], g.vaug[0:NK, p, k, :], start=True, stop=True)
                last.then_inc(pv_ready, 1)
                pe.wait_ge(o_ready, b + 1)
                T.transpose(psB[:, 2 * P:3 * P], o[:, p, :], ident).then_inc(o_turned, 1)
                pe.wait_ge(oT_ready, b + 1)
                T.matmul(psB[:, 3 * P:4 * P], oT[:, p, :], g.w_small[:, 0:P], start=True, stop=True).then_inc(y_ready, 1)
                pe.wait_ge(xn1_ready, b + 1)
                T.transpose(psB[:, P:2 * P], xn1[:, p, :], ident).then_inc(xn1_turned, 1)
                pe.wait_ge(xn1T_ready, b + 1)
                T.matmul(psB[:, 0:E0], xn1T[:, p, :], g.w_small[:, P:P + E0], start=True, stop=True).then_inc(logits_ready, 1)
                pe.wait_ge(rank_steps, 9 * b + 9)
                T.matmul(psB[:, 8:8 + E0], g.consts[:, C_TRI:C_TRI + P], picked[:, p, :], start=True, stop=True)
                T.matmul(psB[:, 16:16 + E0], g.consts[:, C_ONE:C_ONE + P], picked[:, p, :], start=True, stop=True).then_inc(counted, 1)

            pipeline(pe, [None, stage_q, stage_soft, stage_out], NB, 6)


def tables(nc, g):
    with ExitStack() as ctx:
        def sb(name, shape, dt=F32):
            return ctx.enter_context(nc.sbuf_tensor(name, shape, dt))

        count, tiles_i, tiles, upto, upto2, before = (sb("count", [P, E0]), sb("tiles_i", [P, E0], I32), sb("tiles", [P, E0]),
                                                      sb("upto", [P, E0]), sb("upto2", [P, E0]), sb("before", [P, E0]))
        pad_f, pad = sb("pad_f", [P, E0]), sb("pad", [P, E0], I32)
        past, te, used, hot = sb("past", [P, NT * E0]), sb("te", [P, NT]), sb("used", [P, NT]), sb("hot", [P, NT * E0])
        first, row, tab, moved, step = (sb("first", [P, NT]), sb("row", [P, NT]), sb("tab", [P, 2 * NT]), sb("moved", [P, E0]), sb("step", [P, E0]))
        over, shift_by = sb("over", [P, 2 * NB * E0]), sb("shift_by", [P, 2 * NB])
        table_steps, pads_ready = ctx.enter_context(nc.semaphore("table_steps")), ctx.enter_context(nc.semaphore("pads_ready"))
        padded = ctx.enter_context(nc.semaphore("padded"))
        block = ctx.enter_context(nc.Block())

        @block.vector
        def _(dve):
            V = nc.vector
            st = Steps(dve, table_steps, 0, 0)

            def do(instruction):
                st(instruction)
                st.wait()

            do(V.tensor_scalar(pad_f[:, :], g.run[:, :], g.consts[:, C_P:C_P + 1], None, ALU.add))
            V.tensor_copy(pad[:, :], pad_f[:, :]).then_inc(pads_ready, 1)
            do(V.tensor_tensor(count[:, :], g.run[:, :], g.consts[:, C_RUN:C_RUN + E0], ALU.subtract))
            do(V.tensor_scalar(count[:, :], count[:, :], float(P - 1), None, ALU.add))
            do(V.tensor_copy(tiles_i[:, :], count[:, :]))
            do(V.tensor_scalar(tiles_i[:, :], tiles_i[:, :], 7, None, ALU.logical_shift_right))
            do(V.tensor_copy(tiles[:, :], tiles_i[:, :]))
            a, b = tiles, upto
            do(V.tensor_copy(upto[:, :], tiles[:, :]))
            do(V.tensor_copy(upto2[:, :], tiles[:, :]))
            a, b = upto, upto2
            for shift in (1, 2, 4):
                do(V.tensor_copy(b[:, 0:shift], a[:, 0:shift]))
                do(V.tensor_tensor(b[:, shift:E0], a[:, shift:E0], a[:, 0:E0 - shift], ALU.add))
                a, b = b, a
            do(V.tensor_tensor(before[:, :], a[:, :], tiles[:, :], ALU.subtract))
            jrow = g.consts[:, C_J:C_J + NT]
            pastv, hotv = (x[:, :].rearrange("p (j e) -> p j e", j=NT) for x in (past, hot))
            do(V.tensor_tensor(pastv, bcast(a[:, :].unsqueeze(1), P, NT, E0), bcast(jrow.unsqueeze(2), P, NT, E0), ALU.is_le))
            do(V.tensor_reduce(te[:, :], pastv, AX, ALU.add))
            do(V.tensor_scalar(used[:, :], te[:, :], E0 - 0.5, None, ALU.is_lt))
            do(V.tensor_scalar(tab[:, 0:NT], te[:, :], float(E0 - 1), None, ALU.min))
            do(V.tensor_tensor(hotv, bcast(tab[:, 0:NT].unsqueeze(2), P, NT, E0),
                               bcast(g.consts[:, C_J:C_J + E0].unsqueeze(1), P, NT, E0), ALU.is_equal))
            do(V.tensor_tensor(hotv, hotv, bcast(before[:, :].unsqueeze(1), P, NT, E0), ALU.mult))
            do(V.tensor_reduce(first[:, :], hotv, AX, ALU.add))
            do(V.tensor_tensor(first[:, :], jrow, first[:, :], ALU.subtract))
            do(V.tensor_scalar(first[:, :], first[:, :], float(P), None, ALU.mult))
            do(V.tensor_scalar(row[:, :], tab[:, 0:NT], float(REGION), None, ALU.mult))
            do(V.tensor_tensor(row[:, :], row[:, :], first[:, :], ALU.add))
            do(V.tensor_scalar(row[:, :], row[:, :], float(ZERO_ROW), None, ALU.subtract))
            do(V.tensor_tensor(row[:, :], row[:, :], used[:, :], ALU.mult))
            do(V.tensor_scalar(tab[:, NT:2 * NT], row[:, :], float(ZERO_ROW), None, ALU.add))
            do(V.tensor_copy(g.table[:, :], tab[:, :]))
            starts = g.consts[:, C_RUN:C_RUN + E0]
            do(V.tensor_scalar(moved[:, :], before[:, :], float(P), None, ALU.mult))
            do(V.tensor_tensor(moved[:, :], moved[:, :], starts, ALU.subtract))
            do(V.tensor_copy(step[:, 0:1], moved[:, 0:1]))
            do(V.tensor_tensor(step[:, 1:E0], moved[:, 1:E0], moved[:, 0:E0 - 1], ALU.subtract))
            slots = g.slotf[:, :, :].rearrange("p b c -> p (b c)")
            overv = over[:, :].rearrange("p (s e) -> p s e", e=E0)
            do(V.tensor_tensor(overv, bcast(slots.unsqueeze(2), P, 2 * NB, E0), bcast(starts.unsqueeze(1), P, 2 * NB, E0), ALU.is_ge))
            do(V.tensor_tensor(overv, overv, bcast(step[:, :].unsqueeze(1), P, 2 * NB, E0), ALU.mult))
            do(V.tensor_reduce(shift_by[:, :], overv, AX, ALU.add))
            do(V.tensor_tensor(g.slots[:, :, :].rearrange("p b c -> p (b c)"), shift_by[:, :], slots, ALU.add))

        @block.gpsimd
        def _(pool):
            pool.wait_ge(pads_ready, 1)
            for e in range(E0):
                nc.gpsimd.indirect_dma_start(g.xs[:, :], bass.IndirectOffsetOnAxis(pad[:, e:e + 1], 0),
                                             g.zeros[:, :], None).then_inc(padded, 16)
            pool.wait_ge(padded, 16 * E0)


def experts0(nc, g):
    with ExitStack() as ctx:
        def sb(name, shape, dt=F32):
            return ctx.enter_context(nc.sbuf_tensor(name, shape, dt))

        def sem(name):
            return ctx.enter_context(nc.semaphore(name))

        xt, xtT = sb("xt", [P, 2, P]), sb("xtT", [P, 2, P])
        zg, y, z1, hid, hT, yt = (sb("zg", [P, 2, F0]), sb("y", [P, 2, F0]), sb("z1", [P, 2, F0]), sb("hid", [P, 2, F0]), sb("hT", [P, 2, F0]), sb("yt", [P, 2, P]))
        w_up, w_down, b_row, b_down = sb("w_up0", [P, E0, 2 * F0]), sb("w_down0", [P, E0, FC * P]), sb("b_row0", [P, E0, 2 * F0]), sb("b_down0", [P, E0, P])
        weights_in = sem("weights_in")
        rows_in, rows_out = [sem("rows_in_even"), sem("rows_in_odd")], [sem("rows_out_even"), sem("rows_out_odd")]
        turned, xtT_ready, zg_done, z1_done = sem("x_turned"), sem("xtT_ready"), sem("zg_done"), sem("z1_done")
        zg_ready, z1_ready, y_ready, hid_ready = sem("zg_ready"), sem("z1_ready"), sem("gelu_ready"), sem("hid_ready")
        h_turned, hT_ready, down_done, yt_ready = sem("h_turned"), sem("hT_ready"), sem("down_done"), sem("yt_ready")
        block = ctx.enter_context(nc.Block())
        psX, psH, psY = g.bank[0], g.bank[5], g.bank[6]
        psG, psZ = [g.bank[1], g.bank[2]], [g.bank[3], g.bank[4]]

        @block.sync
        def _(sp):
            sp.dma_start(w_up[:, 0:4, :], g.d_w_up0[:, 0:4, :]).then_inc(weights_in, 16)
            sp.dma_start(w_up[:, 4:8, :], g.d_w_up0[:, 4:8, :]).then_inc(weights_in, 16)
            sp.dma_start(w_down[:, :, :], g.d_w_down0).then_inc(weights_in, 16)

            def load_rows(h, p):
                j = 2 * h + p
                wait_free(sp, turned, j, 2)
                row = sp.value_load(g.table[0:1, ds(NT + j, 1)], min_val=0, max_val=ZERO_ROW)
                sp.dma_start(xt[:, p, :], g.xs[ds(row, P), :]).then_inc(rows_in[p], 16)
            pipeline(sp, [load_rows], NT, 2)

        @block.scalar
        def _(act):
            act.dma_start(b_row[:, :, :].rearrange("p e f -> p (e f)"), g.d_b_row0.partition_broadcast(P)).then_inc(weights_in, 16)
            act.dma_start(b_down[:, :, :].rearrange("p e f -> p (e f)"), g.d_b_down0.partition_broadcast(P)).then_inc(weights_in, 16)

            def stage_in(h, p):
                j = 2 * h + p
                act.wait_ge(turned, j + 1)
                wait_free(act, z1_done, j, 2)
                nc.scalar.activation(xtT[:, p, :], psX[:, 0:P], ACT.Copy).then_inc(xtT_ready, 1)

            def stage_gelu(h, p):
                j = 2 * h + p
                act.wait_ge(zg_ready, j + 1)
                wait_free(act, hid_ready, j, 2)
                nc.scalar.activation(y[:, p, :], zg[:, p, :], ACT.Gelu).then_inc(y_ready, 1)

            def stage_out(h, p):
                j = 2 * h + p
                act.wait_ge(h_turned, j + 1)
                wait_free(act, down_done, j, 2)
                nc.scalar.activation(hT[:, p, :], psH[:, :], ACT.Copy).then_inc(hT_ready, 1)
            pipeline(act, [stage_in, stage_gelu, stage_out], NT, 6)

        @block.tensor
        def _(pe):
            T = nc.tensor
            ident = g.consts[:, C_ID:C_ID + P]
            pe.wait_ge(weights_in, 48 + 32)

            def stage_in(h, p):
                j = 2 * h + p
                pe.wait_ge(rows_in[p], 16 * h + 16)
                wait_free(pe, xtT_ready, j, 1)
                T.transpose(psX[:, 0:P], xt[:, p, :], ident).then_inc(turned, 1)
                e = pe.value_load(g.table[0:1, ds(j, 1)], min_val=0, max_val=E0 - 1)
                pe.wait_ge(xtT_ready, j + 1)
                wait_free(pe, zg_ready, j, 2)
                wait_free(pe, z1_ready, j, 2)
                T.matmul(psG[p][:, :], xtT[:, p, :], w_up[:, ds(e, 1), 0:F0].rearrange("p a f -> p (a f)"), start=True, stop=True).then_inc(zg_done, 1)
                T.matmul(psZ[p][:, :], xtT[:, p, :], w_up[:, ds(e, 1), F0:2 * F0].rearrange("p a f -> p (a f)"), start=True, stop=True).then_inc(z1_done, 1)

            def stage_out(h, p):
                j = 2 * h + p
                pe.wait_ge(hid_ready, j + 1)
                wait_free(pe, hT_ready, j, 1)
                for c in range(FC):
                    last = T.transpose(psH[:, P * c:P * c + P], hid[:, p, P * c:P * c + P], ident)
                last.then_inc(h_turned, 1)
                e = pe.value_load(g.table[0:1, ds(j, 1)], min_val=0, max_val=E0 - 1)
                pe.wait_ge(hT_ready, j + 1)
                wait_free(pe, yt_ready, j, 1)
                for c in range(FC):
                    last = T.matmul(psY[:, 0:P], hT[:, p, P * c:P * c + P], w_down[:, ds(e, 1), P * c:P * c + P].rearrange("p a f -> p (a f)"),
                                    start=c == 0, stop=c == FC - 1)
                last.then_inc(down_done, 1)
            pipeline(pe, [stage_in, None, stage_out], NT, 6)

        @block.vector
        def _(dve):
            V = nc.vector
            dve.wait_ge(weights_in, 48 + 32)

            def stage_bias(h, p):
                j = 2 * h + p
                e = dve.value_load(g.table[0:1, ds(j, 1)], min_val=0, max_val=E0 - 1)
                dve.wait_ge(zg_done, j + 1)
                wait_free(dve, y_ready, j, 2)
                V.tensor_tensor(zg[:, p, :], psG[p][:, :], b_row[:, ds(e, 1), 0:F0].rearrange("p a f -> p (a f)"), ALU.add).then_inc(zg_ready, 1)
                dve.wait_ge(z1_done, j + 1)
                wait_free(dve, hid_ready, j, 2)
                V.tensor_tensor(z1[:, p, :], psZ[p][:, :], b_row[:, ds(e, 1), F0:2 * F0].rearrange("p a f -> p (a f)"), ALU.add).then_inc(z1_ready, 1)

            def stage_mult(h, p):
                j = 2 * h + p
                dve.wait_ge(y_ready, j + 1)
                dve.wait_ge(z1_ready, j + 1)
                wait_free(dve, h_turned, j, 2)
                V.tensor_tensor(hid[:, p, :], y[:, p, :], z1[:, p, :], ALU.mult).then_inc(hid_ready, 1)

            def stage_out(h, p):
                j = 2 * h + p
                e = dve.value_load(g.table[0:1, ds(j, 1)], min_val=0, max_val=E0 - 1)
                dve.wait_ge(down_done, j + 1)
                if not (isinstance(j, int) and j < 2):
                    dve.wait_ge(rows_out[p], 16 * h)
                V.tensor_tensor(yt[:, p, :], psY[:, 0:P], b_down[:, ds(e, 1), :].rearrange("p a f -> p (a f)"), ALU.add).then_inc(yt_ready, 1)
            pipeline(dve, [stage_bias, stage_mult, stage_out], NT, 6)

        @block.gpsimd
        def _(pool):
            def store_rows(h, p):
                j = 2 * h + p
                pool.wait_ge(yt_ready, j + 1)
                pool.dma_start(g.ys[ds(P * j, P), :], yt[:, p, :]).then_inc(rows_out[p], 16)
            pipeline(pool, [store_rows], NT, 2)
            for p in range(2):
                pool.wait_ge(rows_out[p], 16 * (NT // 2))


def attention1(nc, g):
    with ExitStack() as ctx:
        def sb(name, shape, dt=F32):
            return ctx.enter_context(nc.sbuf_tensor(name, shape, dt))

        def sem(name):
            return ctx.enter_context(nc.semaphore(name))

        idx, got = sb("idx", [P, 2, 2], I32), sb("got", [P, 2, 2 * P])
        st2, mv2, ve2, rstd2 = sb("st2", [P, 2, 6]), sb("mv2", [P, 2, 2]), sb("ve2", [P, 2, 1]), sb("rstd2", [P, 2, 1])
        xn2, xn2T, q1T, k1T = sb("xn2", [P, 2, P]), sb("xn2T", [P, 2, P]), sb("q1T", [P, 2, P]), sb("k1T", [P, 2, NK])
        mx1, p1, den, rden, p1T, r, rT = (sb("mx1", [P, 2, 1]), sb("p1", [P, 2, NK]), sb("den", [P, 2, 1]), sb("rden", [P, 2, 1]),
                                          sb("p1T", [P, 2, P]), sb("r", [P, 2, P]), sb("rT", [P, 2, P]))
        st3, mv3, ve3, rstd3 = sb("st3", [P, 2, 6]), sb("mv3_", [P, 2, 2]), sb("ve3_", [P, 2, 1]), sb("rstd3_", [P, 2, 1])
        xn3, xn3T = sb("xn3", [P, 2, P]), sb("xn3T", [P, 2, P])
        biased, top, rest, mask = sb("biased", [P, 2, E1]), sb("top", [P, 2, 8]), sb("rest", [P, 2, E1]), sb("mask", [P, 2, E1])
        en, sig, ws, wsum = sb("en", [P, 2, E1]), sb("sig", [P, 2, E1]), sb("ws", [P, 2, E1]), sb("wsum", [P, 2, 1])
        cw, low, parts = sb("cw", [P, 2, E1]), sb("low", [P, 2, E1]), sb("parts", [P, 2, 2 * E1], F16)

        psA, psB, psC, psD = g.bank[0], g.bank[1], g.bank[2], g.bank[3]
        psD16 = psD.bitcast(F16)
        gathered = [sem("gathered_even"), sem("gathered_odd")]
        idx_ready, comb_steps, x2_stats, x2_var, x2_rstd, xn2_ready = sem("idx_ready"), sem("comb_steps"), sem("x2_stats"), sem("x2_var"), sem("x2_rstd"), sem("xn2_ready")
        xn2_turned, xn2T_ready, qk_done, k1T_ready, s_done = sem("xn2_turned"), sem("xn2T_ready"), sem("qk_done"), sem("k1T_ready"), sem("s_done")
        mx1_steps, p1_ready, p1_turned, p1T_ready, av_done = sem("mx1_steps"), sem("p1_ready"), sem("p1_turned"), sem("p1T_ready"), sem("av_done")
        rden_ready, r_ready, r_turned, rT_ready, o1_done, bo1_added = sem("rden_ready"), sem("r_ready"), sem("r_turned"), sem("rT_ready"), sem("o1_done"), sem("bo1_added")
        x3_ready, x3_stats, x3_var, x3_rstd, xn3_ready, xn3_turned = sem("x3_ready"), sem("x3_stats"), sem("x3_var"), sem("x3_rstd"), sem("xn3_ready"), sem("xn3_turned")
        xn3T_ready, xn3T_kept, aff_done, en_ready, top_steps, cw_steps = sem("xn3T_ready"), sem("xn3T_kept"), sem("aff_done"), sem("en_ready"), sem("top_steps"), sem("cw_steps")
        parts_ready, parts_turned, cwT_ready = sem("parts_ready"), sem("parts_turned"), sem("cwT_ready")
        block = ctx.enter_context(nc.Block())

        @block.gpsimd
        def _(pool):
            def rstd_of(var, var_eps, out, b, steps, ready):
                st = Steps(pool, steps, 1, b)
                st(nc.gpsimd.tensor_scalar(var_eps, var, EPS, None, ALU.add))
                st.wait()
                nc.gpsimd.tensor_tensor(out, var_eps, g.mhalf[:, 0:1], ALU.pow).then_inc(ready, 1)

            def stage_gather(h, p):
                b = 2 * h + p
                wait_apart(g, pool, idx_ready, b + 1)
                wait_free(pool, comb_steps, b, 2, 2, apart=g)
                for c in range(2):
                    nc.gpsimd.indirect_dma_start(got[:, p, P * c:P * c + P], None, g.ys[:, :],
                                                 bass.IndirectOffsetOnAxis(idx[:, p, c:c + 1], 0)).then_inc(gathered[p], 16)

            def stage_norm(h, p):
                b = 2 * h + p
                wait_apart(g, pool, x2_stats, 2 * b + 2)
                wait_free(pool, xn2_ready, b, 2, apart=g)
                rstd_of(mv2[:, p, 1:2], ve2[:, p, :], rstd2[:, p, :], b, x2_var, x2_rstd)
                pool.wait_ge(xn2_ready, b + 1)
                xb = g.X[:, ds(b, 1), :].rearrange("p a d -> p (a d)")
                nc.gpsimd.tensor_tensor(xb, xb, g.rows[:, R_BO1:R_BO1 + P], ALU.add).then_inc(bo1_added, 1)

            def stage_out(h, p):
                b = 2 * h + p
                wait_apart(g, pool, x3_stats, 2 * b + 2)
                wait_free(pool, xn3_ready, b, 2, apart=g)
                rstd_of(mv3[:, p, 1:2], ve3[:, p, :], rstd3[:, p, :], b, x3_var, x3_rstd)
                pool.wait_ge(xn3T_ready, b + 1)
                nc.gpsimd.tensor_copy(g.XT[:, ds(b, 1), :].rearrange("p a t -> p (a t)"), xn3T[:, p, :]).then_inc(xn3T_kept, 1)
            pipeline(pool, [stage_gather, stage_norm, None, stage_out], NB, 6)

        @block.vector
        def _(dve):
            V = nc.vector

            def stage_idx(h, p):
                b = 2 * h + p
                if not (isinstance(b, int) and b < 2):
                    dve.wait_ge(gathered[p], 32 * h)
                V.tensor_copy(idx[:, p, :], g.slots[:, ds(b, 1), :].rearrange("p a c -> p (a c)")).then_inc(idx_ready, 1)

            def stage_norm(h, p):
                b = 2 * h + p
                dve.wait_ge(gathered[p], 32 * h + 32)
                xb = g.X[:, ds(b, 1), :].rearrange("p a d -> p (a d)")
                st = Steps(dve, comb_steps, 2, b)
                for c in range(2):
                    st(V.scalar_tensor_tensor(xb, got[:, p, P * c:P * c + P], g.gate[:, ds(b, 1), c:c + 1].rearrange("p a c -> p (a c)"), xb, ALU.mult, ALU.add))
                    st.wait_apart(g)
                wait_free(dve, x2_rstd, b, 2, apart=g)
                st = Steps(dve, x2_stats, 2, b)
                st(V.bn_stats(st2[:, p, :], xb))
                st.wait_apart(g)
                wait_free(dve, xn2_ready, b, 2, apart=g)
                st(V.bn_aggr(mv2[:, p, :], st2[:, p, :]))
                dve.wait_ge(x2_rstd, b + 1)
                st.wait()
                wait_free(dve, xn2_turned, b, 2)
                wait_free(dve, r_ready, b, 2)
                V.tensor_scalar(xn2[:, p, :], xb, mv2[:, p, 0:1], rstd2[:, p, :], ALU.subtract, ALU.mult).then_inc(xn2_ready, 1)

            def stage_soft(h, p):
                b = 2 * h + p
                dve.wait_ge(s_done, b + 1)
                wait_free(dve, p1_ready, b, 2)
                st = Steps(dve, mx1_steps, 2, b)
                st(V.tensor_reduce(mx1[:, p, :], psA[:, 384:384 + NK], AX, ALU.max))
                st.wait()
                st(V.tensor_scalar(mx1[:, p, :], mx1[:, p, :], -float(P) ** -0.5, None, ALU.mult))
                dve.wait_ge(p1_ready, b + 1)
                V.reciprocal(rden[:, p, :], den[:, p, :]).then_inc(rden_ready, 1)
                dve.wait_ge(p1_turned, b + 1)
                wait_free(dve, av_done, b, 2)
                V.tensor_copy(p1T[0:NK, p, :], psB[0:NK, 0:P]).then_inc(p1T_ready, 1)
                dve.wait_ge(av_done, b + 1)
                dve.wait_ge(rden_ready, b + 1)
                dve.wait_ge(xn2_ready, b + 1)
                wait_free(dve, r_turned, b, 2)
                V.scalar_tensor_tensor(r[:, p, :], psB[:, P:2 * P], rden[:, p, :], xn2[:, p, :], ALU.mult, ALU.add).then_inc(r_ready, 1)

            def stage_out(h, p):
                b = 2 * h + p
                dve.wait_ge(o1_done, b + 1)
                dve.wait_ge(bo1_added, b + 1)
                xb = g.X[:, ds(b, 1), :].rearrange("p a d -> p (a d)")
                V.tensor_tensor(xb, psC[:, P:2 * P], xb, ALU.add).then_inc(x3_ready, 1)
                wait_apart(g, dve, x3_ready, b + 1)
                wait_free(dve, x3_rstd, b, 2, apart=g)
                st = Steps(dve, x3_stats, 2, b)
                st(V.bn_stats(st3[:, p, :], xb))
                st.wait_apart(g)
                wait_free(dve, xn3_ready, b, 2, apart=g)
                st(V.bn_aggr(mv3[:, p, :], st3[:, p, :]))
                dve.wait_ge(x3_rstd, b + 1)
                st.wait()
                wait_free(dve, xn3_turned, b, 2)
                V.tensor_scalar(xn3[:, p, :], xb, mv3[:, p, 0:1], rstd3[:, p, :], ALU.subtract, ALU.mult).then_inc(xn3_ready, 1)
                dve.wait_ge(aff_done, b + 1)
                st = Steps(dve, top_steps, 4, b)
                st(V.tensor_tensor(biased[:, p, :], psD[:, 0:E1], g.rows[:, R_EB:R_EB + E1], ALU.add))
                st.wait_apart(g)
                st(V.max(top[:, p, :], biased[:, p, :]))
                st.wait_apart(g)
                st(V.match_replace(rest[:, p, :], top[:, p, :], biased[:, p, :], -3.0e38))
                st.wait()
                st(V.tensor_tensor(mask[:, p, :], biased[:, p, :], rest[:, p, :], ALU.not_equal))
                dve.wait_ge(en_ready, b + 1)
                st.wait()
                st = Steps(dve, cw_steps, 9, b)
                st(V.tensor_scalar(sig[:, p, :], en[:, p, :], 1.0, None, ALU.add))
                st.wait()
                st(V.reciprocal(sig[:, p, :], sig[:, p, :]))
                st.wait()
                st(V.tensor_tensor(ws[:, p, :], sig[:, p, :], mask[:, p, :], ALU.mult))
                st.wait()
                st(V.tensor_reduce(wsum[:, p, :], ws[:, p, :], AX, ALU.add))
                st.wait()
                st(V.tensor_scalar(wsum[:, p, :], wsum[:, p, :], 1e-8, None, ALU.add))
                st.wait()
                st(V.reciprocal(wsum[:, p, :], wsum[:, p, :]))
                st.wait()
                st(V.tensor_scalar(cw[:, p, :], ws[:, p, :], wsum[:, p, :], None, ALU.mult))
                st.wait()
                wait_free(dve, parts_turned, b, 2)
                st(V.tensor_copy(parts[:, p, 0:E1], cw[:, p, :]))
                st.wait()
                st(V.tensor_tensor(low[:, p, :], cw[:, p, :], parts[:, p, 0:E1], ALU.subtract))
                st.wait()
                V.tensor_scalar(parts[:, p, E1:2 * E1], low[:, p, :], 2048.0, None, ALU.mult).then_inc(parts_ready, 1)
            pipeline(dve, [stage_idx, stage_norm, stage_soft, stage_out], NB, 6)

        @block.scalar
        def _(act):
            A = nc.scalar

            def stage_norm(h, p):
                b = 2 * h + p
                act.wait_ge(xn2_turned, b + 1)
                wait_free(act, qk_done, b, 2)
                A.activation(xn2T[:, p, :], psA[:, 0:P], ACT.Copy).then_inc(xn2T_ready, 1)
                act.wait_ge(qk_done, b + 1)
                wait_free(act, s_done, b, 2)
                A.activation(q1T[:, p, :], psA[:, P:2 * P], ACT.Identity, bias=g.cols[:, BQ1:BQ1 + 1]).then_inc(k1T_ready, 1)
                A.activation(k1T[:, p, :], psA[:, 2 * P:2 * P + NK], ACT.Identity, bias=g.cols[:, BK1:BK1 + 1]).then_inc(k1T_ready, 1)

            def stage_soft(h, p):
                b = 2 * h + p
                act.wait_ge(mx1_steps, 2 * b + 2)
                wait_free(act, p1_turned, b, 2)
                wait_free(act, rden_ready, b, 2)
                A.activation(p1[:, p, :], psA[:, 384:384 + NK], ACT.Exp, bias=mx1[:, p, :], scale=float(P) ** -0.5,
                             accum_out=den[:, p, :]).then_inc(p1_ready, 1)
                act.wait_ge(r_turned, b + 1)
                wait_free(act, o1_done, b, 2)
                A.activation(rT[:, p, :], psC[:, 0:P], ACT.Copy).then_inc(rT_ready, 1)

            def stage_out(h, p):
                b = 2 * h + p
                act.wait_ge(xn3_turned, b + 1)
                wait_free(act, aff_done, b, 2)
                wait_free(act, xn3T_kept, b, 2)
                A.activation(xn3T[:, p, :], psC[:, 2 * P:3 * P], ACT.Copy).then_inc(xn3T_ready, 1)
                act.wait_ge(top_steps, 4 * b + 1)
                wait_free(act, cw_steps, b, 2, 9)
                A.activation(en[:, p, :], psD[:, 0:E1], ACT.Exp, scale=-1.0).then_inc(en_ready, 1)
                act.wait_ge(parts_turned, b + 1)
                A.activation(g.CWT[:, ds(b, 1), :].rearrange("p a t -> p (a t)"), psD16[:, 512:512 + P], ACT.Copy).then_inc(cwT_ready, 1)
            pipeline(act, [None, stage_norm, stage_soft, stage_out], NB, 6)

        @block.tensor
        def _(pe):
            T = nc.tensor
            ident = g.consts[:, C_ID:C_ID + P]
            wo1, cent, wq1, wk1 = (g.w_small[:, 136:264], g.w_small[:, 264:328], g.w_small[:, 328:456], g.w_small[:, 456:584])

            def stage_norm(h, p):
                b = 2 * h + p
                pe.wait_ge(xn2_ready, b + 1)
                wait_free(pe, p1_ready, b, 1)
                T.transpose(psA[:, 0:P], xn2[:, p, :], ident).then_inc(xn2_turned, 1)
                pe.wait_ge(xn2T_ready, b + 1)
                T.matmul(psA[:, P:2 * P], wq1, xn2T[:, p, :], start=True, stop=True)
                T.matmul(psA[:, 2 * P:2 * P + NK], wk1, g.ctxT[:, ds(b, 1), :].rearrange("p a k -> p (a k)"), start=True, stop=True).then_inc(qk_done, 1)
                pe.wait_ge(k1T_ready, 2 * b + 2)
                T.matmul(psA[:, 384:384 + NK], q1T[:, p, :], k1T[:, p, :], start=True, stop=True).then_inc(s_done, 1)

            def stage_soft(h, p):
                b = 2 * h + p
                pe.wait_ge(p1_ready, b + 1)
                wait_free(pe, r_ready, b, 1)
                T.transpose(psB[0:NK, 0:P], p1[:, p, :], ident).then_inc(p1_turned, 1)
                pe.wait_ge(p1T_ready, b + 1)
                T.matmul(psB[:, P:2 * P], p1T[0:NK, p, :], g.V1[0:NK, ds(b, 1), :].rearrange("p a d -> p (a d)"), start=True, stop=True).then_inc(av_done, 1)
                pe.wait_ge(r_ready, b + 1)
                wait_free(pe, xn3T_ready, b, 1)
                T.transpose(psC[:, 0:P], r[:, p, :], ident).then_inc(r_turned, 1)
                pe.wait_ge(rT_ready, b + 1)
                T.matmul(psC[:, P:2 * P], rT[:, p, :], wo1, start=True, stop=True).then_inc(o1_done, 1)

            def stage_out(h, p):
                b = 2 * h + p
                pe.wait_ge(xn3_ready, b + 1)
                T.transpose(psC[:, 2 * P:3 * P], xn3[:, p, :], ident).then_inc(xn3_turned, 1)
                pe.wait_ge(xn3T_ready, b + 1)
                wait_free(pe, cwT_ready, b, 1)
                T.matmul(psD[:, 0:E1], xn3T[:, p, :], cent, start=True, stop=True).then_inc(aff_done, 1)
                pe.wait_ge(parts_ready, b + 1)
                T.transpose(psD16[:, 512:512 + P], parts[:, p, :], g.ident16[:, :]).then_inc(parts_turned, 1)
            pipeline(pe, [None, stage_norm, stage_soft, stage_out], NB, 6)


def experts1(nc, g):
    with ExitStack() as ctx:
        def sb(name, shape, dt=F32):
            return ctx.enter_context(nc.sbuf_tensor(name, shape, dt))

        def sem(name):
            return ctx.enter_context(nc.semaphore(name))

        N = LOTS * P
        w_up, w_down, ws_down, ws_up = sb("w_up1", [P, NFT * P]), sb("w_down1", [P, NFT * P]), sb("ws_down", [F1, P]), sb("ws_up", [P, F1])
        act_out, hid = sb("act_out", [P, 2, N]), sb("hid1", [P, 2, N])
        sumT, res = sb("sumT", [P, N]), sb("res", [P, N])
        weights_in = sem("weights1_in")
        up_done, silu_ready, hid_ready, down_done = sem("up_done"), sem("silu_ready"), sem("hid1_ready"), sem("down1_done")
        sum_ready, sum_turned, res_ready, stored = sem("sum_ready"), sem("sum_turned"), sem("res_ready"), sem("stored")
        block = ctx.enter_context(nc.Block())
        psW, psU, psO, psR = [g.bank[0], g.bank[1]], [g.bank[2], g.bank[3], g.bank[6]], g.bank[4], g.bank[5]
        NS = NFT + 1

        @block.sync
        def _(sp):
            for i in range(2):
                half = NFT * P // 2
                sp.dma_start(w_up[:, half * i:half * i + half], g.d_w_up1[:, half * i:half * i + half]).then_inc(weights_in, 16)
                sp.dma_start(w_down[:, half * i:half * i + half], g.d_w_down1[:, half * i:half * i + half]).then_inc(weights_in, 16)
            sp.dma_start(ws_down[:, :], g.d_ws_down).then_inc(weights_in, 16)
            sp.dma_start(ws_up[:, :], g.d_ws_up).then_inc(weights_in, 16)
            with sp.Fori(0, NG) as i:
                sp.wait_ge(res_ready, i + 1)
                sp.dma_start(g.d_out[ds(i * LOTS, LOTS), :, :].rearrange("b p d -> p b d"),
                             res[:, :].rearrange("p (b d) -> p b d", b=LOTS)).then_inc(stored, 16)
            sp.wait_ge(stored, 16 * NG)

        @block.tensor
        def _(pe):
            T = nc.tensor
            ident = g.consts[:, C_ID:C_ID + P]
            pe.wait_ge(weights_in, 96)

            def up(i, f):
                n = i * NS + f
                first_step = isinstance(i, int) and i == 0
                x = g.XT[:, ds(i * LOTS, LOTS), :].rearrange("p b t -> p (b t)")
                if f < NFT:
                    if not (first_step and f < 2):
                        pe.wait_ge(hid_ready, i * NFT + f - 1)
                    T.matmul(psW[f % 2][:, :], g.sel[:, P * f:P * f + P], g.CWT[:, ds(i * LOTS, LOTS), :].rearrange("p b t -> p (b t)"), start=True, stop=True)
                if not (first_step and f < 3):
                    wait_apart(g, pe, silu_ready, n - 2)
                if f < NFT:
                    T.matmul(psU[f % 3][:, :], w_up[:, P * f:P * f + P], x, start=True, stop=True).then_inc(up_done, 1)
                else:
                    T.matmul(psU[f % 3][0:F1, :], ws_up[:, :], x, start=True, stop=True).then_inc(up_done, 1)

            def down(i, f):
                if f == 0 and not (isinstance(i, int) and i == 0):
                    pe.wait_ge(sum_ready, i)
                if f < NFT:
                    pe.wait_ge(hid_ready, i * NFT + f + 1)
                    T.matmul(psO[:, :], w_down[:, P * f:P * f + P], hid[:, f % 2, :], start=f == 0, stop=False).then_inc(down_done, 1)
                else:
                    pe.wait_ge(silu_ready, i * NS + NS)
                    T.matmul(psO[:, :], ws_down[:, :], act_out[0:F1, f % 2, :], start=False, stop=True).then_inc(down_done, 1)

            def group(i):
                for f in range(NS + 2):
                    if f < NS:
                        up(i, f)
                    if f >= 2:
                        down(i, f - 2)
                pe.wait_ge(sum_ready, i + 1)
                if not (isinstance(i, int) and i == 0):
                    pe.wait_ge(res_ready, i)
                for b in range(LOTS):
                    last = T.transpose(psR[:, P * b:P * b + P], sumT[:, P * b:P * b + P], ident)
                last.then_inc(sum_turned, 1)
            group(0)
            with pe.Fori(1, NG) as i:
                group(i)

        @block.scalar
        def _(act):
            def group(i):
                for f in range(NS):
                    n = i * NS + f
                    act.wait_ge(up_done, n + 1)
                    if not (isinstance(i, int) and i == 0 and f < 2):
                        if f == NFT:
                            act.wait_ge(hid_ready, i * NFT + f - 1)
                        elif f >= 2:
                            act.wait_ge(hid_ready, i * NFT + f - 1)
                        elif f == 1:
                            act.wait_ge(hid_ready, i * NFT)
                        else:
                            act.wait_ge(down_done, i * NS)
                    rows = P if f < NFT else F1
                    nc.scalar.activation(act_out[0:rows, f % 2, :], psU[f % 3][0:rows, :], ACT.Silu).then_inc(silu_ready, 1)
                act.wait_ge(down_done, i * NS + NS)
                if not (isinstance(i, int) and i == 0):
                    act.wait_ge(sum_turned, i)
                nc.scalar.activation(sumT[:, :], psO[:, :], ACT.Copy).then_inc(sum_ready, 1)
            group(0)
            with act.Fori(1, NG) as i:
                group(i)

        @block.vector
        def _(dve):
            def group(i):
                for f in range(NFT):
                    dve.wait_ge(silu_ready, i * NS + f + 1)
                    if not (isinstance(i, int) and i == 0 and f < 2):
                        dve.wait_ge(down_done, i * NS + f - 1 if f >= 2 else i * NS - 2 + f)
                    nc.vector.tensor_tensor(hid[:, f % 2, :], psW[f % 2][:, :], act_out[:, f % 2, :], ALU.mult).then_inc(hid_ready, 1)
                dve.wait_ge(sum_turned, i + 1)
                if not (isinstance(i, int) and i == 0):
                    dve.wait_ge(stored, 16 * i)
                nc.vector.tensor_tensor(res[:, :], psR[:, :], g.X[:, ds(i * LOTS, LOTS), :].rearrange("p b d -> p (b d)"), ALU.add).then_inc(res_ready, 1)
            group(0)
            with dve.Fori(1, NG) as i:
                group(i)


def program(nc, d, out):
    g = Shared()
    (g.d_x, g.d_ctx, g.d_consts, g.d_sel, g.d_ident16, g.d_cols, g.d_rows, g.d_w_ctx, g.d_w_small, g.d_w_up0, g.d_w_down0,
     g.d_b_row0, g.d_b_down0, g.d_w_up1, g.d_w_down1, g.d_ws_up, g.d_ws_down) = d
    g.d_out = out
    g.xs = nc.dram_tensor("xs", (E0 * REGION + P, P), F32, kind="Internal").ap()
    g.ys = nc.dram_tensor("ys", (NT * P, P), F32, kind="Internal").ap()
    with ExitStack() as ctx:
        def sb(name, shape, dt=F32):
            return ctx.enter_context(nc.sbuf_tensor(name, shape, dt))

        g.apart = {eng: ctx.enter_context(nc.semaphore(f"apart_{i}")) for i, eng in enumerate((nc.gpsimd, nc.vector, nc.tensor))}
        g.X = sb("X", [P, NB, P])
        g.consts, g.cols, g.rows = sb("consts", [P, C_END]), sb("cols", [P, N_COL]), sb("rows", [P, R_END])
        g.w_small = sb("w_small", [P, 584])
        g.zeros, g.mhalf = sb("zeros", [P, P]), sb("mhalf", [P, 4])
        g.run = sb("run", [P, E0])
        g.gate, g.slotf, g.slots = sb("gate", [P, NB, 2]), sb("slot_in_xs", [P, NB, 2]), sb("slots", [P, NB, 2], I32)
        g.table = sb("table", [P, 2 * NT], I32)
        g.psum = ctx.enter_context(nc.psum_tensor("psum", [P, 8, 512], F32))
        g.bank = [g.psum[:, i, :] for i in range(8)]
        with ExitStack() as late:
            def sb2(name, shape, dt=F32):
                return late.enter_context(nc.sbuf_tensor(name, shape, dt))
            g.V1, g.ctxT = sb2("V1", [P, NB, P]), sb2("ctxT", [P, NB, NK])
            with ExitStack() as early:
                g.cstage, g.vaug, g.w_ctx = (early.enter_context(nc.sbuf_tensor(n, s, F32))
                                             for n, s in (("cstage", [P, 2, P]), ("vaug", [P, 2, H, HD + 1]), ("w_ctx", [P, 4 * P])))
                load(nc, g)
                attention0(nc, g)
            tables(nc, g)
            experts0(nc, g)
            g.XT = sb2("XT", [P, NB, P])
            g.CWT = sb2("CWT", [P, NB, P], F16)
            g.sel = sb2("sel", [P, NFT * P], F16)
            g.ident16 = sb2("ident16", [P, P], F16)
            with ExitStack() as ctx2:
                sel_in = ctx2.enter_context(nc.semaphore("sel_in"))
                block = ctx2.enter_context(nc.Block())

                @block.sync
                def _(sp):
                    sp.dma_start(g.sel[:, :], g.d_sel).then_inc(sel_in, 16)
                    sp.dma_start(g.ident16[:, :], g.d_ident16).then_inc(sel_in, 16)
                    sp.wait_ge(sel_in, 32)
            attention1(nc, g)
            experts1(nc, g)


def kernel(**inputs):
    import numpy as np
    import concourse.bacc as bacc
    from concourse.bass_utils import run_bass_kernel_spmd

    a = {k: np.asarray(v) for k, v in inputs.items()}
    c = np.zeros((P, C_END), np.float32)
    i, e = np.arange(P), np.arange(E0)
    c[:, C_ID:C_ID + P] = np.eye(P)
    c[:, C_TRI:C_TRI + P] = np.triu(np.ones((P, P)), 1)
    c[:, C_ONE:C_ONE + P] = 1
    c[:, C_MASK:C_MASK + HG] = (i[:, None] // HD) % HG == np.arange(HG)
    c[:, C_LT:C_LT + E0 * E0] = (e[None, :] < e[:, None]).reshape(-1)
    c[:, C_K:C_K + 2 * E0] = np.repeat([0, 1], E0)
    c[:, C_RUN:C_RUN + E0] = e * REGION
    c[:, C_P] = i
    c[:, C_J:C_J + NT] = np.arange(NT)
    sel = np.zeros((P, NFT * P), np.float16)
    spread = np.arange(E1)[:, None] == np.arange(NFT * P) // F1
    sel[:E1], sel[E1:] = spread, spread / 2048
    d = {
        "x": a["x"], "ctx": a["ctx_1024"], "consts": c, "sel": sel, "ident16": np.eye(P, dtype=np.float16),
        "cols": np.stack([a[n] for n in ("L0_xattn_gq", "L0_xattn_betq", "L0_xattn_gk", "L0_xattn_betk", "L0_xattn_gv", "L0_xattn_betv",
                                         "L1_xattn_bq", "L1_xattn_bk")], 1),
        "rows": np.concatenate([a[n] for n in ("L0_xattn_bq", "L0_xattn_bk", "L0_xattn_bv", "L1_xattn_bv", "L0_xattn_bo",
                                               "L1_ffn_expert_biases", "L1_xattn_bo")]),
        "w_ctx": np.concatenate([a["L0_xattn_Wq"], a["L0_xattn_Wk"], a["L0_xattn_Wv"], a["L1_xattn_Wv"].T], 1),
        "w_small": np.concatenate([a["L0_xattn_Wo"], a["L0_ffn_router_w"].T, a["L1_xattn_Wo"].T, a["L1_ffn_centroids"].T,
                                   a["L1_xattn_Wq"].T, a["L1_xattn_Wk"].T], 1),
        "w_up0": np.concatenate([a["L0_ffn_wg_w"], a["L0_ffn_w1_w"]], 1).transpose(2, 0, 1),
        "w_down0": a["L0_ffn_w2_w"].reshape(E0, P, FC, P).transpose(3, 0, 2, 1).reshape(P, E0, FC * P),
        "b_row0": np.concatenate([a["L0_ffn_wg_b"], a["L0_ffn_w1_b"]], 1).reshape(-1),
        "b_down0": a["L0_ffn_w2_b"].reshape(-1),
        "w_up1": a["L1_ffn_W_up"].transpose(1, 0, 2).reshape(P, E1 * F1),
        "w_down1": a["L1_ffn_W_down"].reshape(NFT, P, P).transpose(1, 0, 2).reshape(P, NFT * P),
        "ws_up": a["L1_ffn_Ws_up"], "ws_down": a["L1_ffn_Ws_down"],
    }
    nc = bacc.Bacc("TRN2", target_bir_lowering=False, num_devices=1)
    arrays, args = {}, []
    for name, v in d.items():
        v = np.ascontiguousarray(v)
        arrays["in_" + name] = v
        args.append(nc.dram_tensor("in_" + name, v.shape, mybir.dt.from_np(v.dtype), kind="ExternalInput").ap())
    out = nc.dram_tensor("out_x", (NB, P, P), F32, kind="ExternalOutput").ap()
    program(nc, args, out)
    r = run_bass_kernel_spmd(nc, [arrays], core_ids=[0])
    return r.results[0]["out_x"]
```

```python
import concourse.bass as bass
from concourse import mybir
from contextlib import ExitStack

F32 = mybir.dt.float32
F16 = mybir.dt.float16
I32 = mybir.dt.int32
ALU = mybir.AluOpType
ACT = mybir.ActivationFunctionType
AX = mybir.AxisListType.X
ds = bass.ds

P = 128
NB = 32
NK = 120
H = 16
HD = P // H
HG = 4
E0, F0 = 8, 512
FC = F0 // P
E1, F1 = 64, 64
NFT = E1 * F1 // P
EPS = 1e-5
REGION = NB * P + P
NT = 2 * NB + E0
ZERO_ROW = E0 * REGION
LOTS = 4
NG = NB // LOTS

C_ID, C_TRI, C_ONE, C_MASK, C_LT, C_K, C_RUN, C_P, C_J, C_END = 0, 128, 256, 384, 388, 452, 468, 476, 477, 477 + NT
GQ, BQN, GK, BKN, GV, BVN, BQ1, BK1, N_COL = 0, 1, 2, 3, 4, 5, 6, 7, 8
R_QKV, R_BO0, R_EB, R_BO1, R_END = 0, 512, 640, 704, 832


class Shared:
    pass


def bcast(ap, *shape):
    return ap.to_broadcast(list(shape))


class Steps:

    def __init__(self, eng, sem, per, b):
        self.eng, self.sem, self.first, self.done = eng, sem, b * per, 0

    def __call__(self, instruction):
        instruction.then_inc(self.sem, 1)
        self.done += 1

    def wait(self):
        self.eng.wait_ge(self.sem, self.first + self.done)

    def wait_apart(self, g):
        wait_apart(g, self.eng, self.sem, self.first + self.done)


def wait_apart(g, eng, sem, value):
    eng.wait_ge(sem, value)
    if not isinstance(value, int):
        eng.sem_inc(g.apart[eng], 1)


def wait_free(eng, sem, b, back, per=1, apart=None):
    if isinstance(b, int) and b < back:
        return
    if apart is None:
        eng.wait_ge(sem, (b - back) * per + per)
    else:
        wait_apart(apart, eng, sem, (b - back) * per + per)


def pipeline(eng, pieces, n, lead):
    def step(half, parity):
        for lag, work in pieces:
            h, p = half + (parity - lag) // 2, (parity - lag) % 2
            if isinstance(half, int) and not 0 <= 2 * h + p < n:
                continue
            work(h, p)
    for t in range(lead):
        step(t // 2, t % 2)
    with eng.Fori(lead // 2, n // 2) as half:
        for parity in range(2):
            step(half, parity)
    for t in range(n, n + max(lag for lag, _ in pieces)):
        step(t // 2, t % 2)


def load(nc, g):
    with ExitStack() as ctx:
        zeroed = ctx.enter_context(nc.semaphore("zeroed"))
        loaded = ctx.enter_context(nc.semaphore("loaded"))
        consts_in = ctx.enter_context(nc.semaphore("consts_in"))
        block = ctx.enter_context(nc.Block())

        @block.gpsimd
        def _(pool):
            nc.gpsimd.memset(g.zeros[:, :], 0.0).then_inc(zeroed, 1)
            nc.gpsimd.memset(g.cstage[:, :, :], 0.0).then_inc(zeroed, 1)
            nc.gpsimd.memset(g.vaug[:, :, :, :], 1.0).then_inc(zeroed, 1)
            nc.gpsimd.memset(g.mhalf[:, :], -0.5).then_inc(zeroed, 1)
            pool.wait_ge(zeroed, 4)

        @block.sync
        def _(sp):
            n = 0
            sp.dma_start(g.consts[:, :], g.d_consts).then_inc(consts_in, 16)
            for to, of in ((g.cols[:, :], g.d_cols), (g.w_ctx[:, :], g.d_w_ctx),
                           (g.rows[:, :], g.d_rows.partition_broadcast(P)), (g.w_small[:, :], g.d_w_small)):
                sp.dma_start(to, of).then_inc(loaded, 16)
                n += 16
            for i in range(4):
                sp.dma_start(g.X[:, 8 * i:8 * i + 8, :], g.d_x[8 * i:8 * i + 8].rearrange("b p d -> p b d")).then_inc(loaded, 16)
                n += 16
            sp.wait_ge(zeroed, 1)
            sp.dma_start(g.xs[ZERO_ROW:ZERO_ROW + P, :], g.zeros[:, :]).then_inc(loaded, 16)
            sp.wait_ge(loaded, n + 16)
            sp.wait_ge(consts_in, 16)

        @block.vector
        def _(dve):
            dve.wait_ge(consts_in, 16)
            nc.vector.tensor_copy(g.run[:, :], g.consts[:, C_RUN:C_RUN + E0])


def attention0(nc, g):
    with ExitStack() as ctx:
        def sb(name, shape, dt=F32):
            return ctx.enter_context(nc.sbuf_tensor(name, shape, dt))

        def sem(name):
            return ctx.enter_context(nc.semaphore(name))

        st6, mv, ve, rstd = sb("st6", [P, 2, 6]), sb("mv", [P, 2, 2]), sb("ve", [P, 2, 1]), sb("rstd", [P, 2, 1])
        xn, xcT = sb("xn", [P, 2, P]), sb("xcT", [P, 2, 2 * P])
        qkv = sb("qkv", [P, 2, 4 * P])
        st18, mv3, ve3, rstd3 = sb("st18", [P, 2, 3, 6]), sb("mv3", [P, 2, 3, 2]), sb("ve3", [P, 2, 3]), sb("rstd3", [P, 2, 3])
        qkn = sb("qkn", [P, 2, 2 * P])
        qT, kT, kbd = sb("qT", [P, 2, P]), sb("kT", [P, 2, NK]), sb("kbd", [P, 2, HG * NK])
        mx, nmx, prob, pT = sb("mx", [P, 2, H]), sb("nmx", [P, 2, H]), sb("prob", [P, 2, H * NK]), sb("pT", [P, 2, H * P])
        rs, o, oT = sb("rs", [P, 2, H]), sb("o", [P, 2, P]), sb("oT", [P, 2, P])
        st1, mv1, ve1, rstd1 = sb("st1", [P, 2, 6]), sb("mv1", [P, 2, 2]), sb("ve1", [P, 2, 1]), sb("rstd1", [P, 2, 1])
        xn1, xn1T = sb("xn1", [P, 2, P]), sb("xn1T", [P, 2, P])
        lmax, lg, ex, esum, erec, pr = (sb("lmax", [P, 2, 1]), sb("lg", [P, 2, E0]), sb("ex", [P, 2, E0]), sb("esum", [P, 2, 1]),
                                        sb("erec", [P, 2, 1]), sb("pr", [P, 2, E0]))
        gt, eq, rank = sb("gt", [P, 2, E0 * E0]), sb("eq", [P, 2, E0 * E0]), sb("rank", [P, 2, E0])
        chosen, picked = sb("chosen", [P, 2, 2 * E0]), sb("picked", [P, 2, E0])
        place, tmp, slotf, slot = (sb("place", [P, 2, E0]), sb("tmp", [P, 2, 2 * E0]), sb("slotf", [P, 2, 2]), sb("slot", [P, 2, 2], I32))
        tmp2 = sb("tmp2", [P, 2, 2 * E0])

        psA, psB, psT, psR = g.bank[0], g.bank[1], g.bank[6], g.bank[7]
        psS = g.psum[:, 2:6, :]

        ctx_in = [sem("ctx_in_even"), sem("ctx_in_odd")]
        scattered = [sem("scattered_even"), sem("scattered_odd")]
        x_stats, x_var, x_rstd, xn_ready = sem("x_stats"), sem("x_var"), sem("x_rstd"), sem("xn_ready")
        xc_turned, xcT_ready, ctxT_kept, projected = sem("xc_turned"), sem("xcT_ready"), sem("ctxT_kept"), sem("projected")
        qkv_ready, qkv_stats, qkv_var, qkv_rstd, v1_kept = sem("qkv_ready"), sem("qkv_stats"), sem("qkv_var"), sem("qkv_rstd"), sem("v1_kept")
        qkn_ready, vn_ready, qk_turned, kT_ready, kbd_ready = sem("qkn_ready"), sem("vn_ready"), sem("qk_turned"), sem("kT_ready"), sem("kbd_ready")
        scores_ready, max_ready, nmx_ready, exp_ready = sem("scores_ready"), sem("max_ready"), sem("nmx_ready"), sem("exp_ready")
        p_turned, pT_ready, pv_ready = sem("p_turned"), sem("pT_ready"), sem("pv_ready")
        rs_ready, o_ready, o_turned, oT_ready, y_ready = sem("rs_ready"), sem("o_ready"), sem("o_turned"), sem("oT_ready"), sem("y_ready")
        bo_added, x1_ready, x1_stats, x1_var, x1_rstd = sem("bo_added"), sem("x1_ready"), sem("x1_stats"), sem("x1_var"), sem("x1_rstd")
        xn1_ready, xn1_turned, xn1T_ready, logits_ready = sem("xn1_ready"), sem("xn1_turned"), sem("xn1T_ready"), sem("logits_ready")
        shift_steps, lg_exp, rank_steps = sem("shift_steps"), sem("lg_exp"), sem("rank_steps")
        counted, place_steps, routed = sem("counted"), sem("place_steps"), sem("routed")

        block = ctx.enter_context(nc.Block())

        @block.sync
        def _(sp):
            def load_ctx(h, p):
                wait_free(sp, xc_turned, 2 * h + p, 2)
                sp.dma_start(g.cstage[0:NK, p, :], g.d_ctx[ds(2 * h + p, 1), :, :].rearrange("b k d -> (b k) d")).then_inc(ctx_in[p], 16)
            pipeline(sp, [(0, load_ctx)], NB, 2)

        @block.gpsimd
        def _(pool):
            def rstd_of(var, var_eps, out, n, b, steps, sem_ready):
                st = Steps(pool, steps, 1, b)
                st(nc.gpsimd.tensor_scalar(var_eps, var, EPS, None, ALU.add))
                st.wait()
                nc.gpsimd.tensor_tensor(out, var_eps, g.mhalf[:, 0:n], ALU.pow).then_inc(sem_ready, 1)

            def x_scale(h, p):
                b = 2 * h + p
                wait_apart(g, pool, x_stats, 2 * b + 2)
                wait_free(pool, xn_ready, b, 2, apart=g)
                rstd_of(mv[:, p, 1:2], ve[:, p, :], rstd[:, p, :], 1, b, x_var, x_rstd)

            def keep_ctx(h, p):
                b = 2 * h + p
                pool.wait_ge(xcT_ready, b + 1)
                nc.gpsimd.tensor_copy(g.ctxT[:, ds(b, 1), :].rearrange("p a k -> p (a k)"), xcT[:, p, P:P + NK]).then_inc(ctxT_kept, 1)

            def qkv_scale(h, p):
                b = 2 * h + p
                wait_apart(g, pool, qkv_stats, 6 * b + 6)
                wait_free(pool, qkn_ready, b, 2, 2, apart=g)
                wait_free(pool, vn_ready, b, 2, apart=g)
                rstd_of(mv3[:, p, :, 1:2].rearrange("p a c -> p (a c)"), ve3[:, p, :], rstd3[:, p, :], 3, b, qkv_var, qkv_rstd)

            def keep_v1(h, p):
                b = 2 * h + p
                pool.wait_ge(qkv_ready, b + 1)
                nc.gpsimd.tensor_copy(g.V1[:, ds(b, 1), :].rearrange("p a k -> p (a k)"), qkv[:, p, 3 * P:4 * P]).then_inc(v1_kept, 1)

            def block_keys(h, p):
                b = 2 * h + p
                pool.wait_ge(kT_ready, 2 * b + 2)
                wait_free(pool, scores_ready, b, 2, 2)
                nc.gpsimd.tensor_tensor(kbd[:, p, :].rearrange("p (j k) -> p j k", j=HG),
                                        bcast(kT[:, p, :].unsqueeze(1), P, HG, NK),
                                        bcast(g.consts[:, C_MASK:C_MASK + HG].unsqueeze(2), P, HG, NK), ALU.mult).then_inc(kbd_ready, 1)

            def v_norm(h, p):
                b = 2 * h + p
                pool.wait_ge(qkv_rstd, b + 1)
                wait_free(pool, pv_ready, b, 2, apart=g)
                nc.gpsimd.tensor_scalar(g.vaug[:, p, :, 0:HD], qkv[:, p, 2 * P:3 * P].rearrange("p (h i) -> p h i", h=H),
                                        mv3[:, p, 2, 0:1], rstd3[:, p, 2:3], ALU.subtract, ALU.mult).then_inc(vn_ready, 1)

            def add_bo(h, p):
                b = 2 * h + p
                pool.wait_ge(xn_ready, b + 1)
                xb = g.X[:, ds(b, 1), :].rearrange("p a d -> p (a d)")
                nc.gpsimd.tensor_tensor(xb, xb, g.rows[:, R_BO0:R_BO0 + P], ALU.add).then_inc(bo_added, 1)

            def x1_scale(h, p):
                b = 2 * h + p
                wait_apart(g, pool, x1_stats, 2 * b + 2)
                wait_free(pool, xn1_ready, b, 2, apart=g)
                rstd_of(mv1[:, p, 1:2], ve1[:, p, :], rstd1[:, p, :], 1, b, x1_var, x1_rstd)

            def scatter(h, p):
                b = 2 * h + p
                wait_apart(g, pool, routed, b + 1)
                for c in range(2):
                    nc.gpsimd.indirect_dma_start(g.xs[:, :], bass.IndirectOffsetOnAxis(slot[:, p, c:c + 1], 0),
                                                 xn1[:, p, :], None).then_inc(scattered[p], 16)

            pipeline(pool, [(0, x_scale), (1, keep_ctx), (2, add_bo), (1, qkv_scale), (1, keep_v1), (4, x1_scale), (1, block_keys),
                            (2, v_norm), (5, scatter)], NB, 8)
            for p in range(2):
                pool.wait_ge(scattered[p], 32 * (NB // 2))

        @block.vector
        def _(dve):
            V = nc.vector

            def x_statistics(h, p):
                b = 2 * h + p
                wait_free(dve, xn_ready, b, 2, apart=g)
                wait_free(dve, x_rstd, b, 2, apart=g)
                st = Steps(dve, x_stats, 2, b)
                st(V.bn_stats(st6[:, p, :], g.X[:, ds(b, 1), :].rearrange("p a d -> p (a d)")))
                st.wait_apart(g)
                st(V.bn_aggr(mv[:, p, :], st6[:, p, :]))

            def x_norm(h, p):
                b = 2 * h + p
                dve.wait_ge(x_rstd, b + 1)
                wait_free(dve, xc_turned, b, 2)
                V.tensor_scalar(xn[:, p, :], g.X[:, ds(b, 1), :].rearrange("p a d -> p (a d)"), mv[:, p, 0:1], rstd[:, p, :],
                                ALU.subtract, ALU.mult).then_inc(xn_ready, 1)

            def qkv_statistics(h, p):
                b = 2 * h + p
                dve.wait_ge(projected, b + 1)
                wait_free(dve, qkn_ready, b, 2, 2)
                wait_free(dve, vn_ready, b, 2)
                wait_free(dve, v1_kept, b, 2)
                V.tensor_tensor(qkv[:, p, :], psA[:, 0:4 * P], g.rows[:, R_QKV:R_QKV + 4 * P], ALU.add).then_inc(qkv_ready, 1)
                wait_free(dve, qkv_rstd, b, 2, apart=g)
                wait_apart(g, dve, qkv_ready, b + 1)
                st = Steps(dve, qkv_stats, 6, b)
                for i in range(3):
                    st(V.bn_stats(st18[:, p, i, :], qkv[:, p, P * i:P * i + P]))
                st.wait_apart(g)
                for i in range(3):
                    st(V.bn_aggr(mv3[:, p, i, :], st18[:, p, i, :]))

            def qk_norm(h, p):
                b = 2 * h + p
                dve.wait_ge(qkv_rstd, b + 1)
                wait_free(dve, qk_turned, b, 2)
                for i in range(2):
                    V.tensor_scalar(qkn[:, p, P * i:P * i + P], qkv[:, p, P * i:P * i + P], mv3[:, p, i, 0:1], rstd3[:, p, i:i + 1],
                                    ALU.subtract, ALU.mult).then_inc(qkn_ready, 1)

            def maximum(part):
                def work(h, p):
                    b = 2 * h + p
                    dve.wait_ge(scores_ready, 2 * b + part + 1)
                    wait_free(dve, exp_ready, b, 2, 2)
                    heads = slice(8 * part, 8 * part + 8)
                    V.tensor_reduce(mx[:, p, heads].rearrange("p (g j) -> p g j", g=2),
                                    psS[:, 2 * part:2 * part + 2, 0:HG * NK].rearrange("p g (j k) -> p g j k", j=HG), AX, ALU.max).then_inc(max_ready, 1)
                    dve.wait_ge(max_ready, 2 * b + part + 1)
                    V.tensor_scalar(nmx[:, p, heads], mx[:, p, heads], -float(HD) ** -0.5, None, ALU.mult).then_inc(nmx_ready, 1)
                return work

            def out_scale(h, p):
                b = 2 * h + p
                dve.wait_ge(pv_ready, b + 1)
                av = psB[:, 0:H * (HD + 1)].rearrange("p (h i) -> p h i", h=H)
                V.reciprocal(rs[:, p, :], av[:, :, HD:HD + 1].rearrange("p h i -> p (h i)")).then_inc(rs_ready, 1)
                dve.wait_ge(rs_ready, b + 1)
                wait_free(dve, o_turned, b, 2)
                V.tensor_tensor(o[:, p, :].rearrange("p (h i) -> p h i", h=H), av[:, :, 0:HD],
                                bcast(rs[:, p, :].unsqueeze(2), P, H, HD), ALU.mult).then_inc(o_ready, 1)

            def x1_statistics(h, p):
                b = 2 * h + p
                dve.wait_ge(y_ready, b + 1)
                dve.wait_ge(bo_added, b + 1)
                xb = g.X[:, ds(b, 1), :].rearrange("p a d -> p (a d)")
                V.tensor_tensor(xb, psB[:, 3 * P:4 * P], xb, ALU.add).then_inc(x1_ready, 1)
                wait_apart(g, dve, x1_ready, b + 1)
                wait_free(dve, x1_rstd, b, 2, apart=g)
                st = Steps(dve, x1_stats, 2, b)
                st(V.bn_stats(st1[:, p, :], xb))
                st.wait_apart(g)
                st(V.bn_aggr(mv1[:, p, :], st1[:, p, :]))

            def x1_norm(h, p):
                b = 2 * h + p
                xb = g.X[:, ds(b, 1), :].rearrange("p a d -> p (a d)")
                dve.wait_ge(x1_rstd, b + 1)
                if not (isinstance(b, int) and b < 2):
                    dve.wait_ge(scattered[p], 32 * h)
                V.tensor_scalar(xn1[:, p, :], xb, mv1[:, p, 0:1], rstd1[:, p, :], ALU.subtract, ALU.mult).then_inc(xn1_ready, 1)

            def logits_shift(h, p):
                b = 2 * h + p
                dve.wait_ge(logits_ready, b + 1)
                st = Steps(dve, shift_steps, 2, b)
                st(V.tensor_reduce(lmax[:, p, :], psR[:, 0:E0], AX, ALU.max))
                st.wait()
                st(V.tensor_scalar(lg[:, p, :], psR[:, 0:E0], lmax[:, p, :], None, ALU.subtract))

            def choose(h, p):
                b = 2 * h + p
                dve.wait_ge(lg_exp, b + 1)
                st = Steps(dve, rank_steps, 9, b)
                st(V.reciprocal(erec[:, p, :], esum[:, p, :]))
                st.wait()
                st(V.tensor_scalar(pr[:, p, :], ex[:, p, :], erec[:, p, :], None, ALU.mult))
                st.wait()
                other = bcast(pr[:, p, :].unsqueeze(1), P, E0, E0)
                own = bcast(pr[:, p, :].unsqueeze(2), P, E0, E0)
                gtv, eqv = (x[:, p, :].rearrange("p (e f) -> p e f", e=E0) for x in (gt, eq))
                st(V.tensor_tensor(gtv, other, own, ALU.is_gt))
                st(V.tensor_tensor(eqv, other, own, ALU.is_equal))
                st.wait()
                st(V.tensor_tensor(eq[:, p, :], eq[:, p, :], g.consts[:, C_LT:C_LT + E0 * E0], ALU.mult))
                st.wait()
                st(V.tensor_tensor(gt[:, p, :], gt[:, p, :], eq[:, p, :], ALU.add))
                st.wait()
                st(V.tensor_reduce(rank[:, p, :], gtv, AX, ALU.add))
                st.wait()
                st(V.tensor_tensor(chosen[:, p, :].rearrange("p (c e) -> p c e", c=2), bcast(rank[:, p, :].unsqueeze(1), P, 2, E0),
                                   g.consts[:, C_K:C_K + 2 * E0].rearrange("p (c e) -> p c e", c=2), ALU.is_equal))
                wait_free(dve, counted, b, 2)
                st(V.tensor_scalar(picked[:, p, :], rank[:, p, :], 1.5, None, ALU.is_lt))

            def give_slots(h, p):
                b = 2 * h + p
                dve.wait_ge(counted, b + 1)
                dve.wait_ge(rank_steps, 9 * b + 9)
                st = Steps(dve, place_steps, 6, b)
                st(V.tensor_tensor(place[:, p, :], psR[:, 8:8 + E0], g.run[:, :], ALU.add))
                st.wait()
                st(V.tensor_tensor(g.run[:, :], psR[:, 16:16 + E0], g.run[:, :], ALU.add))
                ch = chosen[:, p, :].rearrange("p (c e) -> p c e", c=2)
                st(V.tensor_tensor(tmp[:, p, :].rearrange("p (c e) -> p c e", c=2), ch, bcast(place[:, p, :].unsqueeze(1), P, 2, E0), ALU.mult))
                st(V.tensor_tensor(tmp2[:, p, :].rearrange("p (c e) -> p c e", c=2), ch, bcast(pr[:, p, :].unsqueeze(1), P, 2, E0), ALU.mult))
                st.wait()
                st(V.tensor_reduce(slotf[:, p, :], tmp[:, p, :].rearrange("p (c e) -> p c e", c=2), AX, ALU.add))
                st(V.tensor_reduce(g.gate[:, ds(b, 1), :].rearrange("p a c -> p (a c)"), tmp2[:, p, :].rearrange("p (c e) -> p c e", c=2), AX, ALU.add))
                st.wait()
                if not (isinstance(b, int) and b < 2):
                    dve.wait_ge(scattered[p], 32 * h)
                V.tensor_copy(g.slotf[:, ds(b, 1), :].rearrange("p a c -> p (a c)"), slotf[:, p, :])
                V.tensor_copy(slot[:, p, :], slotf[:, p, :]).then_inc(routed, 1)

            pipeline(dve, [(0, x_statistics), (4, out_scale), (2, maximum(0)), (1, qkv_statistics), (5, logits_shift), (2, maximum(1)),
                           (0, x_norm), (4, x1_statistics), (1, qk_norm), (5, choose), (4, x1_norm), (5, give_slots)], NB, 8)

        @block.scalar
        def _(act):
            A = nc.scalar

            def xc_copy(h, p):
                b = 2 * h + p
                act.wait_ge(xc_turned, b + 1)
                wait_free(act, projected, b, 2)
                wait_free(act, ctxT_kept, b, 2)
                A.activation(xcT[:, p, :], psA[:, 0:2 * P], ACT.Copy).then_inc(xcT_ready, 1)

            def qk_affine(h, p):
                b = 2 * h + p
                act.wait_ge(qk_turned, b + 1)
                wait_free(act, scores_ready, b, 2, 2)
                wait_free(act, kbd_ready, b, 2)
                A.activation(qT[:, p, :], psA[:, 0:P], ACT.Identity, bias=g.cols[:, BQN:BQN + 1], scale=g.cols[:, GQ:GQ + 1]).then_inc(kT_ready, 1)
                A.activation(kT[:, p, :], psA[:, P:P + NK], ACT.Identity, bias=g.cols[:, BKN:BKN + 1], scale=g.cols[:, GK:GK + 1]).then_inc(kT_ready, 1)

            def exponential(part):
                def work(h, p):
                    b = 2 * h + p
                    act.wait_ge(nmx_ready, 2 * b + part + 1)
                    wait_free(act, p_turned, b, 2, 4)
                    for k in range(8 * part, 8 * part + 8):
                        last = A.activation(prob[:, p, NK * k:NK * k + NK], psS[:, k // HG, NK * (k % HG):NK * (k % HG) + NK], ACT.Exp,
                                            bias=nmx[:, p, k:k + 1], scale=float(HD) ** -0.5)
                    last.then_inc(exp_ready, 1)
                return work

            def p_copy(c):
                def work(h, p):
                    b = 2 * h + p
                    act.wait_ge(p_turned, 4 * b + c + 1)
                    wait_free(act, pv_ready, b, 2)
                    A.activation(pT[0:NK, p, 4 * P * c:4 * P * c + 4 * P], psT[0:NK, :], ACT.Copy).then_inc(pT_ready, 1)
                return work

            def o_affine(h, p):
                b = 2 * h + p
                act.wait_ge(o_turned, b + 1)
                wait_free(act, y_ready, b, 2)
                A.activation(oT[:, p, :], psB[:, 2 * P:3 * P], ACT.Identity, bias=g.cols[:, BVN:BVN + 1], scale=g.cols[:, GV:GV + 1]).then_inc(oT_ready, 1)

            def xn1_copy(h, p):
                b = 2 * h + p
                act.wait_ge(xn1_turned, b + 1)
                wait_free(act, logits_ready, b, 2)
                A.activation(xn1T[:, p, :], psR[:, P:2 * P], ACT.Copy).then_inc(xn1T_ready, 1)

            def logits_exp(h, p):
                b = 2 * h + p
                act.wait_ge(shift_steps, 2 * b + 2)
                wait_free(act, rank_steps, b, 2, 9)
                A.activation(ex[:, p, :], lg[:, p, :], ACT.Exp, accum_out=esum[:, p, :]).then_inc(lg_exp, 1)

            pipeline(act, [(1, xc_copy), (5, xn1_copy), (3, p_copy(0)), (4, o_affine), (2, exponential(0)), (3, p_copy(1)), (5, logits_exp),
                           (3, p_copy(2)), (1, qk_affine), (2, exponential(1)), (3, p_copy(3))], NB, 8)

        @block.tensor
        def _(pe):
            T = nc.tensor
            ident = g.consts[:, C_ID:C_ID + P]

            def turn_xc(h, p):
                b = 2 * h + p
                wait_free(pe, kT_ready, b, 1, 2)
                pe.wait_ge(xn_ready, b + 1)
                pe.wait_ge(ctx_in[p], 16 * h + 16)
                T.transpose(psA[:, 0:P], xn[:, p, :], ident)
                T.transpose(psA[:, P:2 * P], g.cstage[:, p, :], ident).then_inc(xc_turned, 1)

            def project(h, p):
                b = 2 * h + p
                pe.wait_ge(xcT_ready, b + 1)
                T.matmul(psA[:, 0:P], xcT[:, p, 0:P], g.w_ctx[:, 0:P], start=True, stop=True)
                T.matmul(psA[:, P:4 * P], xcT[:, p, P:2 * P], g.w_ctx[:, P:4 * P], start=True, stop=True).then_inc(projected, 1)

            def turn_qk(h, p):
                b = 2 * h + p
                pe.wait_ge(qkv_ready, b + 1)
                pe.wait_ge(qkn_ready, 2 * b + 2)
                T.transpose(psA[:, 0:P], qkn[:, p, 0:P], ident)
                T.transpose(psA[:, P:2 * P], qkn[:, p, P:2 * P], ident).then_inc(qk_turned, 1)

            def scores(part):
                def work(h, p):
                    b = 2 * h + p
                    pe.wait_ge(kbd_ready, b + 1)
                    pe.wait_ge(kT_ready, 2 * b + 2)
                    if not (isinstance(b, int) and b < 1):
                        pe.wait_ge(exp_ready, 2 * b - 1 + part)
                    for i in range(2 * part, 2 * part + 2):
                        last = T.matmul(psS[:, i, 0:HG * NK], qT[32 * i:32 * i + 32, p, :], kbd[32 * i:32 * i + 32, p, :], start=True, stop=True)
                    last.then_inc(scores_ready, 1)
                return work

            def turn_p(c):
                def work(h, p):
                    b = 2 * h + p
                    pe.wait_ge(exp_ready, 2 * b + 1 + c // 2)
                    if not (isinstance(b, int) and b == c == 0):
                        pe.wait_ge(pT_ready, 4 * b + c)
                    for i in range(4):
                        k = 4 * c + i
                        last = T.transpose(psT[0:NK, P * i:P * i + P], prob[:, p, NK * k:NK * k + NK], ident)
                    last.then_inc(p_turned, 1)
                return work

            def weigh(h, p):
                b = 2 * h + p
                pe.wait_ge(pT_ready, 4 * b + 4)
                pe.wait_ge(vn_ready, b + 1)
                wait_free(pe, x1_ready, b, 1)
                for k in range(H):
                    last = T.matmul(psB[:, (HD + 1) * k:(HD + 1) * (k + 1)], pT[0:NK, p, P * k:P * k + P], g.vaug[0:NK, p, k, :], start=True, stop=True)
                last.then_inc(pv_ready, 1)

            def turn_o(h, p):
                b = 2 * h + p
                pe.wait_ge(o_ready, b + 1)
                T.transpose(psB[:, 2 * P:3 * P], o[:, p, :], ident).then_inc(o_turned, 1)

            def out_project(h, p):
                b = 2 * h + p
                pe.wait_ge(oT_ready, b + 1)
                T.matmul(psB[:, 3 * P:4 * P], oT[:, p, :], g.w_small[:, 0:P], start=True, stop=True).then_inc(y_ready, 1)

            def turn_xn1(h, p):
                b = 2 * h + p
                wait_free(pe, place_steps, b, 1, 6)
                pe.wait_ge(xn1_ready, b + 1)
                T.transpose(psR[:, P:2 * P], xn1[:, p, :], ident).then_inc(xn1_turned, 1)

            def route(h, p):
                b = 2 * h + p
                pe.wait_ge(xn1T_ready, b + 1)
                T.matmul(psR[:, 0:E0], xn1T[:, p, :], g.w_small[:, P:P + E0], start=True, stop=True).then_inc(logits_ready, 1)

            def count(h, p):
                b = 2 * h + p
                pe.wait_ge(rank_steps, 9 * b + 9)
                T.matmul(psR[:, 8:8 + E0], g.consts[:, C_TRI:C_TRI + P], picked[:, p, :], start=True, stop=True)
                T.matmul(psR[:, 16:16 + E0], g.consts[:, C_ONE:C_ONE + P], picked[:, p, :], start=True, stop=True).then_inc(counted, 1)

            pipeline(pe, [(1, turn_xc), (4, weigh), (2, scores(0)), (5, turn_xn1), (1, project), (3, turn_p(0)), (2, scores(1)), (4, turn_o),
                          (5, route), (3, turn_p(1)), (4, out_project), (3, turn_p(2)), (1, turn_qk), (5, count), (3, turn_p(3))], NB, 8)


def tables(nc, g):
    with ExitStack() as ctx:
        def sb(name, shape, dt=F32):
            return ctx.enter_context(nc.sbuf_tensor(name, shape, dt))

        count, tiles_i, tiles, upto, upto2, before = (sb("count", [P, E0]), sb("tiles_i", [P, E0], I32), sb("tiles", [P, E0]),
                                                      sb("upto", [P, E0]), sb("upto2", [P, E0]), sb("before", [P, E0]))
        pad_f, pad = sb("pad_f", [P, E0]), sb("pad", [P, E0], I32)
        past, te, used, hot = sb("past", [P, NT * E0]), sb("te", [P, NT]), sb("used", [P, NT]), sb("hot", [P, NT * E0])
        first, row, tab, moved, step = (sb("first", [P, NT]), sb("row", [P, NT]), sb("tab", [P, 2 * NT]), sb("moved", [P, E0]), sb("step", [P, E0]))
        over, shift_by = sb("over", [P, 2 * NB * E0]), sb("shift_by", [P, 2 * NB])
        table_steps, pads_ready = ctx.enter_context(nc.semaphore("table_steps")), ctx.enter_context(nc.semaphore("pads_ready"))
        padded = ctx.enter_context(nc.semaphore("padded"))
        block = ctx.enter_context(nc.Block())

        @block.vector
        def _(dve):
            V = nc.vector
            st = Steps(dve, table_steps, 0, 0)

            def do(instruction):
                st(instruction)
                st.wait()

            do(V.tensor_scalar(pad_f[:, :], g.run[:, :], g.consts[:, C_P:C_P + 1], None, ALU.add))
            V.tensor_copy(pad[:, :], pad_f[:, :]).then_inc(pads_ready, 1)
            do(V.tensor_tensor(count[:, :], g.run[:, :], g.consts[:, C_RUN:C_RUN + E0], ALU.subtract))
            do(V.tensor_scalar(count[:, :], count[:, :], float(P - 1), None, ALU.add))
            do(V.tensor_copy(tiles_i[:, :], count[:, :]))
            do(V.tensor_scalar(tiles_i[:, :], tiles_i[:, :], 7, None, ALU.logical_shift_right))
            do(V.tensor_copy(tiles[:, :], tiles_i[:, :]))
            a, b = tiles, upto
            do(V.tensor_copy(upto[:, :], tiles[:, :]))
            do(V.tensor_copy(upto2[:, :], tiles[:, :]))
            a, b = upto, upto2
            for shift in (1, 2, 4):
                do(V.tensor_copy(b[:, 0:shift], a[:, 0:shift]))
                do(V.tensor_tensor(b[:, shift:E0], a[:, shift:E0], a[:, 0:E0 - shift], ALU.add))
                a, b = b, a
            do(V.tensor_tensor(before[:, :], a[:, :], tiles[:, :], ALU.subtract))
            jrow = g.consts[:, C_J:C_J + NT]
            pastv, hotv = (x[:, :].rearrange("p (j e) -> p j e", j=NT) for x in (past, hot))
            do(V.tensor_tensor(pastv, bcast(a[:, :].unsqueeze(1), P, NT, E0), bcast(jrow.unsqueeze(2), P, NT, E0), ALU.is_le))
            do(V.tensor_reduce(te[:, :], pastv, AX, ALU.add))
            do(V.tensor_scalar(used[:, :], te[:, :], E0 - 0.5, None, ALU.is_lt))
            do(V.tensor_scalar(tab[:, 0:NT], te[:, :], float(E0 - 1), None, ALU.min))
            do(V.tensor_tensor(hotv, bcast(tab[:, 0:NT].unsqueeze(2), P, NT, E0),
                               bcast(g.consts[:, C_J:C_J + E0].unsqueeze(1), P, NT, E0), ALU.is_equal))
            do(V.tensor_tensor(hotv, hotv, bcast(before[:, :].unsqueeze(1), P, NT, E0), ALU.mult))
            do(V.tensor_reduce(first[:, :], hotv, AX, ALU.add))
            do(V.tensor_tensor(first[:, :], jrow, first[:, :], ALU.subtract))
            do(V.tensor_scalar(first[:, :], first[:, :], float(P), None, ALU.mult))
            do(V.tensor_scalar(row[:, :], tab[:, 0:NT], float(REGION), None, ALU.mult))
            do(V.tensor_tensor(row[:, :], row[:, :], first[:, :], ALU.add))
            do(V.tensor_scalar(row[:, :], row[:, :], float(ZERO_ROW), None, ALU.subtract))
            do(V.tensor_tensor(row[:, :], row[:, :], used[:, :], ALU.mult))
            do(V.tensor_scalar(tab[:, NT:2 * NT], row[:, :], float(ZERO_ROW), None, ALU.add))
            do(V.tensor_copy(g.table[:, :], tab[:, :]))
            starts = g.consts[:, C_RUN:C_RUN + E0]
            do(V.tensor_scalar(moved[:, :], before[:, :], float(P), None, ALU.mult))
            do(V.tensor_tensor(moved[:, :], moved[:, :], starts, ALU.subtract))
            do(V.tensor_copy(step[:, 0:1], moved[:, 0:1]))
            do(V.tensor_tensor(step[:, 1:E0], moved[:, 1:E0], moved[:, 0:E0 - 1], ALU.subtract))
            slots = g.slotf[:, :, :].rearrange("p b c -> p (b c)")
            overv = over[:, :].rearrange("p (s e) -> p s e", e=E0)
            do(V.tensor_tensor(overv, bcast(slots.unsqueeze(2), P, 2 * NB, E0), bcast(starts.unsqueeze(1), P, 2 * NB, E0), ALU.is_ge))
            do(V.tensor_tensor(overv, overv, bcast(step[:, :].unsqueeze(1), P, 2 * NB, E0), ALU.mult))
            do(V.tensor_reduce(shift_by[:, :], overv, AX, ALU.add))
            do(V.tensor_tensor(g.slots[:, :, :].rearrange("p b c -> p (b c)"), shift_by[:, :], slots, ALU.add))

        @block.gpsimd
        def _(pool):
            pool.wait_ge(pads_ready, 1)
            for e in range(E0):
                nc.gpsimd.indirect_dma_start(g.xs[:, :], bass.IndirectOffsetOnAxis(pad[:, e:e + 1], 0),
                                             g.zeros[:, :], None).then_inc(padded, 16)
            pool.wait_ge(padded, 16 * E0)


def experts0(nc, g):
    with ExitStack() as ctx:
        def sb(name, shape, dt=F32):
            return ctx.enter_context(nc.sbuf_tensor(name, shape, dt))

        def sem(name):
            return ctx.enter_context(nc.semaphore(name))

        xt, xtT = sb("xt", [P, 2, P]), sb("xtT", [P, 2, P])
        zg, y, z1, hid, hT, yt = (sb("zg", [P, 2, F0]), sb("y", [P, 2, F0]), sb("z1", [P, 2, F0]), sb("hid", [P, 2, F0]), sb("hT", [P, 2, F0]), sb("yt", [P, 2, P]))
        w_up, w_down, b_row, b_down = sb("w_up0", [P, E0, 2 * F0]), sb("w_down0", [P, E0, FC * P]), sb("b_row0", [P, E0, 2 * F0]), sb("b_down0", [P, E0, P])
        weights_in = sem("weights_in")
        rows_in, rows_out = [sem("rows_in_even"), sem("rows_in_odd")], [sem("rows_out_even"), sem("rows_out_odd")]
        turned, xtT_ready, zg_done, z1_done = sem("x_turned"), sem("xtT_ready"), sem("zg_done"), sem("z1_done")
        zg_ready, z1_ready, y_ready, hid_ready = sem("zg_ready"), sem("z1_ready"), sem("gelu_ready"), sem("hid_ready")
        h_turned, hT_ready, down_done, yt_ready = sem("h_turned"), sem("hT_ready"), sem("down_done"), sem("yt_ready")
        block = ctx.enter_context(nc.Block())
        psX, psH, psY = g.bank[0], g.bank[5], g.bank[6]
        psG, psZ = [g.bank[1], g.bank[2]], [g.bank[3], g.bank[4]]

        @block.sync
        def _(sp):
            sp.dma_start(w_up[:, 0:4, :], g.d_w_up0[:, 0:4, :]).then_inc(weights_in, 16)
            sp.dma_start(w_up[:, 4:8, :], g.d_w_up0[:, 4:8, :]).then_inc(weights_in, 16)
            sp.dma_start(w_down[:, :, :], g.d_w_down0).then_inc(weights_in, 16)

            def load_rows(h, p):
                j = 2 * h + p
                wait_free(sp, turned, j, 2)
                row = sp.value_load(g.table[0:1, ds(NT + j, 1)], min_val=0, max_val=ZERO_ROW)
                sp.dma_start(xt[:, p, :], g.xs[ds(row, P), :]).then_inc(rows_in[p], 16)

            def store_rows(h, p):
                j = 2 * h + p
                sp.wait_ge(yt_ready, j + 1)
                sp.dma_start(g.ys[ds(P * j, P), :], yt[:, p, :]).then_inc(rows_out[p], 16)
            pipeline(sp, [(0, load_rows), (4, store_rows)], NT, 6)
            for p in range(2):
                sp.wait_ge(rows_out[p], 16 * (NT // 2))

        @block.scalar
        def _(act):
            act.dma_start(b_row[:, :, :].rearrange("p e f -> p (e f)"), g.d_b_row0.partition_broadcast(P)).then_inc(weights_in, 16)
            act.dma_start(b_down[:, :, :].rearrange("p e f -> p (e f)"), g.d_b_down0.partition_broadcast(P)).then_inc(weights_in, 16)

            def x_copy(h, p):
                j = 2 * h + p
                act.wait_ge(turned, j + 1)
                wait_free(act, z1_done, j, 2)
                nc.scalar.activation(xtT[:, p, :], psX[:, 0:P], ACT.Copy).then_inc(xtT_ready, 1)

            def gelu(h, p):
                j = 2 * h + p
                act.wait_ge(zg_ready, j + 1)
                wait_free(act, hid_ready, j, 2)
                nc.scalar.activation(y[:, p, :], zg[:, p, :], ACT.Gelu).then_inc(y_ready, 1)

            def hid_copy(h, p):
                j = 2 * h + p
                act.wait_ge(h_turned, j + 1)
                wait_free(act, down_done, j, 2)
                nc.scalar.activation(hT[:, p, :], psH[:, :], ACT.Copy).then_inc(hT_ready, 1)
            pipeline(act, [(1, x_copy), (3, hid_copy), (2, gelu)], NT, 6)

        @block.tensor
        def _(pe):
            T = nc.tensor
            ident = g.consts[:, C_ID:C_ID + P]
            pe.wait_ge(weights_in, 48 + 32)

            def turn_x(h, p):
                j = 2 * h + p
                pe.wait_ge(rows_in[p], 16 * h + 16)
                wait_free(pe, xtT_ready, j, 1)
                T.transpose(psX[:, 0:P], xt[:, p, :], ident).then_inc(turned, 1)

            def up(h, p):
                j = 2 * h + p
                e = pe.value_load(g.table[0:1, ds(j, 1)], min_val=0, max_val=E0 - 1)
                pe.wait_ge(xtT_ready, j + 1)
                wait_free(pe, zg_ready, j, 2)
                wait_free(pe, z1_ready, j, 2)
                T.matmul(psG[p][:, :], xtT[:, p, :], w_up[:, ds(e, 1), 0:F0].rearrange("p a f -> p (a f)"), start=True, stop=True).then_inc(zg_done, 1)
                T.matmul(psZ[p][:, :], xtT[:, p, :], w_up[:, ds(e, 1), F0:2 * F0].rearrange("p a f -> p (a f)"), start=True, stop=True).then_inc(z1_done, 1)

            def turn_hid(h, p):
                j = 2 * h + p
                pe.wait_ge(hid_ready, j + 1)
                wait_free(pe, hT_ready, j, 1)
                for c in range(FC):
                    last = T.transpose(psH[:, P * c:P * c + P], hid[:, p, P * c:P * c + P], ident)
                last.then_inc(h_turned, 1)

            def down(h, p):
                j = 2 * h + p
                e = pe.value_load(g.table[0:1, ds(j, 1)], min_val=0, max_val=E0 - 1)
                pe.wait_ge(hT_ready, j + 1)
                wait_free(pe, yt_ready, j, 1)
                for c in range(FC):
                    last = T.matmul(psY[:, 0:P], hT[:, p, P * c:P * c + P], w_down[:, ds(e, 1), P * c:P * c + P].rearrange("p a f -> p (a f)"),
                                    start=c == 0, stop=c == FC - 1)
                last.then_inc(down_done, 1)
            pipeline(pe, [(1, turn_x), (3, turn_hid), (1, up), (3, down)], NT, 6)

        @block.vector
        def _(dve):
            V = nc.vector
            dve.wait_ge(weights_in, 48 + 32)

            def add_bias(h, p):
                j = 2 * h + p
                e = dve.value_load(g.table[0:1, ds(j, 1)], min_val=0, max_val=E0 - 1)
                dve.wait_ge(zg_done, j + 1)
                wait_free(dve, y_ready, j, 2)
                V.tensor_tensor(zg[:, p, :], psG[p][:, :], b_row[:, ds(e, 1), 0:F0].rearrange("p a f -> p (a f)"), ALU.add).then_inc(zg_ready, 1)
                dve.wait_ge(z1_done, j + 1)
                wait_free(dve, hid_ready, j, 2)
                V.tensor_tensor(z1[:, p, :], psZ[p][:, :], b_row[:, ds(e, 1), F0:2 * F0].rearrange("p a f -> p (a f)"), ALU.add).then_inc(z1_ready, 1)

            def multiply(h, p):
                j = 2 * h + p
                dve.wait_ge(y_ready, j + 1)
                dve.wait_ge(z1_ready, j + 1)
                wait_free(dve, h_turned, j, 2)
                V.tensor_tensor(hid[:, p, :], y[:, p, :], z1[:, p, :], ALU.mult).then_inc(hid_ready, 1)

            def down_bias(h, p):
                j = 2 * h + p
                e = dve.value_load(g.table[0:1, ds(j, 1)], min_val=0, max_val=E0 - 1)
                dve.wait_ge(down_done, j + 1)
                if not (isinstance(j, int) and j < 2):
                    dve.wait_ge(rows_out[p], 16 * h)
                V.tensor_tensor(yt[:, p, :], psY[:, 0:P], b_down[:, ds(e, 1), :].rearrange("p a f -> p (a f)"), ALU.add).then_inc(yt_ready, 1)
            pipeline(dve, [(2, multiply), (1, add_bias), (3, down_bias)], NT, 6)


def attention1(nc, g):
    with ExitStack() as ctx:
        def sb(name, shape, dt=F32):
            return ctx.enter_context(nc.sbuf_tensor(name, shape, dt))

        def sem(name):
            return ctx.enter_context(nc.semaphore(name))

        idx, got = sb("idx", [P, 2, 2], I32), sb("got", [P, 2, 2 * P])
        st2, mv2, ve2, rstd2 = sb("st2", [P, 2, 6]), sb("mv2", [P, 2, 2]), sb("ve2", [P, 2, 1]), sb("rstd2", [P, 2, 1])
        xn2, xn2T, q1T, k1T = sb("xn2", [P, 2, P]), sb("xn2T", [P, 2, P]), sb("q1T", [P, 2, P]), sb("k1T", [P, 2, NK])
        mx1, p1, den, rden, p1T, r, rT = (sb("mx1", [P, 2, 1]), sb("p1", [P, 2, NK]), sb("den", [P, 2, 1]), sb("rden", [P, 2, 1]),
                                          sb("p1T", [P, 2, P]), sb("r", [P, 2, P]), sb("rT", [P, 2, P]))
        st3, mv3, ve3, rstd3 = sb("st3", [P, 2, 6]), sb("mv3_", [P, 2, 2]), sb("ve3_", [P, 2, 1]), sb("rstd3_", [P, 2, 1])
        xn3, xn3T = sb("xn3", [P, 2, P]), sb("xn3T", [P, 2, P])
        biased, top, rest, mask = sb("biased", [P, 2, E1]), sb("top", [P, 2, 8]), sb("rest", [P, 2, E1]), sb("mask", [P, 2, E1])
        en, sig, ws, wsum = sb("en", [P, 2, E1]), sb("sig", [P, 2, E1]), sb("ws", [P, 2, E1]), sb("wsum", [P, 2, 1])
        cw, low, parts = sb("cw", [P, 2, E1]), sb("low", [P, 2, E1]), sb("parts", [P, 2, 2 * E1], F16)

        psA, psB, psC, psD, psE = g.bank[0], g.bank[1], g.bank[2], g.bank[3], [g.bank[4], g.bank[5]]
        psG16 = g.bank[6].bitcast(F16)
        gathered = [sem("gathered_even"), sem("gathered_odd")]
        idx_ready, comb_steps, x2_stats, x2_var, x2_rstd, xn2_ready = sem("idx_ready"), sem("comb_steps"), sem("x2_stats"), sem("x2_var"), sem("x2_rstd"), sem("xn2_ready")
        xn2_turned, xn2T_ready, qk_done, k1T_ready, s_done = sem("xn2_turned"), sem("xn2T_ready"), sem("qk_done"), sem("k1T_ready"), sem("s_done")
        mx1_steps, p1_ready, p1_turned, p1T_ready, av_done = sem("mx1_steps"), sem("p1_ready"), sem("p1_turned"), sem("p1T_ready"), sem("av_done")
        rden_ready, r_ready, r_turned, rT_ready, o1_done, bo1_added = sem("rden_ready"), sem("r_ready"), sem("r_turned"), sem("rT_ready"), sem("o1_done"), sem("bo1_added")
        x3_ready, x3_stats, x3_var, x3_rstd, xn3_ready, xn3_turned = sem("x3_ready"), sem("x3_stats"), sem("x3_var"), sem("x3_rstd"), sem("xn3_ready"), sem("xn3_turned")
        xn3T_ready, xn3T_kept, aff_done, en_ready, top_steps, cw_steps = sem("xn3T_ready"), sem("xn3T_kept"), sem("aff_done"), sem("en_ready"), sem("top_steps"), sem("cw_steps")
        parts_ready, parts_turned, cwT_ready = sem("parts_ready"), sem("parts_turned"), sem("cwT_ready")
        block = ctx.enter_context(nc.Block())

        @block.gpsimd
        def _(pool):
            def rstd_of(var, var_eps, out, b, steps, ready):
                st = Steps(pool, steps, 1, b)
                st(nc.gpsimd.tensor_scalar(var_eps, var, EPS, None, ALU.add))
                st.wait()
                nc.gpsimd.tensor_tensor(out, var_eps, g.mhalf[:, 0:1], ALU.pow).then_inc(ready, 1)

            def gather(h, p):
                b = 2 * h + p
                wait_apart(g, pool, idx_ready, b + 1)
                wait_free(pool, comb_steps, b, 2, 2, apart=g)
                for c in range(2):
                    nc.gpsimd.indirect_dma_start(got[:, p, P * c:P * c + P], None, g.ys[:, :],
                                                 bass.IndirectOffsetOnAxis(idx[:, p, c:c + 1], 0)).then_inc(gathered[p], 16)

            def x2_scale(h, p):
                b = 2 * h + p
                wait_apart(g, pool, x2_stats, 2 * b + 2)
                wait_free(pool, xn2_ready, b, 2, apart=g)
                rstd_of(mv2[:, p, 1:2], ve2[:, p, :], rstd2[:, p, :], b, x2_var, x2_rstd)

            def add_bo(h, p):
                b = 2 * h + p
                pool.wait_ge(xn2_ready, b + 1)
                xb = g.X[:, ds(b, 1), :].rearrange("p a d -> p (a d)")
                nc.gpsimd.tensor_tensor(xb, xb, g.rows[:, R_BO1:R_BO1 + P], ALU.add).then_inc(bo1_added, 1)

            def x3_scale(h, p):
                b = 2 * h + p
                wait_apart(g, pool, x3_stats, 2 * b + 2)
                wait_free(pool, xn3_ready, b, 2, apart=g)
                rstd_of(mv3[:, p, 1:2], ve3[:, p, :], rstd3[:, p, :], b, x3_var, x3_rstd)

            def keep_xn3(h, p):
                b = 2 * h + p
                pool.wait_ge(xn3T_ready, b + 1)
                nc.gpsimd.tensor_copy(g.XT[:, ds(b, 1), :].rearrange("p a t -> p (a t)"), xn3T[:, p, :]).then_inc(xn3T_kept, 1)
            pipeline(pool, [(0, gather), (2, add_bo), (1, x2_scale), (5, keep_xn3), (4, x3_scale)], NB, 8)

        @block.vector
        def _(dve):
            V = nc.vector

            def copy_slots(h, p):
                b = 2 * h + p
                if not (isinstance(b, int) and b < 2):
                    dve.wait_ge(gathered[p], 32 * h)
                V.tensor_copy(idx[:, p, :], g.slots[:, ds(b, 1), :].rearrange("p a c -> p (a c)")).then_inc(idx_ready, 1)

            def combine(h, p):
                b = 2 * h + p
                dve.wait_ge(gathered[p], 32 * h + 32)
                xb = g.X[:, ds(b, 1), :].rearrange("p a d -> p (a d)")
                st = Steps(dve, comb_steps, 2, b)
                for c in range(2):
                    st(V.scalar_tensor_tensor(xb, got[:, p, P * c:P * c + P], g.gate[:, ds(b, 1), c:c + 1].rearrange("p a c -> p (a c)"), xb, ALU.mult, ALU.add))
                    st.wait_apart(g)
                wait_free(dve, x2_rstd, b, 2, apart=g)
                st = Steps(dve, x2_stats, 2, b)
                st(V.bn_stats(st2[:, p, :], xb))
                st.wait_apart(g)
                wait_free(dve, xn2_ready, b, 2, apart=g)
                st(V.bn_aggr(mv2[:, p, :], st2[:, p, :]))

            def x2_norm(h, p):
                b = 2 * h + p
                xb = g.X[:, ds(b, 1), :].rearrange("p a d -> p (a d)")
                dve.wait_ge(x2_rstd, b + 1)
                wait_free(dve, xn2_turned, b, 2)
                wait_free(dve, r_ready, b, 2)
                V.tensor_scalar(xn2[:, p, :], xb, mv2[:, p, 0:1], rstd2[:, p, :], ALU.subtract, ALU.mult).then_inc(xn2_ready, 1)

            def maximum(h, p):
                b = 2 * h + p
                dve.wait_ge(s_done, b + 1)
                wait_free(dve, p1_ready, b, 2)
                st = Steps(dve, mx1_steps, 2, b)
                st(V.tensor_reduce(mx1[:, p, :], psE[p][:, 0:NK], AX, ALU.max))
                st.wait()
                st(V.tensor_scalar(mx1[:, p, :], mx1[:, p, :], -float(P) ** -0.5, None, ALU.mult))

            def p_copy(h, p):
                b = 2 * h + p
                dve.wait_ge(p1_ready, b + 1)
                wait_free(dve, r_ready, b, 2)
                V.reciprocal(rden[:, p, :], den[:, p, :]).then_inc(rden_ready, 1)
                dve.wait_ge(p1_turned, b + 1)
                wait_free(dve, av_done, b, 2)
                V.tensor_copy(p1T[0:NK, p, :], psB[0:NK, 0:P]).then_inc(p1T_ready, 1)

            def attended(h, p):
                b = 2 * h + p
                dve.wait_ge(av_done, b + 1)
                dve.wait_ge(rden_ready, b + 1)
                dve.wait_ge(xn2_ready, b + 1)
                wait_free(dve, r_turned, b, 2)
                V.scalar_tensor_tensor(r[:, p, :], psB[:, P:2 * P], rden[:, p, :], xn2[:, p, :], ALU.mult, ALU.add).then_inc(r_ready, 1)

            def x3_statistics(h, p):
                b = 2 * h + p
                dve.wait_ge(o1_done, b + 1)
                dve.wait_ge(bo1_added, b + 1)
                xb = g.X[:, ds(b, 1), :].rearrange("p a d -> p (a d)")
                V.tensor_tensor(xb, psC[:, P:2 * P], xb, ALU.add).then_inc(x3_ready, 1)
                wait_apart(g, dve, x3_ready, b + 1)
                wait_free(dve, x3_rstd, b, 2, apart=g)
                st = Steps(dve, x3_stats, 2, b)
                st(V.bn_stats(st3[:, p, :], xb))
                st.wait_apart(g)
                wait_free(dve, xn3_ready, b, 2, apart=g)
                st(V.bn_aggr(mv3[:, p, :], st3[:, p, :]))

            def x3_norm(h, p):
                b = 2 * h + p
                xb = g.X[:, ds(b, 1), :].rearrange("p a d -> p (a d)")
                dve.wait_ge(x3_rstd, b + 1)
                wait_free(dve, xn3_turned, b, 2)
                V.tensor_scalar(xn3[:, p, :], xb, mv3[:, p, 0:1], rstd3[:, p, :], ALU.subtract, ALU.mult).then_inc(xn3_ready, 1)

            def choose(h, p):
                b = 2 * h + p
                dve.wait_ge(aff_done, b + 1)
                st = Steps(dve, top_steps, 4, b)
                st(V.tensor_tensor(biased[:, p, :], psD[:, 0:E1], g.rows[:, R_EB:R_EB + E1], ALU.add))
                st.wait_apart(g)
                st(V.max(top[:, p, :], biased[:, p, :]))
                st.wait_apart(g)
                st(V.match_replace(rest[:, p, :], top[:, p, :], biased[:, p, :], -3.0e38))
                st.wait()
                st(V.tensor_tensor(mask[:, p, :], biased[:, p, :], rest[:, p, :], ALU.not_equal))

            def weights(h, p):
                b = 2 * h + p
                dve.wait_ge(top_steps, 4 * b + 4)
                dve.wait_ge(en_ready, b + 1)
                st = Steps(dve, cw_steps, 9, b)
                st(V.tensor_scalar(sig[:, p, :], en[:, p, :], 1.0, None, ALU.add))
                st.wait()
                st(V.reciprocal(sig[:, p, :], sig[:, p, :]))
                st.wait()
                st(V.tensor_tensor(ws[:, p, :], sig[:, p, :], mask[:, p, :], ALU.mult))
                st.wait()
                st(V.tensor_reduce(wsum[:, p, :], ws[:, p, :], AX, ALU.add))
                st.wait()
                st(V.tensor_scalar(wsum[:, p, :], wsum[:, p, :], 1e-8, None, ALU.add))
                st.wait()
                st(V.reciprocal(wsum[:, p, :], wsum[:, p, :]))
                st.wait()
                st(V.tensor_scalar(cw[:, p, :], ws[:, p, :], wsum[:, p, :], None, ALU.mult))
                st.wait()
                wait_free(dve, parts_turned, b, 2)
                st(V.tensor_copy(parts[:, p, 0:E1], cw[:, p, :]))
                st.wait()
                st(V.tensor_tensor(low[:, p, :], cw[:, p, :], parts[:, p, 0:E1], ALU.subtract))
                st.wait()
                V.tensor_scalar(parts[:, p, E1:2 * E1], low[:, p, :], 2048.0, None, ALU.mult).then_inc(parts_ready, 1)
            pipeline(dve, [(0, copy_slots), (3, maximum), (1, combine), (3, p_copy), (4, x3_statistics), (5, choose), (3, attended),
                           (1, x2_norm), (4, x3_norm), (5, weights)], NB, 8)

        @block.scalar
        def _(act):
            A = nc.scalar

            def xn2_copy(h, p):
                b = 2 * h + p
                act.wait_ge(xn2_turned, b + 1)
                wait_free(act, qk_done, b, 2)
                A.activation(xn2T[:, p, :], psA[:, 0:P], ACT.Copy).then_inc(xn2T_ready, 1)

            def qk_bias(h, p):
                b = 2 * h + p
                act.wait_ge(qk_done, b + 1)
                wait_free(act, s_done, b, 2)
                A.activation(q1T[:, p, :], psA[:, P:2 * P], ACT.Identity, bias=g.cols[:, BQ1:BQ1 + 1]).then_inc(k1T_ready, 1)
                A.activation(k1T[:, p, :], psA[:, 2 * P:2 * P + NK], ACT.Identity, bias=g.cols[:, BK1:BK1 + 1]).then_inc(k1T_ready, 1)

            def exponential(h, p):
                b = 2 * h + p
                act.wait_ge(mx1_steps, 2 * b + 2)
                wait_free(act, p1_turned, b, 2)
                wait_free(act, rden_ready, b, 2)
                A.activation(p1[:, p, :], psE[p][:, 0:NK], ACT.Exp, bias=mx1[:, p, :], scale=float(P) ** -0.5,
                             accum_out=den[:, p, :]).then_inc(p1_ready, 1)

            def r_copy(h, p):
                b = 2 * h + p
                act.wait_ge(r_turned, b + 1)
                wait_free(act, o1_done, b, 2)
                A.activation(rT[:, p, :], psC[:, 0:P], ACT.Copy).then_inc(rT_ready, 1)

            def xn3_copy(h, p):
                b = 2 * h + p
                act.wait_ge(xn3_turned, b + 1)
                wait_free(act, aff_done, b, 2)
                wait_free(act, xn3T_kept, b, 2)
                A.activation(xn3T[:, p, :], psD[:, P:2 * P], ACT.Copy).then_inc(xn3T_ready, 1)

            def aff_exp(h, p):
                b = 2 * h + p
                act.wait_ge(top_steps, 4 * b + 1)
                wait_free(act, cw_steps, b, 2, 9)
                A.activation(en[:, p, :], psD[:, 0:E1], ACT.Exp, scale=-1.0).then_inc(en_ready, 1)

            def cw_copy(h, p):
                b = 2 * h + p
                act.wait_ge(parts_turned, b + 1)
                A.activation(g.CWT[:, ds(b, 1), :].rearrange("p a t -> p (a t)"), psG16[:, 0:P], ACT.Copy).then_inc(cwT_ready, 1)
            pipeline(act, [(3, exponential), (2, xn2_copy), (4, r_copy), (5, xn3_copy), (2, qk_bias), (5, aff_exp), (5, cw_copy)], NB, 8)

        @block.tensor
        def _(pe):
            T = nc.tensor
            ident = g.consts[:, C_ID:C_ID + P]
            wo1, cent, wq1, wk1 = (g.w_small[:, 136:264], g.w_small[:, 264:328], g.w_small[:, 328:456], g.w_small[:, 456:584])

            def turn_xn2(h, p):
                b = 2 * h + p
                pe.wait_ge(xn2_ready, b + 1)
                wait_free(pe, k1T_ready, b, 1, 2)
                T.transpose(psA[:, 0:P], xn2[:, p, :], ident).then_inc(xn2_turned, 1)

            def project(h, p):
                b = 2 * h + p
                pe.wait_ge(xn2T_ready, b + 1)
                T.matmul(psA[:, P:2 * P], wq1, xn2T[:, p, :], start=True, stop=True)
                T.matmul(psA[:, 2 * P:2 * P + NK], wk1, g.ctxT[:, ds(b, 1), :].rearrange("p a k -> p (a k)"), start=True, stop=True).then_inc(qk_done, 1)

            def scores(h, p):
                b = 2 * h + p
                pe.wait_ge(k1T_ready, 2 * b + 2)
                wait_free(pe, p1_ready, b, 2)
                T.matmul(psE[p][:, 0:NK], q1T[:, p, :], k1T[:, p, :], start=True, stop=True).then_inc(s_done, 1)

            def turn_p(h, p):
                b = 2 * h + p
                pe.wait_ge(p1_ready, b + 1)
                wait_free(pe, r_ready, b, 1)
                T.transpose(psB[0:NK, 0:P], p1[:, p, :], ident).then_inc(p1_turned, 1)

            def attend(h, p):
                b = 2 * h + p
                pe.wait_ge(p1T_ready, b + 1)
                T.matmul(psB[:, P:2 * P], p1T[0:NK, p, :], g.V1[0:NK, ds(b, 1), :].rearrange("p a d -> p (a d)"), start=True, stop=True).then_inc(av_done, 1)

            def turn_r(h, p):
                b = 2 * h + p
                pe.wait_ge(r_ready, b + 1)
                wait_free(pe, x3_ready, b, 1)
                T.transpose(psC[:, 0:P], r[:, p, :], ident).then_inc(r_turned, 1)

            def out_project(h, p):
                b = 2 * h + p
                pe.wait_ge(rT_ready, b + 1)
                T.matmul(psC[:, P:2 * P], rT[:, p, :], wo1, start=True, stop=True).then_inc(o1_done, 1)

            def turn_xn3(h, p):
                b = 2 * h + p
                pe.wait_ge(xn3_ready, b + 1)
                wait_free(pe, en_ready, b, 1)
                T.transpose(psD[:, P:2 * P], xn3[:, p, :], ident).then_inc(xn3_turned, 1)

            def affinities(h, p):
                b = 2 * h + p
                pe.wait_ge(xn3T_ready, b + 1)
                T.matmul(psD[:, 0:E1], xn3T[:, p, :], cent, start=True, stop=True).then_inc(aff_done, 1)

            def turn_parts(h, p):
                b = 2 * h + p
                pe.wait_ge(parts_ready, b + 1)
                wait_free(pe, cwT_ready, b, 1)
                T.transpose(psG16[:, 0:P], parts[:, p, :], g.ident16[:, :]).then_inc(parts_turned, 1)
            pipeline(pe, [(2, turn_xn2), (4, turn_r), (5, turn_xn3), (3, turn_p), (2, project), (4, out_project), (5, affinities), (3, attend),
                          (2, scores), (5, turn_parts)], NB, 8)


def experts1(nc, g):
    with ExitStack() as ctx:
        def sb(name, shape, dt=F32):
            return ctx.enter_context(nc.sbuf_tensor(name, shape, dt))

        def sem(name):
            return ctx.enter_context(nc.semaphore(name))

        N = LOTS * P
        w_up, w_down, ws_down, ws_up = sb("w_up1", [P, NFT * P]), sb("w_down1", [P, NFT * P]), sb("ws_down", [F1, P]), sb("ws_up", [P, F1])
        act_out, hid = sb("act_out", [P, 2, N]), sb("hid1", [P, 2, N])
        sumT, res = sb("sumT", [P, N]), sb("res", [P, N])
        weights_in = sem("weights1_in")
        up_done, silu_ready, hid_ready, down_done = sem("up_done"), sem("silu_ready"), sem("hid1_ready"), sem("down1_done")
        sum_ready, sum_turned, res_ready, stored = sem("sum_ready"), sem("sum_turned"), sem("res_ready"), sem("stored")
        block = ctx.enter_context(nc.Block())
        psW, psU, psO, psR = [g.bank[0], g.bank[1]], [g.bank[2], g.bank[3], g.bank[6]], g.bank[4], g.bank[5]
        NS = NFT + 1

        @block.sync
        def _(sp):
            for i in range(2):
                half = NFT * P // 2
                sp.dma_start(w_up[:, half * i:half * i + half], g.d_w_up1[:, half * i:half * i + half]).then_inc(weights_in, 16)
                sp.dma_start(w_down[:, half * i:half * i + half], g.d_w_down1[:, half * i:half * i + half]).then_inc(weights_in, 16)
            sp.dma_start(ws_down[:, :], g.d_ws_down).then_inc(weights_in, 16)
            sp.dma_start(ws_up[:, :], g.d_ws_up).then_inc(weights_in, 16)
            with sp.Fori(0, NG) as i:
                sp.wait_ge(res_ready, i + 1)
                sp.dma_start(g.d_out[ds(i * LOTS, LOTS), :, :].rearrange("b p d -> p b d"),
                             res[:, :].rearrange("p (b d) -> p b d", b=LOTS)).then_inc(stored, 16)
            sp.wait_ge(stored, 16 * NG)

        @block.tensor
        def _(pe):
            T = nc.tensor
            ident = g.consts[:, C_ID:C_ID + P]
            pe.wait_ge(weights_in, 96)

            def up(i, f):
                n = i * NS + f
                first_step = isinstance(i, int) and i == 0
                x = g.XT[:, ds(i * LOTS, LOTS), :].rearrange("p b t -> p (b t)")
                if f < NFT:
                    if not (first_step and f < 2):
                        pe.wait_ge(hid_ready, i * NFT + f - 1)
                    T.matmul(psW[f % 2][:, :], g.sel[:, P * f:P * f + P], g.CWT[:, ds(i * LOTS, LOTS), :].rearrange("p b t -> p (b t)"), start=True, stop=True)
                if not (first_step and f < 3):
                    wait_apart(g, pe, silu_ready, n - 2)
                if f < NFT:
                    T.matmul(psU[f % 3][:, :], w_up[:, P * f:P * f + P], x, start=True, stop=True).then_inc(up_done, 1)
                else:
                    T.matmul(psU[f % 3][0:F1, :], ws_up[:, :], x, start=True, stop=True).then_inc(up_done, 1)

            def down(i, f):
                if f == 0 and not (isinstance(i, int) and i == 0):
                    pe.wait_ge(sum_ready, i)
                if f < NFT:
                    pe.wait_ge(hid_ready, i * NFT + f + 1)
                    T.matmul(psO[:, :], w_down[:, P * f:P * f + P], hid[:, f % 2, :], start=f == 0, stop=False).then_inc(down_done, 1)
                else:
                    pe.wait_ge(silu_ready, i * NS + NS)
                    T.matmul(psO[:, :], ws_down[:, :], act_out[0:F1, f % 2, :], start=False, stop=True).then_inc(down_done, 1)

            def group(i):
                for f in range(NS + 2):
                    if f < NS:
                        up(i, f)
                    if f >= 2:
                        down(i, f - 2)
                pe.wait_ge(sum_ready, i + 1)
                if not (isinstance(i, int) and i == 0):
                    pe.wait_ge(res_ready, i)
                for b in range(LOTS):
                    last = T.transpose(psR[:, P * b:P * b + P], sumT[:, P * b:P * b + P], ident)
                last.then_inc(sum_turned, 1)
            group(0)
            with pe.Fori(1, NG) as i:
                group(i)

        @block.scalar
        def _(act):
            def group(i):
                for f in range(NS):
                    n = i * NS + f
                    act.wait_ge(up_done, n + 1)
                    if not (isinstance(i, int) and i == 0 and f < 2):
                        if f == NFT:
                            act.wait_ge(hid_ready, i * NFT + f - 1)
                        elif f >= 2:
                            act.wait_ge(hid_ready, i * NFT + f - 1)
                        elif f == 1:
                            act.wait_ge(hid_ready, i * NFT)
                        else:
                            act.wait_ge(down_done, i * NS)
                    rows = P if f < NFT else F1
                    nc.scalar.activation(act_out[0:rows, f % 2, :], psU[f % 3][0:rows, :], ACT.Silu).then_inc(silu_ready, 1)
                act.wait_ge(down_done, i * NS + NS)
                if not (isinstance(i, int) and i == 0):
                    act.wait_ge(sum_turned, i)
                nc.scalar.activation(sumT[:, :], psO[:, :], ACT.Copy).then_inc(sum_ready, 1)
            group(0)
            with act.Fori(1, NG) as i:
                group(i)

        @block.vector
        def _(dve):
            def group(i):
                for f in range(NFT):
                    dve.wait_ge(silu_ready, i * NS + f + 1)
                    if not (isinstance(i, int) and i == 0 and f < 2):
                        dve.wait_ge(down_done, i * NS + f - 1 if f >= 2 else i * NS - 2 + f)
                    nc.vector.tensor_tensor(hid[:, f % 2, :], psW[f % 2][:, :], act_out[:, f % 2, :], ALU.mult).then_inc(hid_ready, 1)
                dve.wait_ge(sum_turned, i + 1)
                if not (isinstance(i, int) and i == 0):
                    dve.wait_ge(stored, 16 * i)
                nc.vector.tensor_tensor(res[:, :], psR[:, :], g.X[:, ds(i * LOTS, LOTS), :].rearrange("p b d -> p (b d)"), ALU.add).then_inc(res_ready, 1)
            group(0)
            with dve.Fori(1, NG) as i:
                group(i)


def program(nc, d, out):
    g = Shared()
    (g.d_x, g.d_ctx, g.d_consts, g.d_sel, g.d_ident16, g.d_cols, g.d_rows, g.d_w_ctx, g.d_w_small, g.d_w_up0, g.d_w_down0,
     g.d_b_row0, g.d_b_down0, g.d_w_up1, g.d_w_down1, g.d_ws_up, g.d_ws_down) = d
    g.d_out = out
    g.xs = nc.dram_tensor("xs", (E0 * REGION + P, P), F32, kind="Internal").ap()
    g.ys = nc.dram_tensor("ys", (NT * P, P), F32, kind="Internal").ap()
    with ExitStack() as ctx:
        def sb(name, shape, dt=F32):
            return ctx.enter_context(nc.sbuf_tensor(name, shape, dt))

        g.apart = {eng: ctx.enter_context(nc.semaphore(f"apart_{i}")) for i, eng in enumerate((nc.gpsimd, nc.vector, nc.tensor))}
        g.X = sb("X", [P, NB, P])
        g.consts, g.cols, g.rows = sb("consts", [P, C_END]), sb("cols", [P, N_COL]), sb("rows", [P, R_END])
        g.w_small = sb("w_small", [P, 584])
        g.zeros, g.mhalf = sb("zeros", [P, P]), sb("mhalf", [P, 4])
        g.run = sb("run", [P, E0])
        g.gate, g.slotf, g.slots = sb("gate", [P, NB, 2]), sb("slot_in_xs", [P, NB, 2]), sb("slots", [P, NB, 2], I32)
        g.table = sb("table", [P, 2 * NT], I32)
        g.psum = ctx.enter_context(nc.psum_tensor("psum", [P, 8, 512], F32))
        g.bank = [g.psum[:, i, :] for i in range(8)]
        with ExitStack() as late:
            def sb2(name, shape, dt=F32):
                return late.enter_context(nc.sbuf_tensor(name, shape, dt))
            g.V1, g.ctxT = sb2("V1", [P, NB, P]), sb2("ctxT", [P, NB, NK])
            with ExitStack() as early:
                g.cstage, g.vaug, g.w_ctx = (early.enter_context(nc.sbuf_tensor(n, s, F32))
                                             for n, s in (("cstage", [P, 2, P]), ("vaug", [P, 2, H, HD + 1]), ("w_ctx", [P, 4 * P])))
                load(nc, g)
                attention0(nc, g)
            tables(nc, g)
            experts0(nc, g)
            g.XT = sb2("XT", [P, NB, P])
            g.CWT = sb2("CWT", [P, NB, P], F16)
            g.sel = sb2("sel", [P, NFT * P], F16)
            g.ident16 = sb2("ident16", [P, P], F16)
            with ExitStack() as ctx2:
                sel_in = ctx2.enter_context(nc.semaphore("sel_in"))
                block = ctx2.enter_context(nc.Block())

                @block.sync
                def _(sp):
                    sp.dma_start(g.sel[:, :], g.d_sel).then_inc(sel_in, 16)
                    sp.dma_start(g.ident16[:, :], g.d_ident16).then_inc(sel_in, 16)
                    sp.wait_ge(sel_in, 32)
            attention1(nc, g)
            experts1(nc, g)


def kernel(**inputs):
    import numpy as np
    import concourse.bacc as bacc
    from concourse.bass_utils import run_bass_kernel_spmd

    a = {k: np.asarray(v) for k, v in inputs.items()}
    c = np.zeros((P, C_END), np.float32)
    i, e = np.arange(P), np.arange(E0)
    c[:, C_ID:C_ID + P] = np.eye(P)
    c[:, C_TRI:C_TRI + P] = np.triu(np.ones((P, P)), 1)
    c[:, C_ONE:C_ONE + P] = 1
    c[:, C_MASK:C_MASK + HG] = (i[:, None] // HD) % HG == np.arange(HG)
    c[:, C_LT:C_LT + E0 * E0] = (e[None, :] < e[:, None]).reshape(-1)
    c[:, C_K:C_K + 2 * E0] = np.repeat([0, 1], E0)
    c[:, C_RUN:C_RUN + E0] = e * REGION
    c[:, C_P] = i
    c[:, C_J:C_J + NT] = np.arange(NT)
    sel = np.zeros((P, NFT * P), np.float16)
    spread = np.arange(E1)[:, None] == np.arange(NFT * P) // F1
    sel[:E1], sel[E1:] = spread, spread / 2048
    d = {
        "x": a["x"], "ctx": a["ctx_1024"], "consts": c, "sel": sel, "ident16": np.eye(P, dtype=np.float16),
        "cols": np.stack([a[n] for n in ("L0_xattn_gq", "L0_xattn_betq", "L0_xattn_gk", "L0_xattn_betk", "L0_xattn_gv", "L0_xattn_betv",
                                         "L1_xattn_bq", "L1_xattn_bk")], 1),
        "rows": np.concatenate([a[n] for n in ("L0_xattn_bq", "L0_xattn_bk", "L0_xattn_bv", "L1_xattn_bv", "L0_xattn_bo",
                                               "L1_ffn_expert_biases", "L1_xattn_bo")]),
        "w_ctx": np.concatenate([a["L0_xattn_Wq"], a["L0_xattn_Wk"], a["L0_xattn_Wv"], a["L1_xattn_Wv"].T], 1),
        "w_small": np.concatenate([a["L0_xattn_Wo"], a["L0_ffn_router_w"].T, a["L1_xattn_Wo"].T, a["L1_ffn_centroids"].T,
                                   a["L1_xattn_Wq"].T, a["L1_xattn_Wk"].T], 1),
        "w_up0": np.concatenate([a["L0_ffn_wg_w"], a["L0_ffn_w1_w"]], 1).transpose(2, 0, 1),
        "w_down0": a["L0_ffn_w2_w"].reshape(E0, P, FC, P).transpose(3, 0, 2, 1).reshape(P, E0, FC * P),
        "b_row0": np.concatenate([a["L0_ffn_wg_b"], a["L0_ffn_w1_b"]], 1).reshape(-1),
        "b_down0": a["L0_ffn_w2_b"].reshape(-1),
        "w_up1": a["L1_ffn_W_up"].transpose(1, 0, 2).reshape(P, E1 * F1),
        "w_down1": a["L1_ffn_W_down"].reshape(NFT, P, P).transpose(1, 0, 2).reshape(P, NFT * P),
        "ws_up": a["L1_ffn_Ws_up"], "ws_down": a["L1_ffn_Ws_down"],
    }
    nc = bacc.Bacc("TRN2", target_bir_lowering=False, num_devices=1)
    arrays, args = {}, []
    for name, v in d.items():
        v = np.ascontiguousarray(v)
        arrays["in_" + name] = v
        args.append(nc.dram_tensor("in_" + name, v.shape, mybir.dt.from_np(v.dtype), kind="ExternalInput").ap())
    out = nc.dram_tensor("out_x", (NB, P, P), F32, kind="ExternalOutput").ap()
    program(nc, args, out)
    r = run_bass_kernel_spmd(nc, [arrays], core_ids=[0])
    return r.results[0]["out_x"]
```

```python
import concourse.bass as bass
from concourse import mybir
from contextlib import ExitStack

F32 = mybir.dt.float32
F16 = mybir.dt.float16
I32 = mybir.dt.int32
ALU = mybir.AluOpType
ACT = mybir.ActivationFunctionType
AX = mybir.AxisListType.X
ds = bass.ds

P = 128
NB = 32
NK = 120
H = 16
HD = P // H
HG = 4
E0, F0 = 8, 512
FC = F0 // P
E1, F1 = 64, 64
NFT = E1 * F1 // P
EPS = 1e-5
SPLIT = 8.0
X_SCALE, W_SCALE, H_SCALE = 8.0, 64.0, 64.0
W_PART = 2 * NFT * P // NB
E_SCALE = 12 * 0.6931471805599453
REGION = NB * P + P
NT = 2 * NB + E0
ZERO_ROW = E0 * REGION
LOTS = 4
NG = NB // LOTS

C_ID, C_TRI, C_ONE, C_MASK, C_LT, C_K, C_RUN, C_P, C_J, C_END = 0, 128, 256, 384, 388, 452, 468, 476, 477, 477 + NT
GQ, BQN, GK, BKN, GV, BVN, BQ1, BK1, N_COL = 0, 1, 2, 3, 4, 5, 6, 7, 8
R_QKV, R_BO0, R_EB, R_BO1, R_AFF, R_END = 0, 512, 640, 704, 832, 1344


class Shared:
    pass


def bcast(ap, *shape):
    return ap.to_broadcast(list(shape))


class Steps:

    def __init__(self, eng, sem, per, b, done=0):
        self.eng, self.sem, self.first, self.done = eng, sem, b * per, done

    def __call__(self, instruction):
        instruction.then_inc(self.sem, 1)
        self.done += 1

    def wait(self):
        self.eng.wait_ge(self.sem, self.first + self.done)

    def wait_apart(self, g):
        wait_apart(g, self.eng, self.sem, self.first + self.done)


def wait_apart(g, eng, sem, value):
    eng.wait_ge(sem, value)
    if not isinstance(value, int):
        eng.sem_inc(g.apart[eng], 1)


def wait_free(eng, sem, b, back, per=1, apart=None):
    if isinstance(b, int) and b < back:
        return
    if apart is None:
        eng.wait_ge(sem, (b - back) * per + per)
    else:
        wait_apart(apart, eng, sem, (b - back) * per + per)


def pipeline(eng, pieces, n, lead):
    def step(half, parity):
        for lag, work in pieces:
            h, p = half + (parity - lag) // 2, (parity - lag) % 2
            if isinstance(half, int) and not 0 <= 2 * h + p < n:
                continue
            work(h, p)
    for t in range(lead):
        step(t // 2, t % 2)
    with eng.Fori(lead // 2, n // 2) as half:
        for parity in range(2):
            step(half, parity)
    for t in range(n, n + max(lag for lag, _ in pieces)):
        step(t // 2, t % 2)


def load(nc, g):
    with ExitStack() as ctx:
        zeroed = ctx.enter_context(nc.semaphore("zeroed"))
        loaded = ctx.enter_context(nc.semaphore("loaded"))
        consts_in, rows_in = ctx.enter_context(nc.semaphore("consts_in")), ctx.enter_context(nc.semaphore("rows_in"))
        block = ctx.enter_context(nc.Block())

        @block.gpsimd
        def _(pool):
            nc.gpsimd.memset(g.zeros[:, :], 0.0).then_inc(zeroed, 1)
            nc.gpsimd.memset(g.cstage[:, :, :], 0.0).then_inc(zeroed, 1)
            nc.gpsimd.memset(g.vaug[:, :, :, :, :], 0.0).then_inc(zeroed, 1)
            nc.gpsimd.memset(g.mhalf[:, :], -0.5).then_inc(zeroed, 1)
            nc.gpsimd.memset(g.split[:, :, :, :, :, :], 0.0).then_inc(zeroed, 1)
            pool.wait_ge(zeroed, 5)
            for p in range(2):
                nc.gpsimd.memset(g.split[:, p, 1, :, 3, 0], SPLIT ** 2).then_inc(zeroed, 1)
                nc.gpsimd.memset(g.vaug[:, p, :, 0, HD], SPLIT).then_inc(zeroed, 1)
            pool.wait_ge(zeroed, 9)

        @block.sync
        def _(sp):
            n = 0
            sp.dma_start(g.consts[:, :], g.d_consts).then_inc(consts_in, 16)
            sp.dma_start(g.rows[:, :], g.d_rows.partition_broadcast(P)).then_inc(rows_in, 16)
            for to, of in ((g.cols[:, :], g.d_cols), (g.w_ctx[:, :], g.d_w_ctx), (g.ident16[:, :], g.d_ident16), (g.w_small[:, :], g.d_w_small)):
                sp.dma_start(to, of).then_inc(loaded, 16)
                n += 16
            for i in range(4):
                sp.dma_start(g.X[:, 8 * i:8 * i + 8, :], g.d_x[8 * i:8 * i + 8].rearrange("b p d -> p b d")).then_inc(loaded, 16)
                n += 16
            sp.wait_ge(zeroed, 1)
            sp.dma_start(g.xs[ZERO_ROW:ZERO_ROW + P, :], g.zeros[:, :]).then_inc(loaded, 16)
            sp.wait_ge(loaded, n + 16)
            sp.wait_ge(consts_in, 16)

        @block.scalar
        def _(act):
            act.wait_ge(loaded, 16 * 9)
            act.dma_start(g.w_up0[:, 0:4, :], g.d_w_up0[:, 0:4, :]).then_inc(g.weights0_in, 16)
            act.dma_start(g.w_up0[:, 4:8, :], g.d_w_up0[:, 4:8, :]).then_inc(g.weights0_in, 16)
            act.dma_start(g.w_down0[:, :, :], g.d_w_down0).then_inc(g.weights0_in, 16)
            act.dma_start(g.b_down0[:, :, :].rearrange("p e f -> p (e f)"), g.d_b_down0.partition_broadcast(P)).then_inc(g.biases0_in, 16)

        @block.vector
        def _(dve):
            dve.wait_ge(consts_in, 16)
            nc.vector.tensor_copy(g.run[:, :], g.consts[:, C_RUN:C_RUN + E0])
            dve.wait_ge(rows_in, 16)
            nc.vector.tensor_scalar(g.affine[:, :], g.rows[:, R_AFF:R_AFF + 4 * P], SPLIT, None, ALU.mult)


def attention0(nc, g):
    with ExitStack() as ctx:
        def sb(name, shape, dt=F32):
            return ctx.enter_context(nc.sbuf_tensor(name, shape, dt))

        def sem(name):
            return ctx.enter_context(nc.semaphore(name))

        st6, mv, ve, rstd = sb("st6", [P, 2, 6]), sb("mv", [P, 2, 2]), sb("ve", [P, 2, 1]), sb("rstd", [P, 2, 1])
        xn, xcT = sb("xn", [P, 2, P]), sb("xcT", [P, 2, 2 * P])
        qkv = sb("qkv", [P, 2, 4 * P])
        st18, mv3, ve3, rstd3, nmr3 = (sb("st18", [P, 2, 3, 6]), sb("mv3", [P, 2, 3, 2]), sb("ve3", [P, 2, 3]), sb("rstd3", [P, 2, 3]),
                                       sb("nmr3", [P, 2, 3]))
        qkn = sb("qkn", [P, 2, 2 * P])
        qT, q2T, kT = sb("qT", [P, 2, H * 4 * HD], F16), sb("q2T", [P, 2, H * 4 * HD], F16), sb("kT", [P, 2, H * 4 * HD], F16)
        mx, vn = sb("mx", [P, 2, H]), sb("vn", [P, 2, P])
        e32 = sb("e32", [P, 2, HG * P])
        e_hi, e_lo = sb("e_hi", [P, 2, H * P], F16), sb("e_lo", [P, 2, H * P], F16)
        o_sum, e_scale = sb("o_sum", [P, 2, P]), sb("e_scale", [P, 1])
        rs, o, oT = sb("rs", [P, 2, H]), sb("o", [P, 2, P]), sb("oT", [P, 2, P])
        st1, mv1, ve1, rstd1 = sb("st1", [P, 2, 6]), sb("mv1", [P, 2, 2]), sb("ve1", [P, 2, 1]), sb("rstd1", [P, 2, 1])
        xn1, xn1T, sent = sb("xn1", [P, 2, P]), sb("xn1T", [P, 2, P]), sb("sent", [P, 2, P])
        lmax, lg, ex, esum, erec, pr = (sb("lmax", [P, 2, 1]), sb("lg", [P, 2, E0]), sb("ex", [P, 2, E0]), sb("esum", [P, 2, 1]),
                                        sb("erec", [P, 2, 1]), sb("pr", [P, 2, E0]))
        gt, eq, rank = sb("gt", [P, 2, E0 * E0]), sb("eq", [P, 2, E0 * E0]), sb("rank", [P, 2, E0])
        chosen, picked = sb("chosen", [P, 2, 2 * E0]), sb("picked", [P, 2, E0])
        place, tmp, slotf, slot = (sb("place", [P, 2, E0]), sb("tmp", [P, 2, 2 * E0]), sb("slotf", [P, 2, 2]), sb("slot", [P, 2, 2], I32))
        tmp2 = sb("tmp2", [P, 2, 2 * E0])

        psA, psB, psR, psQ = g.bank[0], g.bank[1], g.bank[7], g.bank[6].bitcast(F16)
        psS, psT = [g.bank[2], g.bank[3]], [g.bank[4], g.bank[5]]

        ctx_in = [sem("ctx_in_even"), sem("ctx_in_odd")]
        scattered = [sem("scattered_even"), sem("scattered_odd")]
        x_stats, x_var, x_rstd, xn_ready = sem("x_stats"), sem("x_var"), sem("x_rstd"), sem("xn_ready")
        xc_turned, xcT_ready, projected = sem("xc_turned"), sem("xcT_ready"), sem("projected")
        qkv_ready, qkv_stats, qkv_var, qkv_rstd, nmr_ready = sem("qkv_ready"), sem("qkv_stats"), sem("qkv_var"), sem("qkv_rstd"), sem("nmr_ready")
        qk_normed, affine_steps, hi_ready, split_ready = sem("qk_normed"), sem("affine_steps"), sem("hi_ready"), sem("split_ready")
        vn_ready, v1_kept, qk_turned, qkT_ready = sem("vn_ready"), sem("v1_kept"), sem("qk_turned"), sem("qkT_ready")
        scores_ready, max_ready, shift_ready, q2_turned, q2T_ready = (sem("scores_ready"), sem("max_ready"), sem("shift_ready"),
                                                                      sem("q2_turned"), sem("q2T_ready"))
        shifted_ready, exp_ready, low_ready, pv_ready = (sem("shifted_ready"), sem("exp_ready"), [sem("low_even_ready"), sem("low_odd_ready")],
                                                         sem("pv_ready"))
        v_normed, o_summed, scale_set = sem("v_normed"), sem("o_summed"), sem("scale_set")
        vs, vs_ready = sb("vs", [P, 2, 2]), sem("vs_ready")
        rs_ready, o_ready, o_turned, oT_ready, y_ready = sem("rs_ready"), sem("o_ready"), sem("o_turned"), sem("oT_ready"), sem("y_ready")
        bo_added, x1_ready, x1_stats, x1_var, x1_rstd = sem("bo_added"), sem("x1_ready"), sem("x1_stats"), sem("x1_var"), sem("x1_rstd")
        xn1_ready, xn1_turned, xn1T_ready, logits_ready = sem("xn1_ready"), sem("xn1_turned"), sem("xn1T_ready"), sem("logits_ready")
        sent_ready = sem("sent_ready")
        shift_steps, lg_exp, rank_steps = sem("shift_steps"), sem("lg_exp"), sem("rank_steps")
        counted, place_steps, routed = sem("counted"), sem("place_steps"), sem("routed")

        block = ctx.enter_context(nc.Block())

        @block.sync
        def _(sp):
            def load_ctx(h, p):
                wait_free(sp, xc_turned, 2 * h + p, 2)
                sp.dma_start(g.cstage[0:NK, p, :], g.d_ctx[ds(2 * h + p, 1), :, :].rearrange("b k d -> (b k) d")).then_inc(ctx_in[p], 16)
            pipeline(sp, [(0, load_ctx)], NB, 2)

        @block.gpsimd
        def _(pool):
            def rstd_of(var, var_eps, out, n, b, steps, sem_ready):
                st = Steps(pool, steps, 1, b)
                st(nc.gpsimd.tensor_scalar(var_eps, var, EPS, None, ALU.add))
                st.wait()
                nc.gpsimd.tensor_tensor(out, var_eps, g.mhalf[:, 0:n], ALU.pow).then_inc(sem_ready, 1)

            def x_scale(h, p):
                b = 2 * h + p
                wait_apart(g, pool, x_stats, 2 * b + 2)
                wait_free(pool, xn_ready, b, 2, apart=g)
                rstd_of(mv[:, p, 1:2], ve[:, p, :], rstd[:, p, :], 1, b, x_var, x_rstd)

            def low_exp(j):
                def work(h, p):
                    b = 2 * h + p
                    pool.wait_ge(exp_ready, 4 * b + j + 1)
                    part = slice(j * HG * P, (j + 1) * HG * P)
                    nc.gpsimd.tensor_tensor(e_lo[0:NK, p, part], e32[0:NK, 1, :], e_hi[0:NK, p, part], ALU.subtract).then_inc(low_ready[1], 1)
                return work

            def qkv_scale(h, p):
                b = 2 * h + p
                wait_apart(g, pool, qkv_stats, 6 * b + 6)
                wait_free(pool, qk_normed, b, 2, apart=g)
                wait_free(pool, v_normed, b, 2, apart=g)
                wait_free(pool, nmr_ready, b, 2, apart=g)
                rstd_of(mv3[:, p, :, 1:2].rearrange("p a c -> p (a c)"), ve3[:, p, :], rstd3[:, p, :], 3, b, qkv_var, qkv_rstd)

            def qk_affine(h, p):
                b = 2 * h + p
                pool.wait_ge(qk_normed, b + 1)
                st = Steps(pool, affine_steps, 2, b)
                st(nc.gpsimd.tensor_tensor(qkn[:, p, :], qkn[:, p, :], g.affine[:, 0:2 * P], ALU.mult))
                st.wait()
                st(nc.gpsimd.tensor_tensor(qkn[:, p, :], qkn[:, p, :], g.affine[:, 2 * P:4 * P], ALU.add))

            def add_bo(h, p):
                b = 2 * h + p
                pool.wait_ge(xn_ready, b + 1)
                xb = g.X[:, ds(b, 1), :].rearrange("p a d -> p (a d)")
                nc.gpsimd.tensor_tensor(xb, xb, g.rows[:, R_BO0:R_BO0 + P], ALU.add).then_inc(bo_added, 1)

            def x1_scale(h, p):
                b = 2 * h + p
                wait_apart(g, pool, x1_stats, 2 * b + 2)
                wait_free(pool, xn1_ready, b, 2, apart=g)
                rstd_of(mv1[:, p, 1:2], ve1[:, p, :], rstd1[:, p, :], 1, b, x1_var, x1_rstd)

            def scatter(h, p):
                b = 2 * h + p
                wait_apart(g, pool, sent_ready, b + 1)
                wait_apart(g, pool, routed, b + 1)
                for c in range(2):
                    nc.gpsimd.indirect_dma_start(g.xs[:, :], bass.IndirectOffsetOnAxis(slot[:, p, c:c + 1], 0),
                                                 sent[:, p, :], None).then_inc(scattered[p], 16)

            pipeline(pool, [(2, qkv_scale), (0, x_scale), (4, low_exp(1)), (2, qk_affine), (4, low_exp(3)), (5, x1_scale), (8, scatter), (4, add_bo)], NB, 10)
            for p in range(2):
                pool.wait_ge(scattered[p], 32 * (NB // 2))

        @block.vector
        def _(dve):
            V = nc.vector
            V.memset(e_scale[:, :], E_SCALE).then_inc(scale_set, 1)

            def x_statistics(h, p):
                b = 2 * h + p
                wait_free(dve, xn_ready, b, 2, apart=g)
                wait_free(dve, x_rstd, b, 2, apart=g)
                st = Steps(dve, x_stats, 2, b)
                st(V.bn_stats(st6[:, p, :], g.X[:, ds(b, 1), :].rearrange("p a d -> p (a d)")))
                st.wait_apart(g)
                st(V.bn_aggr(mv[:, p, :], st6[:, p, :]))

            def x_norm(h, p):
                b = 2 * h + p
                dve.wait_ge(x_rstd, b + 1)
                wait_free(dve, xc_turned, b, 2)
                V.tensor_scalar(xn[:, p, :], g.X[:, ds(b, 1), :].rearrange("p a d -> p (a d)"), mv[:, p, 0:1], rstd[:, p, :],
                                ALU.subtract, ALU.mult).then_inc(xn_ready, 1)

            def qkv_bias(h, p):
                b = 2 * h + p
                dve.wait_ge(projected, b + 1)
                wait_free(dve, qk_normed, b, 2)
                wait_free(dve, v_normed, b, 2)
                wait_free(dve, v1_kept, b, 2)
                V.tensor_tensor(qkv[:, p, :], psA[:, 0:4 * P], g.rows[:, R_QKV:R_QKV + 4 * P], ALU.add).then_inc(qkv_ready, 1)

            def qkv_statistics(h, p):
                b = 2 * h + p
                wait_free(dve, qkv_rstd, b, 2, apart=g)
                wait_apart(g, dve, qkv_ready, b + 1)
                st = Steps(dve, qkv_stats, 6, b)
                for i in range(3):
                    st(V.bn_stats(st18[:, p, i, :], qkv[:, p, P * i:P * i + P]))

            def qkv_variances(h, p):
                b = 2 * h + p
                st = Steps(dve, qkv_stats, 6, b, 3)
                st.wait_apart(g)
                for i in range(3):
                    st(V.bn_aggr(mv3[:, p, i, :], st18[:, p, i, :]))

            def qkv_offset(h, p):
                b = 2 * h + p
                dve.wait_ge(qkv_rstd, b + 1)
                dve.wait_ge(qkv_stats, 6 * b + 6)
                wait_free(dve, v_normed, b, 2)
                wait_free(dve, qk_normed, b, 2)
                V.scalar_tensor_tensor(nmr3[:, p, :], mv3[:, p, :, 0:1].rearrange("p a c -> p (a c)"), -1.0, rstd3[:, p, :],
                                       ALU.mult, ALU.mult).then_inc(nmr_ready, 1)

            def v_scale(h, p):
                b = 2 * h + p
                V.tensor_scalar(vs[:, p, 0:1], rstd3[:, p, 2:3], SPLIT, None, ALU.mult)
                dve.wait_ge(nmr_ready, b + 1)
                V.tensor_scalar(vs[:, p, 1:2], nmr3[:, p, 2:3], SPLIT, None, ALU.mult).then_inc(vs_ready, 1)

            def v_low(h, p):
                b = 2 * h + p
                dve.wait_ge(v_normed, b + 1)
                V.tensor_tensor(g.vaug[:, p, :, 1, 0:HD], vn[:, p, :].rearrange("p (h d) -> p h d", h=H), g.vaug[:, p, :, 0, 0:HD],
                                ALU.subtract).then_inc(vn_ready, 1)

            def low_exp(j):
                def work(h, p):
                    b = 2 * h + p
                    dve.wait_ge(exp_ready, 4 * b + j + 1)
                    part = slice(j * HG * P, (j + 1) * HG * P)
                    V.tensor_tensor(e_lo[0:NK, p, part], e32[0:NK, 0, :], e_hi[0:NK, p, part], ALU.subtract).then_inc(low_ready[0], 1)
                return work

            def low_parts(h, p):
                b = 2 * h + p
                dve.wait_ge(hi_ready, b + 1)
                for i, part in ((0, 2), (1, 1)):
                    last = V.tensor_tensor(g.split[:, p, i, :, part, :], qkn[:, p, P * i:P * i + P].rearrange("p (h d) -> p h d", h=H),
                                           g.split[:, p, i, :, 0, :], ALU.subtract)
                last.then_inc(split_ready, 1)

            def maximum(j):
                def work(h, p):
                    b = 2 * h + p
                    dve.wait_ge(scores_ready, 4 * b + j + 1)
                    V.tensor_reduce(mx[:, p, :].rearrange("p (g j) -> p g j", j=HG)[:, :, j],
                                    psS[j % 2][:, 0:HG * NK].rearrange("p (g k) -> p g k", g=HG), AX, ALU.max).then_inc(max_ready, 1)
                return work

            def shift(h, p):
                b = 2 * h + p
                dve.wait_ge(max_ready, 4 * b + 4)
                V.tensor_scalar(g.split[:, p, 0, :, 3, 0], mx[:, p, :], -1.0 / SPLIT ** 2, None, ALU.mult).then_inc(shift_ready, 1)

            def out_sums(h, p):
                b = 2 * h + p
                dve.wait_ge(pv_ready, b + 1)
                av = psB[:, 0:2 * H * (HD + 1)].rearrange("p (h c i) -> p h c i", h=H, c=2)
                V.reciprocal(rs[:, p, :], av[:, :, 0, HD]).then_inc(rs_ready, 1)
                V.tensor_copy(o_sum[:, p, :].rearrange("p (h i) -> p h i", h=H), av[:, :, 1, 0:HD]).then_inc(o_summed, 1)

            def out_add(h, p):
                b = 2 * h + p
                av = psB[:, 0:2 * H * (HD + 1)].rearrange("p (h c i) -> p h c i", h=H, c=2)
                ov = o_sum[:, p, :].rearrange("p (h i) -> p h i", h=H)
                dve.wait_ge(o_summed, 2 * b + 1)
                V.tensor_tensor(ov, av[:, :, 0, 0:HD], ov, ALU.add).then_inc(o_summed, 1)

            def out_scale(h, p):
                b = 2 * h + p
                dve.wait_ge(rs_ready, b + 1)
                dve.wait_ge(o_summed, 2 * b + 2)
                wait_free(dve, o_turned, b, 2)
                V.tensor_tensor(o[:, p, :].rearrange("p (h i) -> p h i", h=H), o_sum[:, p, :].rearrange("p (h i) -> p h i", h=H),
                                bcast(rs[:, p, :].unsqueeze(2), P, H, HD), ALU.mult).then_inc(o_ready, 1)

            def residual(h, p):
                b = 2 * h + p
                dve.wait_ge(y_ready, b + 1)
                dve.wait_ge(bo_added, b + 1)
                xb = g.X[:, ds(b, 1), :].rearrange("p a d -> p (a d)")
                V.tensor_tensor(xb, psB[:, 3 * P:4 * P], xb, ALU.add).then_inc(x1_ready, 1)

            def x1_statistics(h, p):
                b = 2 * h + p
                wait_apart(g, dve, x1_ready, b + 1)
                st = Steps(dve, x1_stats, 2, b)
                st(V.bn_stats(st1[:, p, :], g.X[:, ds(b, 1), :].rearrange("p a d -> p (a d)")))

            def x1_variance(h, p):
                b = 2 * h + p
                wait_free(dve, x1_rstd, b, 2, apart=g)
                st = Steps(dve, x1_stats, 2, b, 1)
                st.wait_apart(g)
                st(V.bn_aggr(mv1[:, p, :], st1[:, p, :]))

            def x1_norm(h, p):
                b = 2 * h + p
                dve.wait_ge(x1_rstd, b + 1)
                wait_free(dve, sent_ready, b, 2)
                wait_free(dve, xn1_turned, b, 2)
                V.tensor_scalar(xn1[:, p, :], g.X[:, ds(b, 1), :].rearrange("p a d -> p (a d)"), mv1[:, p, 0:1], rstd1[:, p, :],
                                ALU.subtract, ALU.mult).then_inc(xn1_ready, 1)

            def logits_max(h, p):
                b = 2 * h + p
                dve.wait_ge(logits_ready, b + 1)
                st = Steps(dve, shift_steps, 2, b)
                st(V.tensor_reduce(lmax[:, p, :], psR[:, 0:E0], AX, ALU.max))

            def logits_shift(h, p):
                b = 2 * h + p
                st = Steps(dve, shift_steps, 2, b, 1)
                st.wait()
                st(V.tensor_scalar(lg[:, p, :], psR[:, 0:E0], lmax[:, p, :], None, ALU.subtract))

            def choose(part):
                def work(h, p):
                    b = 2 * h + p
                    st = Steps(dve, rank_steps, 9, b, (0, 1, 2, 4, 5, 6, 7)[part])
                    if part == 0:
                        dve.wait_ge(lg_exp, b + 1)
                    else:
                        st.wait()
                    gtv, eqv = (x[:, p, :].rearrange("p (e f) -> p e f", e=E0) for x in (gt, eq))
                    if part == 0:
                        st(V.reciprocal(erec[:, p, :], esum[:, p, :]))
                    elif part == 1:
                        st(V.tensor_scalar(pr[:, p, :], ex[:, p, :], erec[:, p, :], None, ALU.mult))
                    elif part == 2:
                        other, own = bcast(pr[:, p, :].unsqueeze(1), P, E0, E0), bcast(pr[:, p, :].unsqueeze(2), P, E0, E0)
                        st(V.tensor_tensor(gtv, other, own, ALU.is_gt))
                        st(V.tensor_tensor(eqv, other, own, ALU.is_equal))
                    elif part == 3:
                        st(V.tensor_tensor(eq[:, p, :], eq[:, p, :], g.consts[:, C_LT:C_LT + E0 * E0], ALU.mult))
                    elif part == 4:
                        st(V.tensor_tensor(gt[:, p, :], gt[:, p, :], eq[:, p, :], ALU.add))
                    elif part == 5:
                        st(V.tensor_reduce(rank[:, p, :], gtv, AX, ALU.add))
                    else:
                        st(V.tensor_tensor(chosen[:, p, :].rearrange("p (c e) -> p c e", c=2), bcast(rank[:, p, :].unsqueeze(1), P, 2, E0),
                                           g.consts[:, C_K:C_K + 2 * E0].rearrange("p (c e) -> p c e", c=2), ALU.is_equal))
                        wait_free(dve, counted, b, 2)
                        st(V.tensor_scalar(picked[:, p, :], rank[:, p, :], 1.5, None, ALU.is_lt))
                return work

            def give_slots(part):
                def work(h, p):
                    b = 2 * h + p
                    st = Steps(dve, place_steps, 6, b, (0, 1, 4, 6)[part])
                    ch = chosen[:, p, :].rearrange("p (c e) -> p c e", c=2)
                    if part == 0:
                        dve.wait_ge(counted, b + 1)
                        dve.wait_ge(rank_steps, 9 * b + 9)
                        st(V.tensor_tensor(place[:, p, :], psR[:, 8:8 + E0], g.run[:, :], ALU.add))
                        return
                    st.wait()
                    if part == 1:
                        st(V.tensor_tensor(g.run[:, :], psR[:, 16:16 + E0], g.run[:, :], ALU.add))
                        st(V.tensor_tensor(tmp[:, p, :].rearrange("p (c e) -> p c e", c=2), ch, bcast(place[:, p, :].unsqueeze(1), P, 2, E0), ALU.mult))
                        st(V.tensor_tensor(tmp2[:, p, :].rearrange("p (c e) -> p c e", c=2), ch, bcast(pr[:, p, :].unsqueeze(1), P, 2, E0), ALU.mult))
                    elif part == 2:
                        st(V.tensor_reduce(slotf[:, p, :], tmp[:, p, :].rearrange("p (c e) -> p c e", c=2), AX, ALU.add))
                        st(V.tensor_reduce(g.gate[:, ds(b, 1), :].rearrange("p a c -> p (a c)"), tmp2[:, p, :].rearrange("p (c e) -> p c e", c=2), AX, ALU.add))
                    else:
                        if not (isinstance(b, int) and b < 2):
                            dve.wait_ge(scattered[p], 32 * h)
                        V.tensor_copy(g.slotf[:, ds(b, 1), :].rearrange("p a c -> p (a c)"), slotf[:, p, :])
                        V.tensor_copy(slot[:, p, :], slotf[:, p, :]).then_inc(routed, 1)
                return work

            pipeline(dve, [(0, x_statistics), (8, give_slots(0)), (7, choose(0)), (5, out_add), (8, give_slots(1)), (5, out_scale), (7, choose(1)),
                           (8, give_slots(2)), (7, choose(2)), (7, choose(3)), (3, maximum(0)), (2, qkv_offset), (3, maximum(1)),
                           (4, low_exp(0)), (7, choose(4)), (8, give_slots(3)), (3, maximum(2)), (7, choose(5)), (5, residual),
                           (3, maximum(3)), (3, shift), (7, choose(6)), (6, logits_max), (5, x1_statistics), (6, logits_shift),
                           (0, x_norm), (4, low_exp(2)), (2, v_scale), (5, x1_variance), (2, low_parts), (1, qkv_bias),
                           (1, qkv_statistics), (3, v_low), (4, out_sums), (5, x1_norm), (1, qkv_variances)], NB, 10)

        @block.scalar
        def _(act):
            A = nc.scalar
            act.wait_ge(scale_set, 1)

            def xc_copy(h, p):
                b = 2 * h + p
                act.wait_ge(xc_turned, b + 1)
                wait_free(act, projected, b, 2)
                A.activation(xcT[:, p, :], psA[:, 0:2 * P], ACT.Copy)
                A.activation(g.ctxT[:, ds(b, 1), :].rearrange("p a k -> p (a k)"), psA[:, P:P + NK], ACT.Copy).then_inc(xcT_ready, 1)

            def qk_norm(h, p):
                b = 2 * h + p
                act.wait_ge(nmr_ready, b + 1)
                wait_free(act, split_ready, b, 2)
                for i in range(2):
                    last = A.activation(qkn[:, p, P * i:P * i + P], qkv[:, p, P * i:P * i + P], ACT.Identity,
                                        bias=nmr3[:, p, i:i + 1], scale=rstd3[:, p, i:i + 1])
                last.then_inc(qk_normed, 1)

            def v_norm(h, p):
                b = 2 * h + p
                act.wait_ge(vs_ready, b + 1)
                wait_free(act, pv_ready, b, 2)
                wait_free(act, vn_ready, b, 2)
                A.activation(vn[:, p, :], qkv[:, p, 2 * P:3 * P], ACT.Identity, bias=vs[:, p, 1:2], scale=vs[:, p, 0:1])
                A.activation(g.vaug[:, p, :, 0, 0:HD], qkv[:, p, 2 * P:3 * P].rearrange("p (h i) -> p h i", h=H), ACT.Identity,
                             bias=vs[:, p, 1:2], scale=vs[:, p, 0:1]).then_inc(v_normed, 1)
                A.activation(g.V1[:, ds(b, 1), :].rearrange("p a k -> p (a k)"), qkv[:, p, 3 * P:4 * P], ACT.Copy).then_inc(v1_kept, 1)

            def high_parts(h, p):
                b = 2 * h + p
                act.wait_ge(affine_steps, 2 * b + 2)
                wait_free(act, q2_turned, b, 2)
                for i, step in ((0, 1), (1, 2)):
                    last = A.activation(g.split[:, p, i, :, 0:step + 1:step, :],
                                        bcast(qkn[:, p, P * i:P * i + P].rearrange("p (h d) -> p h d", h=H).unsqueeze(2), P, H, 2, HD), ACT.Copy)
                last.then_inc(hi_ready, 1)

            def qk_copy(h, p):
                b = 2 * h + p
                act.wait_ge(qk_turned, b + 1)
                wait_free(act, scores_ready, b, 2, 4)
                wait_free(act, shifted_ready, b, 2, 4)
                A.activation(qT[:, p, :], psQ[:, 0:4 * P], ACT.Copy)
                A.activation(kT[:, p, :], psQ[:, 4 * P:8 * P], ACT.Copy).then_inc(qkT_ready, 1)

            def q2_copy(h, p):
                b = 2 * h + p
                act.wait_ge(q2_turned, b + 1)
                wait_free(act, shifted_ready, b, 2, 4)
                A.activation(q2T[:, p, :], psQ[:, 0:4 * P], ACT.Copy).then_inc(q2T_ready, 1)

            def exponential(j):
                def work(h, p):
                    b = 2 * h + p
                    act.wait_ge(shifted_ready, 4 * b + j + 1)
                    wait_free(act, pv_ready, b, 2)
                    if not (isinstance(b, int) and b == 0 and j < 2):
                        act.wait_ge(low_ready[j % 2], 2 * b + j // 2)
                    for to in e32[0:NK, j % 2, :], e_hi[0:NK, p, HG * P * j:HG * P * (j + 1)]:
                        last = A.activation(to, psT[j % 2][0:NK, :], ACT.Exp, bias=e_scale[0:NK, :], scale=float(HD) ** -0.5 / SPLIT ** 2)
                    last.then_inc(exp_ready, 1)
                return work

            def o_affine(h, p):
                b = 2 * h + p
                act.wait_ge(o_turned, b + 1)
                wait_free(act, y_ready, b, 2)
                A.activation(oT[:, p, :], psB[:, 3 * P:4 * P], ACT.Identity, bias=g.cols[:, BVN:BVN + 1], scale=g.cols[:, GV:GV + 1]).then_inc(oT_ready, 1)

            def xn1_copy(h, p):
                b = 2 * h + p
                act.wait_ge(xn1_turned, b + 1)
                wait_free(act, logits_ready, b, 2)
                A.activation(xn1T[:, p, :], psR[:, P:2 * P], ACT.Copy).then_inc(xn1T_ready, 1)

            def send(h, p):
                b = 2 * h + p
                act.wait_ge(xn1_ready, b + 1)
                if not (isinstance(b, int) and b < 2):
                    act.wait_ge(scattered[p], 32 * h)
                A.activation(sent[:, p, :], xn1[:, p, :], ACT.Copy).then_inc(sent_ready, 1)

            def logits_exp(h, p):
                b = 2 * h + p
                act.wait_ge(shift_steps, 2 * b + 2)
                wait_free(act, rank_steps, b, 2, 9)
                A.activation(ex[:, p, :], lg[:, p, :], ACT.Exp, accum_out=esum[:, p, :]).then_inc(lg_exp, 1)

            pipeline(act, [(3, qk_copy), (4, exponential(0)), (4, exponential(1)), (1, xc_copy), (5, o_affine), (2, qk_norm), (6, xn1_copy),
                           (4, exponential(2)), (4, exponential(3)), (2, high_parts), (3, v_norm), (3, q2_copy), (7, send), (6, logits_exp)], NB, 10)

        @block.tensor
        def _(pe):
            T = nc.tensor
            ident = g.consts[:, C_ID:C_ID + P]

            def turn_xc(h, p):
                b = 2 * h + p
                wait_free(pe, qkv_ready, b, 1)
                pe.wait_ge(xn_ready, b + 1)
                pe.wait_ge(ctx_in[p], 16 * h + 16)
                T.transpose(psA[:, 0:P], xn[:, p, :], ident)
                T.transpose(psA[:, P:2 * P], g.cstage[:, p, :], ident).then_inc(xc_turned, 1)

            def project(h, p):
                b = 2 * h + p
                pe.wait_ge(xcT_ready, b + 1)
                T.matmul(psA[:, 0:P], xcT[:, p, 0:P], g.w_ctx[:, 0:P], start=True, stop=True)
                T.matmul(psA[:, P:4 * P], xcT[:, p, P:2 * P], g.w_ctx[:, P:4 * P], start=True, stop=True).then_inc(projected, 1)

            def turn_qk(h, p):
                b = 2 * h + p
                pe.wait_ge(split_ready, b + 1)
                wait_free(pe, q2T_ready, b, 1)
                for i in range(2):
                    for k in range(HG):
                        last = T.transpose(psQ[:, 4 * P * i + P * k:4 * P * i + P * k + P],
                                           g.split[:, p, i, HG * k:HG * k + HG, :, :].rearrange("p h c d -> p (h c d)"), g.ident16[:, :])
                last.then_inc(qk_turned, 1)

            def turn_q2(h, p):
                b = 2 * h + p
                pe.wait_ge(shift_ready, b + 1)
                pe.wait_ge(qkT_ready, b + 1)
                for k in range(HG):
                    last = T.transpose(psQ[:, P * k:P * k + P],
                                       g.split[:, p, 0, HG * k:HG * k + HG, :, :].rearrange("p h c d -> p (h c d)"), g.ident16[:, :])
                last.then_inc(q2_turned, 1)

            def scores(j):
                def work(h, p):
                    b = 2 * h + p
                    pe.wait_ge(qkT_ready, b + 1)
                    if not (isinstance(b, int) and b == 0 and j < 2):
                        pe.wait_ge(max_ready, 4 * b + j - 1)
                    rows = slice(32 * j, 32 * j + 3 * HD)
                    for k in range(HG):
                        last = T.matmul(psS[j % 2][:, NK * k:NK * k + NK], qT[rows, p, P * k:P * k + P], kT[rows, p, P * k:P * k + NK],
                                        start=True, stop=True)
                    last.then_inc(scores_ready, 1)
                return work

            def shifted(j):
                def work(h, p):
                    b = 2 * h + p
                    pe.wait_ge(q2T_ready, b + 1)
                    if not (isinstance(b, int) and b == 0 and j < 2):
                        pe.wait_ge(exp_ready, 4 * b + j - 1)
                    rows = slice(32 * j, 32 * j + 4 * HD)
                    for k in range(HG):
                        last = T.matmul(psT[j % 2][0:NK, P * k:P * k + P], kT[rows, p, P * k:P * k + NK], q2T[rows, p, P * k:P * k + P],
                                        start=True, stop=True)
                    last.then_inc(shifted_ready, 1)
                return work

            def weigh(j):
                def work(h, p):
                    b = 2 * h + p
                    pe.wait_ge(low_ready[j % 2], 2 * b + j // 2 + 1)
                    if j == 0:
                        pe.wait_ge(vn_ready, b + 1)
                        wait_free(pe, x1_ready, b, 1)
                    for k in range(HG):
                        head, at = HG * k + j, (HG * j + k) * P
                        for e in e_hi, e_lo:
                            last = T.matmul(psB[:, 2 * (HD + 1) * head:2 * (HD + 1) * (head + 1)], e[0:NK, p, at:at + P],
                                            g.vaug[0:NK, p, head, :, :].rearrange("p c i -> p (c i)"), start=e is e_hi, stop=e is e_lo)
                    if j == HG - 1:
                        last.then_inc(pv_ready, 1)
                return work

            def turn_o(h, p):
                b = 2 * h + p
                pe.wait_ge(o_ready, b + 1)
                T.transpose(psB[:, 3 * P:4 * P], o[:, p, :], ident).then_inc(o_turned, 1)

            def out_project(h, p):
                b = 2 * h + p
                pe.wait_ge(oT_ready, b + 1)
                T.matmul(psB[:, 3 * P:4 * P], oT[:, p, :], g.w_small[:, 0:P], start=True, stop=True).then_inc(y_ready, 1)

            def turn_xn1(h, p):
                b = 2 * h + p
                wait_free(pe, place_steps, b, 2, 6)
                pe.wait_ge(xn1_ready, b + 1)
                T.transpose(psR[:, P:2 * P], xn1[:, p, :], ident).then_inc(xn1_turned, 1)

            def route(h, p):
                b = 2 * h + p
                pe.wait_ge(xn1T_ready, b + 1)
                T.matmul(psR[:, 0:E0], xn1T[:, p, :], g.w_small[:, P:P + E0], start=True, stop=True).then_inc(logits_ready, 1)

            def count(h, p):
                b = 2 * h + p
                pe.wait_ge(rank_steps, 9 * b + 9)
                if not (isinstance(b, int) and b == NB - 1):
                    pe.wait_ge(shift_steps, 2 * b + 4)
                T.matmul(psR[:, 8:8 + E0], g.consts[:, C_TRI:C_TRI + P], picked[:, p, :], start=True, stop=True)
                T.matmul(psR[:, 16:16 + E0], g.consts[:, C_ONE:C_ONE + P], picked[:, p, :], start=True, stop=True).then_inc(counted, 1)

            pipeline(pe, [(5, weigh(3)), (3, turn_qk), (4, shifted(0)), (4, shifted(1)), (1, turn_xc), (5, turn_o), (3, scores(0)), (3, scores(1)),
                          (6, turn_xn1), (4, shifted(2)), (3, scores(2)), (4, shifted(3)), (5, out_project), (3, scores(3)), (6, route),
                          (1, project), (4, weigh(0)), (4, weigh(1)), (3, turn_q2), (7, count), (4, weigh(2))], NB, 10)


def tables(nc, g):
    with ExitStack() as ctx:
        def sb(name, shape, dt=F32):
            return ctx.enter_context(nc.sbuf_tensor(name, shape, dt))

        count, tiles_i, tiles, upto, upto2, before = (sb("count", [P, E0]), sb("tiles_i", [P, E0], I32), sb("tiles", [P, E0]),
                                                      sb("upto", [P, E0]), sb("upto2", [P, E0]), sb("before", [P, E0]))
        pad_f, pad = sb("pad_f", [P, E0]), sb("pad", [P, E0], I32)
        past, te, used, hot = sb("past", [P, NT * E0]), sb("te", [P, NT]), sb("used", [P, NT]), sb("hot", [P, NT * E0])
        first, row, tab, moved, step = (sb("first", [P, NT]), sb("row", [P, NT]), sb("tab", [P, 2 * NT]), sb("moved", [P, E0]), sb("step", [P, E0]))
        over, shift_by = sb("over", [P, 2 * NB * E0]), sb("shift_by", [P, 2 * NB])
        table_steps, pads_ready = ctx.enter_context(nc.semaphore("table_steps")), ctx.enter_context(nc.semaphore("pads_ready"))
        padded = ctx.enter_context(nc.semaphore("padded"))
        block = ctx.enter_context(nc.Block())

        @block.scalar
        def _(act):
            act.dma_start(g.b_row0[:, :, :].rearrange("p e f -> p (e f)"), g.d_b_row0.partition_broadcast(P)).then_inc(g.biases0_in, 16)

        @block.vector
        def _(dve):
            V = nc.vector
            st = Steps(dve, table_steps, 0, 0)

            def do(instruction):
                st(instruction)
                st.wait()

            do(V.tensor_scalar(pad_f[:, :], g.run[:, :], g.consts[:, C_P:C_P + 1], None, ALU.add))
            V.tensor_copy(pad[:, :], pad_f[:, :]).then_inc(pads_ready, 1)
            do(V.tensor_tensor(count[:, :], g.run[:, :], g.consts[:, C_RUN:C_RUN + E0], ALU.subtract))
            do(V.tensor_scalar(count[:, :], count[:, :], float(P - 1), None, ALU.add))
            do(V.tensor_copy(tiles_i[:, :], count[:, :]))
            do(V.tensor_scalar(tiles_i[:, :], tiles_i[:, :], 7, None, ALU.logical_shift_right))
            do(V.tensor_copy(tiles[:, :], tiles_i[:, :]))
            a, b = tiles, upto
            do(V.tensor_copy(upto[:, :], tiles[:, :]))
            do(V.tensor_copy(upto2[:, :], tiles[:, :]))
            a, b = upto, upto2
            for shift in (1, 2, 4):
                do(V.tensor_copy(b[:, 0:shift], a[:, 0:shift]))
                do(V.tensor_tensor(b[:, shift:E0], a[:, shift:E0], a[:, 0:E0 - shift], ALU.add))
                a, b = b, a
            do(V.tensor_tensor(before[:, :], a[:, :], tiles[:, :], ALU.subtract))
            jrow = g.consts[:, C_J:C_J + NT]
            pastv, hotv = (x[:, :].rearrange("p (j e) -> p j e", j=NT) for x in (past, hot))
            do(V.tensor_tensor(pastv, bcast(a[:, :].unsqueeze(1), P, NT, E0), bcast(jrow.unsqueeze(2), P, NT, E0), ALU.is_le))
            do(V.tensor_reduce(te[:, :], pastv, AX, ALU.add))
            do(V.tensor_scalar(used[:, :], te[:, :], E0 - 0.5, None, ALU.is_lt))
            do(V.tensor_scalar(tab[:, 0:NT], te[:, :], float(E0 - 1), None, ALU.min))
            do(V.tensor_tensor(hotv, bcast(tab[:, 0:NT].unsqueeze(2), P, NT, E0),
                               bcast(g.consts[:, C_J:C_J + E0].unsqueeze(1), P, NT, E0), ALU.is_equal))
            do(V.tensor_tensor(hotv, hotv, bcast(before[:, :].unsqueeze(1), P, NT, E0), ALU.mult))
            do(V.tensor_reduce(first[:, :], hotv, AX, ALU.add))
            do(V.tensor_tensor(first[:, :], jrow, first[:, :], ALU.subtract))
            do(V.tensor_scalar(first[:, :], first[:, :], float(P), None, ALU.mult))
            do(V.tensor_scalar(row[:, :], tab[:, 0:NT], float(REGION), None, ALU.mult))
            do(V.tensor_tensor(row[:, :], row[:, :], first[:, :], ALU.add))
            do(V.tensor_scalar(row[:, :], row[:, :], float(ZERO_ROW), None, ALU.subtract))
            do(V.tensor_tensor(row[:, :], row[:, :], used[:, :], ALU.mult))
            do(V.tensor_scalar(tab[:, NT:2 * NT], row[:, :], float(ZERO_ROW), None, ALU.add))
            do(V.tensor_copy(g.table[:, :], tab[:, :]))
            starts = g.consts[:, C_RUN:C_RUN + E0]
            do(V.tensor_scalar(moved[:, :], before[:, :], float(P), None, ALU.mult))
            do(V.tensor_tensor(moved[:, :], moved[:, :], starts, ALU.subtract))
            do(V.tensor_copy(step[:, 0:1], moved[:, 0:1]))
            do(V.tensor_tensor(step[:, 1:E0], moved[:, 1:E0], moved[:, 0:E0 - 1], ALU.subtract))
            slots = g.slotf[:, :, :].rearrange("p b c -> p (b c)")
            overv = over[:, :].rearrange("p (s e) -> p s e", e=E0)
            do(V.tensor_tensor(overv, bcast(slots.unsqueeze(2), P, 2 * NB, E0), bcast(starts.unsqueeze(1), P, 2 * NB, E0), ALU.is_ge))
            do(V.tensor_tensor(overv, overv, bcast(step[:, :].unsqueeze(1), P, 2 * NB, E0), ALU.mult))
            do(V.tensor_reduce(shift_by[:, :], overv, AX, ALU.add))
            do(V.tensor_tensor(g.slots[:, :, :].rearrange("p b c -> p (b c)"), shift_by[:, :], slots, ALU.add))

        @block.gpsimd
        def _(pool):
            pool.wait_ge(pads_ready, 1)
            for e in range(E0):
                nc.gpsimd.indirect_dma_start(g.xs[:, :], bass.IndirectOffsetOnAxis(pad[:, e:e + 1], 0),
                                             g.zeros[:, :], None).then_inc(padded, 16)
            pool.wait_ge(padded, 16 * E0)


def experts0(nc, g):
    with ExitStack() as ctx:
        def sb(name, shape, dt=F32):
            return ctx.enter_context(nc.sbuf_tensor(name, shape, dt))

        def sem(name):
            return ctx.enter_context(nc.semaphore(name))

        xt, xtT = sb("xt", [P, 2, P]), sb("xtT", [P, 2, P])
        zg, y, z1, hid, hT, yt = (sb("zg", [P, 2, F0]), sb("y", [P, 2, F0]), sb("z1", [P, 2, F0]), sb("hid", [P, 2, F0]), sb("hT", [P, 2, F0]), sb("yt", [P, 2, P]))
        w_up, w_down, b_row, b_down = g.w_up0, g.w_down0, g.b_row0, g.b_down0
        rows_in, rows_out = [sem("rows_in_even"), sem("rows_in_odd")], [sem("rows_out_even"), sem("rows_out_odd")]
        turned, xtT_ready, zg_done, z1_done = sem("x_turned"), sem("xtT_ready"), sem("zg_done"), sem("z1_done")
        zg_ready, z1_ready, y_ready, hid_ready = sem("zg_ready"), sem("z1_ready"), sem("gelu_ready"), sem("hid_ready")
        h_turned, hT_ready, down_done, yt_ready = sem("h_turned"), sem("hT_ready"), sem("down_done"), sem("yt_ready")
        block = ctx.enter_context(nc.Block())
        psX, psH, psY = g.bank[0], g.bank[5], g.bank[6]
        psG, psZ = [g.bank[1], g.bank[2]], [g.bank[3], g.bank[4]]

        @block.sync
        def _(sp):
            def load_rows(h, p):
                j = 2 * h + p
                wait_free(sp, turned, j, 2)
                row = sp.value_load(g.table[0:1, ds(NT + j, 1)], min_val=0, max_val=ZERO_ROW)
                sp.dma_start(xt[:, p, :], g.xs[ds(row, P), :]).then_inc(rows_in[p], 16)

            def store_rows(h, p):
                j = 2 * h + p
                sp.wait_ge(yt_ready, j + 1)
                sp.dma_start(g.ys[ds(P * j, P), :], yt[:, p, :]).then_inc(rows_out[p], 16)
            pipeline(sp, [(0, load_rows), (4, store_rows)], NT, 6)
            for p in range(2):
                sp.wait_ge(rows_out[p], 16 * (NT // 2))

        @block.scalar
        def _(act):
            def x_copy(h, p):
                j = 2 * h + p
                act.wait_ge(turned, j + 1)
                wait_free(act, z1_done, j, 2)
                nc.scalar.activation(xtT[:, p, :], psX[:, 0:P], ACT.Copy).then_inc(xtT_ready, 1)

            def gelu(h, p):
                j = 2 * h + p
                act.wait_ge(zg_ready, j + 1)
                wait_free(act, hid_ready, j, 2)
                nc.scalar.activation(y[:, p, :], zg[:, p, :], ACT.Gelu).then_inc(y_ready, 1)

            def hid_copy(h, p):
                j = 2 * h + p
                act.wait_ge(h_turned, j + 1)
                wait_free(act, down_done, j, 2)
                nc.scalar.activation(hT[:, p, :], psH[:, :], ACT.Copy).then_inc(hT_ready, 1)
            pipeline(act, [(1, x_copy), (3, hid_copy), (2, gelu)], NT, 6)

        @block.tensor
        def _(pe):
            T = nc.tensor
            ident = g.consts[:, C_ID:C_ID + P]
            pe.wait_ge(g.weights0_in, 48)

            def turn_x(h, p):
                j = 2 * h + p
                pe.wait_ge(rows_in[p], 16 * h + 16)
                wait_free(pe, xtT_ready, j, 1)
                T.transpose(psX[:, 0:P], xt[:, p, :], ident).then_inc(turned, 1)

            def up(h, p):
                j = 2 * h + p
                e = pe.value_load(g.table[0:1, ds(j, 1)], min_val=0, max_val=E0 - 1)
                pe.wait_ge(xtT_ready, j + 1)
                wait_free(pe, zg_ready, j, 2)
                wait_free(pe, z1_ready, j, 2)
                T.matmul(psG[p][:, :], xtT[:, p, :], w_up[:, ds(e, 1), 0:F0].rearrange("p a f -> p (a f)"), start=True, stop=True).then_inc(zg_done, 1)
                T.matmul(psZ[p][:, :], xtT[:, p, :], w_up[:, ds(e, 1), F0:2 * F0].rearrange("p a f -> p (a f)"), start=True, stop=True).then_inc(z1_done, 1)

            def turn_hid(h, p):
                j = 2 * h + p
                pe.wait_ge(hid_ready, j + 1)
                wait_free(pe, hT_ready, j, 1)
                for c in range(FC):
                    last = T.transpose(psH[:, P * c:P * c + P], hid[:, p, P * c:P * c + P], ident)
                last.then_inc(h_turned, 1)

            def down(h, p):
                j = 2 * h + p
                e = pe.value_load(g.table[0:1, ds(j, 1)], min_val=0, max_val=E0 - 1)
                pe.wait_ge(hT_ready, j + 1)
                wait_free(pe, yt_ready, j, 1)
                for c in range(FC):
                    last = T.matmul(psY[:, 0:P], hT[:, p, P * c:P * c + P], w_down[:, ds(e, 1), P * c:P * c + P].rearrange("p a f -> p (a f)"),
                                    start=c == 0, stop=c == FC - 1)
                last.then_inc(down_done, 1)
            pipeline(pe, [(1, turn_x), (3, turn_hid), (1, up), (3, down)], NT, 6)

        @block.vector
        def _(dve):
            V = nc.vector
            dve.wait_ge(g.biases0_in, 32)

            def add_bias(h, p):
                j = 2 * h + p
                e = dve.value_load(g.table[0:1, ds(j, 1)], min_val=0, max_val=E0 - 1)
                dve.wait_ge(zg_done, j + 1)
                wait_free(dve, y_ready, j, 2)
                V.tensor_tensor(zg[:, p, :], psG[p][:, :], b_row[:, ds(e, 1), 0:F0].rearrange("p a f -> p (a f)"), ALU.add).then_inc(zg_ready, 1)
                dve.wait_ge(z1_done, j + 1)
                wait_free(dve, hid_ready, j, 2)
                V.tensor_tensor(z1[:, p, :], psZ[p][:, :], b_row[:, ds(e, 1), F0:2 * F0].rearrange("p a f -> p (a f)"), ALU.add).then_inc(z1_ready, 1)

            def multiply(h, p):
                j = 2 * h + p
                dve.wait_ge(y_ready, j + 1)
                dve.wait_ge(z1_ready, j + 1)
                wait_free(dve, h_turned, j, 2)
                V.tensor_tensor(hid[:, p, :], y[:, p, :], z1[:, p, :], ALU.mult).then_inc(hid_ready, 1)

            def down_bias(h, p):
                j = 2 * h + p
                e = dve.value_load(g.table[0:1, ds(j, 1)], min_val=0, max_val=E0 - 1)
                dve.wait_ge(down_done, j + 1)
                if not (isinstance(j, int) and j < 2):
                    dve.wait_ge(rows_out[p], 16 * h)
                V.tensor_tensor(yt[:, p, :], psY[:, 0:P], b_down[:, ds(e, 1), :].rearrange("p a f -> p (a f)"), ALU.add).then_inc(yt_ready, 1)
            pipeline(dve, [(2, multiply), (1, add_bias), (3, down_bias)], NT, 6)


def attention1(nc, g):
    with ExitStack() as ctx:
        def sb(name, shape, dt=F32):
            return ctx.enter_context(nc.sbuf_tensor(name, shape, dt))

        def sem(name):
            return ctx.enter_context(nc.semaphore(name))

        idx, got = sb("idx", [P, 2, 2], I32), sb("got", [P, 2, 2 * P])
        st2, mv2, ve2, rstd2 = sb("st2", [P, 2, 6]), sb("mv2", [P, 2, 2]), sb("ve2", [P, 2, 1]), sb("rstd2", [P, 2, 1])
        xn2, xn2T, q1T, k1T = sb("xn2", [P, 2, P]), sb("xn2T", [P, 2, P]), sb("q1T", [P, 2, P]), sb("k1T", [P, 2, NK])
        mx1, p1, den, rden, p1T, r, rT = (sb("mx1", [P, 2, 1]), sb("p1", [P, 2, NK]), sb("den", [P, 2, 1]), sb("rden", [P, 2, 1]),
                                          sb("p1T", [P, 2, P]), sb("r", [P, 2, P]), sb("rT", [P, 2, P]))
        st3, mv3, ve3, rstd3 = sb("st3", [P, 2, 6]), sb("mv3_", [P, 2, 2]), sb("ve3_", [P, 2, 1]), sb("rstd3_", [P, 2, 1])
        xn3, xn3T = sb("xn3", [P, 2, P]), sb("xn3T", [P, 2, P])
        biased, top, rest, mask = sb("biased", [P, 2, E1]), sb("top", [P, 2, 8]), sb("rest", [P, 2, E1]), sb("mask", [P, 2, E1])
        en, sig, ws, wsum = sb("en", [P, 2, E1]), sb("sig", [P, 2, E1]), sb("ws", [P, 2, E1]), sb("wsum", [P, 2, 1])
        cw, low, parts = sb("cw", [P, 2, E1]), sb("low", [P, 2, E1]), sb("parts", [P, 2, 2 * E1], F16)

        stage = sb("stage", [P, 2, W_PART])
        weights_in, w_hi_ready, w_split = [sem("weights_in_even"), sem("weights_in_odd")], sem("w_hi_ready"), sem("w_split")
        sel_in = sem("sel_in")

        psA, psB, psC, psD, psE = g.bank[0], g.bank[1], g.bank[2], g.bank[3], [g.bank[4], g.bank[5]]
        psG16 = g.bank[6].bitcast(F16)
        gathered = [sem("gathered_even"), sem("gathered_odd")]
        idx_ready, comb_steps, x2_stats, x2_var, x2_rstd, xn2_ready = sem("idx_ready"), sem("comb_steps"), sem("x2_stats"), sem("x2_var"), sem("x2_rstd"), sem("xn2_ready")
        xn2_turned, xn2T_ready, qk_done, k1T_ready, s_done = sem("xn2_turned"), sem("xn2T_ready"), sem("qk_done"), sem("k1T_ready"), sem("s_done")
        mx1_steps, p1_ready, p1_turned, p1T_ready, av_done = sem("mx1_steps"), sem("p1_ready"), sem("p1_turned"), sem("p1T_ready"), sem("av_done")
        rden_ready, r_ready, r_turned, rT_ready, o1_done, bo1_added = sem("rden_ready"), sem("r_ready"), sem("r_turned"), sem("rT_ready"), sem("o1_done"), sem("bo1_added")
        x3_ready, x3_stats, x3_var, x3_rstd, xn3_ready, xn3_turned = sem("x3_ready"), sem("x3_stats"), sem("x3_var"), sem("x3_rstd"), sem("xn3_ready"), sem("xn3_turned")
        xn3T_ready, xn3T_kept, aff_done, en_ready, top_steps, cw_steps = sem("xn3T_ready"), sem("xn3T_kept"), sem("aff_done"), sem("en_ready"), sem("top_steps"), sem("cw_steps")
        parts_ready, parts_turned, cwT_ready = sem("parts_ready"), sem("parts_turned"), sem("cwT_ready")
        block = ctx.enter_context(nc.Block())

        @block.sync
        def _(sp):
            def load_weights(h, p):
                b = 2 * h + p
                wait_free(sp, w_split, b, 2)
                sp.dma_start(stage[:, p, :], g.d_w1[:, ds(W_PART * b, W_PART)]).then_inc(weights_in[p], 16)
            sp.dma_start(g.sel[:, :], g.d_sel).then_inc(sel_in, 16)
            pipeline(sp, [(0, load_weights)], NB, 2)
            sp.wait_ge(sel_in, 16)

        @block.gpsimd
        def _(pool):
            def rstd_of(var, var_eps, out, b, steps, ready):
                st = Steps(pool, steps, 1, b)
                st(nc.gpsimd.tensor_scalar(var_eps, var, EPS, None, ALU.add))
                st.wait()
                nc.gpsimd.tensor_tensor(out, var_eps, g.mhalf[:, 0:1], ALU.pow).then_inc(ready, 1)

            def gather(h, p):
                b = 2 * h + p
                wait_apart(g, pool, idx_ready, b + 1)
                wait_free(pool, comb_steps, b, 2, 2, apart=g)
                for c in range(2):
                    nc.gpsimd.indirect_dma_start(got[:, p, P * c:P * c + P], None, g.ys[:, :],
                                                 bass.IndirectOffsetOnAxis(idx[:, p, c:c + 1], 0)).then_inc(gathered[p], 16)

            def x2_scale(h, p):
                b = 2 * h + p
                wait_apart(g, pool, x2_stats, 2 * b + 2)
                wait_free(pool, xn2_ready, b, 2, apart=g)
                rstd_of(mv2[:, p, 1:2], ve2[:, p, :], rstd2[:, p, :], b, x2_var, x2_rstd)

            def add_bo(h, p):
                b = 2 * h + p
                pool.wait_ge(xn2_ready, b + 1)
                xb = g.X[:, ds(b, 1), :].rearrange("p a d -> p (a d)")
                nc.gpsimd.tensor_tensor(xb, xb, g.rows[:, R_BO1:R_BO1 + P], ALU.add).then_inc(bo1_added, 1)

            def x3_scale(h, p):
                b = 2 * h + p
                wait_apart(g, pool, x3_stats, 2 * b + 2)
                wait_free(pool, xn3_ready, b, 2, apart=g)
                rstd_of(mv3[:, p, 1:2], ve3[:, p, :], rstd3[:, p, :], b, x3_var, x3_rstd)

            pipeline(pool, [(6, add_bo), (2, gather), (3, x2_scale), (6, x3_scale)], NB, 10)

        @block.vector
        def _(dve):
            V = nc.vector

            def copy_slots(h, p):
                b = 2 * h + p
                if not (isinstance(b, int) and b < 2):
                    dve.wait_ge(gathered[p], 32 * h)
                V.tensor_copy(idx[:, p, :], g.slots[:, ds(b, 1), :].rearrange("p a c -> p (a c)")).then_inc(idx_ready, 1)

            def combine(part):
                def work(h, p):
                    b = 2 * h + p
                    xb = g.X[:, ds(b, 1), :].rearrange("p a d -> p (a d)")
                    if part == 0:
                        dve.wait_ge(gathered[p], 32 * h + 32)
                    st = Steps(dve, comb_steps, 2, b, part)
                    if part == 1:
                        st.wait_apart(g)
                    st(V.scalar_tensor_tensor(xb, got[:, p, P * part:P * part + P], g.gate[:, ds(b, 1), part:part + 1].rearrange("p a c -> p (a c)"),
                                              xb, ALU.mult, ALU.add))
                return work

            def x2_statistics(h, p):
                b = 2 * h + p
                wait_apart(g, dve, comb_steps, 2 * b + 2)
                st = Steps(dve, x2_stats, 2, b)
                st(V.bn_stats(st2[:, p, :], g.X[:, ds(b, 1), :].rearrange("p a d -> p (a d)")))

            def x2_variance(h, p):
                b = 2 * h + p
                wait_free(dve, x2_rstd, b, 2, apart=g)
                wait_free(dve, xn2_ready, b, 2, apart=g)
                st = Steps(dve, x2_stats, 2, b, 1)
                st.wait_apart(g)
                st(V.bn_aggr(mv2[:, p, :], st2[:, p, :]))

            def x2_norm(h, p):
                b = 2 * h + p
                xb = g.X[:, ds(b, 1), :].rearrange("p a d -> p (a d)")
                dve.wait_ge(x2_rstd, b + 1)
                wait_free(dve, xn2_turned, b, 2)
                wait_free(dve, r_ready, b, 2)
                V.tensor_scalar(xn2[:, p, :], xb, mv2[:, p, 0:1], rstd2[:, p, :], ALU.subtract, ALU.mult).then_inc(xn2_ready, 1)

            def maximum(h, p):
                b = 2 * h + p
                dve.wait_ge(s_done, b + 1)
                wait_free(dve, p1_ready, b, 2)
                st = Steps(dve, mx1_steps, 2, b)
                st(V.tensor_reduce(mx1[:, p, :], psE[p][:, 0:NK], AX, ALU.max))

            def negative(h, p):
                b = 2 * h + p
                st = Steps(dve, mx1_steps, 2, b, 1)
                st.wait()
                st(V.tensor_scalar(mx1[:, p, :], mx1[:, p, :], -float(P) ** -0.5, None, ALU.mult))

            def sum_inverse(h, p):
                b = 2 * h + p
                dve.wait_ge(p1_ready, b + 1)
                wait_free(dve, r_ready, b, 2)
                V.reciprocal(rden[:, p, :], den[:, p, :]).then_inc(rden_ready, 1)

            def p_copy(h, p):
                b = 2 * h + p
                dve.wait_ge(p1_turned, b + 1)
                wait_free(dve, av_done, b, 2)
                V.tensor_copy(p1T[0:NK, p, :], psB[0:NK, 0:P]).then_inc(p1T_ready, 1)

            def attended(h, p):
                b = 2 * h + p
                dve.wait_ge(av_done, b + 1)
                dve.wait_ge(rden_ready, b + 1)
                dve.wait_ge(xn2_ready, b + 1)
                wait_free(dve, r_turned, b, 2)
                V.scalar_tensor_tensor(r[:, p, :], psB[:, P:2 * P], rden[:, p, :], xn2[:, p, :], ALU.mult, ALU.add).then_inc(r_ready, 1)

            def residual(h, p):
                b = 2 * h + p
                dve.wait_ge(o1_done, b + 1)
                dve.wait_ge(bo1_added, b + 1)
                xb = g.X[:, ds(b, 1), :].rearrange("p a d -> p (a d)")
                V.tensor_tensor(xb, psC[:, P:2 * P], xb, ALU.add).then_inc(x3_ready, 1)

            def x3_statistics(h, p):
                b = 2 * h + p
                wait_apart(g, dve, x3_ready, b + 1)
                st = Steps(dve, x3_stats, 2, b)
                st(V.bn_stats(st3[:, p, :], g.X[:, ds(b, 1), :].rearrange("p a d -> p (a d)")))

            def x3_variance(h, p):
                b = 2 * h + p
                wait_free(dve, x3_rstd, b, 2, apart=g)
                wait_free(dve, xn3_ready, b, 2, apart=g)
                st = Steps(dve, x3_stats, 2, b, 1)
                st.wait_apart(g)
                st(V.bn_aggr(mv3[:, p, :], st3[:, p, :]))

            def x3_norm(h, p):
                b = 2 * h + p
                xb = g.X[:, ds(b, 1), :].rearrange("p a d -> p (a d)")
                dve.wait_ge(x3_rstd, b + 1)
                wait_free(dve, xn3_turned, b, 2)
                V.tensor_scalar(xn3[:, p, :], xb, mv3[:, p, 0:1], rstd3[:, p, :], ALU.subtract, ALU.mult).then_inc(xn3_ready, 1)

            def x_low(h, p):
                b = 2 * h + p
                dve.wait_ge(xn3T_ready, b + 1)
                V.scalar_tensor_tensor(g.XT_lo[:, ds(b, 1), :].rearrange("p a t -> p (a t)"), xn3T[:, p, :], X_SCALE,
                                       g.XT_hi[:, ds(b, 1), :].rearrange("p a t -> p (a t)"), ALU.mult, ALU.subtract).then_inc(xn3T_kept, 1)

            def weights_low(h, p):
                b = 2 * h + p
                dve.wait_ge(w_hi_ready, b + 1)
                V.scalar_tensor_tensor(g.W1_lo[:, ds(W_PART * b, W_PART)], stage[:, p, :], W_SCALE, g.W1_hi[:, ds(W_PART * b, W_PART)],
                                       ALU.mult, ALU.subtract).then_inc(w_split, 1)

            def choose(part):
                def work(h, p):
                    b = 2 * h + p
                    st = Steps(dve, top_steps, 4, b, part)
                    if part == 0:
                        dve.wait_ge(aff_done, b + 1)
                        st(V.tensor_tensor(biased[:, p, :], psD[:, 0:E1], g.rows[:, R_EB:R_EB + E1], ALU.add))
                    elif part == 1:
                        st.wait_apart(g)
                        st(V.max(top[:, p, :], biased[:, p, :]))
                    elif part == 2:
                        st.wait_apart(g)
                        st(V.match_replace(rest[:, p, :], top[:, p, :], biased[:, p, :], -3.0e38))
                    else:
                        st.wait()
                        st(V.tensor_tensor(mask[:, p, :], biased[:, p, :], rest[:, p, :], ALU.not_equal))
                return work

            def weights(part):
                def work(h, p):
                    b = 2 * h + p
                    st = Steps(dve, cw_steps, 9, b, part)
                    if part == 0:
                        dve.wait_ge(en_ready, b + 1)
                    else:
                        st.wait()
                    if part == 0:
                        st(V.tensor_scalar(sig[:, p, :], en[:, p, :], 1.0, None, ALU.add))
                    elif part == 1:
                        st(V.reciprocal(sig[:, p, :], sig[:, p, :]))
                    elif part == 2:
                        dve.wait_ge(top_steps, 4 * b + 4)
                        st(V.tensor_tensor(ws[:, p, :], sig[:, p, :], mask[:, p, :], ALU.mult))
                    elif part == 3:
                        st(V.tensor_reduce(wsum[:, p, :], ws[:, p, :], AX, ALU.add))
                    elif part == 4:
                        st(V.tensor_scalar(wsum[:, p, :], wsum[:, p, :], 1e-8, None, ALU.add))
                    elif part == 5:
                        st(V.reciprocal(wsum[:, p, :], wsum[:, p, :]))
                    elif part == 6:
                        st(V.tensor_scalar(cw[:, p, :], ws[:, p, :], wsum[:, p, :], None, ALU.mult))
                    elif part == 7:
                        wait_free(dve, parts_turned, b, 2)
                        st(V.tensor_copy(parts[:, p, 0:E1], cw[:, p, :]))
                    elif part == 8:
                        st(V.tensor_tensor(low[:, p, :], cw[:, p, :], parts[:, p, 0:E1], ALU.subtract))
                    else:
                        V.tensor_scalar(parts[:, p, E1:2 * E1], low[:, p, :], 2048.0, None, ALU.mult).then_inc(parts_ready, 1)
                return work
            pipeline(dve, [(6, choose(2)), (6, weights(0)), (0, copy_slots), (3, maximum), (6, choose(3)), (5, x3_norm), (3, negative),
                           (6, weights(1)), (1, combine(0)), (7, x_low), (1, combine(1)), (2, weights_low), (1, x2_statistics),
                           (6, weights(2)), (3, sum_inverse), (4, residual), (1, x2_variance), (6, weights(3)), (3, p_copy),
                           (6, weights(4)), (7, weights(9)), (6, weights(5)), (4, x3_statistics), (6, weights(6)), (5, choose(0)),
                           (4, x3_variance), (3, attended), (6, weights(7)), (5, choose(1)), (1, x2_norm), (6, weights(8))], NB, 10)

        @block.scalar
        def _(act):
            A = nc.scalar

            def xn2_copy(h, p):
                b = 2 * h + p
                act.wait_ge(xn2_turned, b + 1)
                wait_free(act, qk_done, b, 2)
                A.activation(xn2T[:, p, :], psA[:, 0:P], ACT.Copy).then_inc(xn2T_ready, 1)

            def qk_bias(h, p):
                b = 2 * h + p
                act.wait_ge(qk_done, b + 1)
                wait_free(act, s_done, b, 2)
                A.activation(q1T[:, p, :], psA[:, P:2 * P], ACT.Identity, bias=g.cols[:, BQ1:BQ1 + 1]).then_inc(k1T_ready, 1)
                A.activation(k1T[:, p, :], psA[:, 2 * P:2 * P + NK], ACT.Identity, bias=g.cols[:, BK1:BK1 + 1]).then_inc(k1T_ready, 1)

            def exponential(h, p):
                b = 2 * h + p
                act.wait_ge(mx1_steps, 2 * b + 2)
                wait_free(act, p1_turned, b, 2)
                wait_free(act, rden_ready, b, 2)
                A.activation(p1[:, p, :], psE[p][:, 0:NK], ACT.Exp, bias=mx1[:, p, :], scale=float(P) ** -0.5,
                             accum_out=den[:, p, :]).then_inc(p1_ready, 1)

            def r_copy(h, p):
                b = 2 * h + p
                act.wait_ge(r_turned, b + 1)
                wait_free(act, o1_done, b, 2)
                A.activation(rT[:, p, :], psC[:, 0:P], ACT.Copy).then_inc(rT_ready, 1)

            def xn3_copy(h, p):
                b = 2 * h + p
                act.wait_ge(xn3_turned, b + 1)
                wait_free(act, aff_done, b, 2)
                wait_free(act, xn3T_kept, b, 2)
                A.activation(xn3T[:, p, :], psD[:, P:2 * P], ACT.Copy)
                A.activation(g.XT_hi[:, ds(b, 1), :].rearrange("p a t -> p (a t)"), psD[:, P:2 * P], ACT.Copy, scale=X_SCALE).then_inc(xn3T_ready, 1)

            def weights_high(h, p):
                b = 2 * h + p
                act.wait_ge(weights_in[p], 16 * h + 16)
                A.activation(g.W1_hi[:, ds(W_PART * b, W_PART)], stage[:, p, :], ACT.Copy, scale=W_SCALE).then_inc(w_hi_ready, 1)

            def aff_exp(h, p):
                b = 2 * h + p
                act.wait_ge(top_steps, 4 * b + 1)
                wait_free(act, cw_steps, b, 2, 9)
                A.activation(en[:, p, :], psD[:, 0:E1], ACT.Exp, scale=-1.0).then_inc(en_ready, 1)

            def cw_copy(h, p):
                b = 2 * h + p
                act.wait_ge(parts_turned, b + 1)
                A.activation(g.CWT[:, ds(b, 1), :].rearrange("p a t -> p (a t)"), psG16[:, 0:P], ACT.Copy).then_inc(cwT_ready, 1)
            pipeline(act, [(2, weights_high), (3, qk_bias), (6, aff_exp), (4, r_copy), (3, exponential), (2, xn2_copy), (8, cw_copy), (5, xn3_copy)], NB, 10)

        @block.tensor
        def _(pe):
            T = nc.tensor
            ident = g.consts[:, C_ID:C_ID + P]
            wo1, cent, wq1, wk1 = (g.w_small[:, 136:264], g.w_small[:, 264:328], g.w_small[:, 328:456], g.w_small[:, 456:584])

            def turn_xn2(h, p):
                b = 2 * h + p
                pe.wait_ge(xn2_ready, b + 1)
                wait_free(pe, k1T_ready, b, 1, 2)
                T.transpose(psA[:, 0:P], xn2[:, p, :], ident).then_inc(xn2_turned, 1)

            def project(h, p):
                b = 2 * h + p
                pe.wait_ge(xn2T_ready, b + 1)
                T.matmul(psA[:, P:2 * P], wq1, xn2T[:, p, :], start=True, stop=True)
                T.matmul(psA[:, 2 * P:2 * P + NK], wk1, g.ctxT[:, ds(b, 1), :].rearrange("p a k -> p (a k)"), start=True, stop=True).then_inc(qk_done, 1)

            def scores(h, p):
                b = 2 * h + p
                pe.wait_ge(k1T_ready, 2 * b + 2)
                wait_free(pe, p1_ready, b, 2)
                T.matmul(psE[p][:, 0:NK], q1T[:, p, :], k1T[:, p, :], start=True, stop=True).then_inc(s_done, 1)

            def turn_p(h, p):
                b = 2 * h + p
                pe.wait_ge(p1_ready, b + 1)
                wait_free(pe, r_ready, b, 1)
                T.transpose(psB[0:NK, 0:P], p1[:, p, :], ident).then_inc(p1_turned, 1)

            def attend(h, p):
                b = 2 * h + p
                pe.wait_ge(p1T_ready, b + 1)
                T.matmul(psB[:, P:2 * P], p1T[0:NK, p, :], g.V1[0:NK, ds(b, 1), :].rearrange("p a d -> p (a d)"), start=True, stop=True).then_inc(av_done, 1)

            def turn_r(h, p):
                b = 2 * h + p
                pe.wait_ge(r_ready, b + 1)
                wait_free(pe, x3_ready, b, 1)
                T.transpose(psC[:, 0:P], r[:, p, :], ident).then_inc(r_turned, 1)

            def out_project(h, p):
                b = 2 * h + p
                pe.wait_ge(rT_ready, b + 1)
                T.matmul(psC[:, P:2 * P], rT[:, p, :], wo1, start=True, stop=True).then_inc(o1_done, 1)

            def turn_xn3(h, p):
                b = 2 * h + p
                pe.wait_ge(xn3_ready, b + 1)
                wait_free(pe, en_ready, b, 1)
                T.transpose(psD[:, P:2 * P], xn3[:, p, :], ident).then_inc(xn3_turned, 1)

            def affinities(h, p):
                b = 2 * h + p
                pe.wait_ge(xn3T_ready, b + 1)
                T.matmul(psD[:, 0:E1], xn3T[:, p, :], cent, start=True, stop=True).then_inc(aff_done, 1)

            def turn_parts(h, p):
                b = 2 * h + p
                pe.wait_ge(parts_ready, b + 1)
                wait_free(pe, cwT_ready, b, 1)
                T.transpose(psG16[:, 0:P], parts[:, p, :], g.ident16[:, :]).then_inc(parts_turned, 1)
            pipeline(pe, [(5, out_project), (6, turn_xn3), (4, turn_p), (3, project), (6, affinities), (4, attend), (3, scores), (4, turn_r),
                          (8, turn_parts), (2, turn_xn2)], NB, 10)


def experts1(nc, g):
    with ExitStack() as ctx:
        def sb(name, shape, dt=F32):
            return ctx.enter_context(nc.sbuf_tensor(name, shape, dt))

        def sem(name):
            return ctx.enter_context(nc.semaphore(name))

        N = LOTS * P
        NS = NFT + 1
        LAG = 3
        TURN = LAG + 2
        ws_down, ws_up, ws_hi, ws_lo = sb("ws_down", [F1, P]), sb("ws_up", [P, F1]), sb("ws_hi", [P, F1], F16), sb("ws_lo", [P, F1], F16)
        act_out, shared_out, hid = sb("act_out", [P, 2, N]), sb("shared_out", [F1, N]), sb("hid1", [P, 4, N])
        hid_hi, hid_lo = sb("hid_hi", [P, 4, N], F16), sb("hid_lo", [P, 4, N], F16)
        sumT, res = sb("sumT", [P, N]), sb("res", [P, N])
        shared_in, ws_high, ws_ready = sem("shared_in"), sem("ws_high"), sem("ws_ready")
        up_done, silu_ready, hid_ready, high_ready, low_ready, down_done = (sem("up_done"), sem("silu_ready"), sem("hid1_ready"), sem("high_ready"),
                                                                            sem("low_ready"), sem("down1_done"))
        sum_ready, sum_turned, res_ready, stored = sem("sum_ready"), sem("sum_turned"), sem("res_ready"), sem("stored")
        block = ctx.enter_context(nc.Block())
        psW, psU, psO, psR = [g.bank[0], g.bank[1]], [g.bank[2], g.bank[3], g.bank[6]], g.bank[4], g.bank[5]

        def first(i):
            return isinstance(i, int) and i == 0

        @block.sync
        def _(sp):
            sp.dma_start(ws_up[:, :], g.d_ws_up).then_inc(shared_in, 16)
            sp.dma_start(ws_down[:, :], g.d_ws_down).then_inc(shared_in, 16)
            with sp.Fori(0, NG) as i:
                sp.wait_ge(res_ready, i + 1)
                sp.dma_start(g.d_out[ds(i * LOTS, LOTS), :, :].rearrange("b p d -> p b d"),
                             res[:, :].rearrange("p (b d) -> p b d", b=LOTS)).then_inc(stored, 16)
            sp.wait_ge(stored, 16 * NG)

        @block.tensor
        def _(pe):
            T = nc.tensor
            ident = g.consts[:, C_ID:C_ID + P]

            def up(i, f):
                x_hi, x_lo, weight = (x[:, ds(i * LOTS, LOTS), :].rearrange("p b t -> p (b t)") for x in (g.XT_hi, g.XT_lo, g.CWT))
                if f < NFT:
                    if not (first(i) and f < 2):
                        pe.wait_ge(hid_ready, i * NFT + f - 1)
                    T.matmul(psW[f % 2][:, :], g.sel[:, P * f:P * f + P], weight, start=True, stop=True)
                if not (first(i) and f < 3):
                    wait_apart(g, pe, silu_ready, i * NS + f - 2)
                if f < NFT:
                    hi, lo, rows = g.W1_hi[:, P * f:P * f + P], g.W1_lo[:, P * f:P * f + P], P
                else:
                    if first(i):
                        pe.wait_ge(ws_ready, 2)
                    hi, lo, rows = ws_hi[:, :], ws_lo[:, :], F1
                T.matmul(psU[f % 3][0:rows, :], hi, x_hi, start=True, stop=False)
                T.matmul(psU[f % 3][0:rows, :], lo, x_hi, start=False, stop=False)
                T.matmul(psU[f % 3][0:rows, :], hi, x_lo, start=False, stop=True).then_inc(up_done, 1)

            def down(i, f):
                if f == 0 and not first(i):
                    pe.wait_ge(sum_ready, i)
                if f < NFT:
                    pe.wait_ge(low_ready, i * NFT + f + 1)
                    at = (NFT + f) * P
                    T.matmul(psO[:, :], g.W1_hi[:, at:at + P], hid_hi[:, f % 4, :], start=f == 0, stop=False)
                    T.matmul(psO[:, :], g.W1_lo[:, at:at + P], hid_hi[:, f % 4, :], start=False, stop=False)
                    T.matmul(psO[:, :], g.W1_hi[:, at:at + P], hid_lo[:, f % 4, :], start=False, stop=False).then_inc(down_done, 1)
                else:
                    pe.wait_ge(silu_ready, i * NS + NS)
                    T.matmul(psO[:, :], ws_down[:, :], shared_out[:, :], start=False, stop=True).then_inc(down_done, 1)

            def turn_sum(i):
                pe.wait_ge(sum_ready, i + 1)
                if not first(i):
                    pe.wait_ge(res_ready, i)
                for b in range(LOTS):
                    last = T.transpose(psR[:, P * b:P * b + P], sumT[:, P * b:P * b + P], ident)
                last.then_inc(sum_turned, 1)

            def group(i):
                for f in range(NS):
                    up(i, f)
                    if f >= LAG:
                        down(i, f - LAG)
                    elif not first(i):
                        down(i - 1, NS - LAG + f)
                    if f == TURN and not first(i):
                        turn_sum(i - 1)
            group(0)
            with pe.Fori(1, NG) as i:
                group(i)
            for f in range(NS - LAG, NS):
                down(NG - 1, f)
            turn_sum(NG - 1)

        @block.scalar
        def _(act):
            def silu(i, f):
                act.wait_ge(up_done, i * NS + f + 1)
                if f < NFT:
                    if not (first(i) and f < 2):
                        act.wait_ge(hid_ready, i * NFT + f - 1)
                    to, rows = act_out[:, f % 2, :], P
                else:
                    if not first(i):
                        act.wait_ge(down_done, i * NS)
                    to, rows = shared_out[:, :], F1
                nc.scalar.activation(to, psU[f % 3][0:rows, :], ACT.Silu, scale=1 / (X_SCALE * W_SCALE)).then_inc(silu_ready, 1)

            def high(i, f):
                act.wait_ge(hid_ready, i * NFT + f + 1)
                if not (first(i) and f < 4):
                    act.wait_ge(down_done, i * NS + f - 3 if f >= 4 else i * NS + f - 4)
                nc.scalar.activation(hid_hi[:, f % 4, :], hid[:, f % 4, :], ACT.Copy).then_inc(high_ready, 1)

            def copy_sum(i):
                act.wait_ge(down_done, i * NS + NS)
                if not first(i):
                    act.wait_ge(sum_turned, i)
                nc.scalar.activation(sumT[:, :], psO[:, :], ACT.Copy, scale=1 / (H_SCALE * W_SCALE)).then_inc(sum_ready, 1)

            def group(i):
                for f in range(NS):
                    silu(i, f)
                    if f >= 1:
                        high(i, f - 1)
                    if f == LAG - 1 and not first(i):
                        copy_sum(i - 1)
                    if f == LAG and first(i):
                        act.wait_ge(shared_in, 32)
                        nc.scalar.activation(ws_hi[:, :], ws_up[:, :], ACT.Copy, scale=W_SCALE).then_inc(ws_high, 1)
            group(0)
            with act.Fori(1, NG) as i:
                group(i)
            copy_sum(NG - 1)

        @block.vector
        def _(dve):
            V = nc.vector

            def multiply(i, f):
                dve.wait_ge(silu_ready, i * NS + f + 1)
                if not (first(i) and f < 4):
                    dve.wait_ge(low_ready, i * NFT + f - 3)
                V.tensor_tensor(hid[:, f % 4, :], psW[f % 2][:, :], act_out[:, f % 2, :], ALU.mult).then_inc(hid_ready, 1)

            def low(i, f):
                dve.wait_ge(high_ready, i * NFT + f + 1)
                V.tensor_tensor(hid_lo[:, f % 4, :], hid[:, f % 4, :], hid_hi[:, f % 4, :], ALU.subtract).then_inc(low_ready, 1)

            def add_x(i):
                dve.wait_ge(sum_turned, i + 1)
                if not first(i):
                    dve.wait_ge(stored, 16 * i)
                V.tensor_tensor(res[:, :], psR[:, :], g.X[:, ds(i * LOTS, LOTS), :].rearrange("p b d -> p (b d)"), ALU.add).then_inc(res_ready, 1)

            def group(i):
                for f in range(NS):
                    if f < NFT:
                        multiply(i, f)
                    if f >= 1:
                        low(i, f - 1)
                    if f == TURN + 1 and not first(i):
                        add_x(i - 1)
                    if f == LAG + 2 and first(i):
                        dve.wait_ge(ws_high, 1)
                        V.scalar_tensor_tensor(ws_lo[:, :], ws_up[:, :], W_SCALE, ws_hi[:, :], ALU.mult, ALU.subtract).then_inc(ws_ready, 1)
                        V.tensor_scalar(ws_down[:, :], ws_down[:, :], H_SCALE * W_SCALE, None, ALU.mult).then_inc(ws_ready, 1)
            group(0)
            with dve.Fori(1, NG) as i:
                group(i)
            add_x(NG - 1)


def program(nc, d, out):
    g = Shared()
    (g.d_x, g.d_ctx, g.d_consts, g.d_sel, g.d_ident16, g.d_cols, g.d_rows, g.d_w_ctx, g.d_w_small, g.d_w_up0, g.d_w_down0,
     g.d_b_row0, g.d_b_down0, g.d_w1, g.d_ws_up, g.d_ws_down) = d
    g.d_out = out
    g.xs = nc.dram_tensor("xs", (E0 * REGION + P, P), F32, kind="Internal").ap()
    g.ys = nc.dram_tensor("ys", (NT * P, P), F32, kind="Internal").ap()
    with ExitStack() as ctx:
        def sb(name, shape, dt=F32):
            return ctx.enter_context(nc.sbuf_tensor(name, shape, dt))

        g.apart = {eng: ctx.enter_context(nc.semaphore(f"apart_{i}")) for i, eng in enumerate((nc.gpsimd, nc.vector, nc.tensor))}
        g.X = sb("X", [P, NB, P])
        g.consts, g.cols, g.rows = sb("consts", [P, C_END]), sb("cols", [P, N_COL]), sb("rows", [P, R_END])
        g.w_small, g.ident16 = sb("w_small", [P, 584]), sb("ident16", [P, P], F16)
        g.zeros, g.mhalf = sb("zeros", [P, P]), sb("mhalf", [P, 4])
        g.run = sb("run", [P, E0])
        g.gate, g.slotf, g.slots = sb("gate", [P, NB, 2]), sb("slot_in_xs", [P, NB, 2]), sb("slots", [P, NB, 2], I32)
        g.table = sb("table", [P, 2 * NT], I32)
        g.psum = ctx.enter_context(nc.psum_tensor("psum", [P, 8, 512], F32))
        g.bank = [g.psum[:, i, :] for i in range(8)]
        with ExitStack() as late:
            def sb2(name, shape, dt=F32):
                return late.enter_context(nc.sbuf_tensor(name, shape, dt))
            g.V1, g.ctxT = sb2("V1", [P, NB, P]), sb2("ctxT", [P, NB, NK])
            with ExitStack() as layer0:
                def sb0(name, shape):
                    return layer0.enter_context(nc.sbuf_tensor(name, shape, F32))
                g.w_up0, g.w_down0, g.b_down0 = sb0("w_up0", [P, E0, 2 * F0]), sb0("w_down0", [P, E0, FC * P]), sb0("b_down0", [P, E0, P])
                g.weights0_in, g.biases0_in = (layer0.enter_context(nc.semaphore(n)) for n in ("weights0_in", "biases0_in"))
                with ExitStack() as early:
                    g.cstage, g.w_ctx = (early.enter_context(nc.sbuf_tensor(n, s, F32))
                                                 for n, s in (("cstage", [P, 2, P]), ("w_ctx", [P, 4 * P])))
                    g.vaug = early.enter_context(nc.sbuf_tensor("vaug", [P, 2, H, 2, HD + 1], F16))
                    g.affine = early.enter_context(nc.sbuf_tensor("affine", [P, 4 * P], F32))
                    g.split = early.enter_context(nc.sbuf_tensor("split", [P, 2, 2, H, 4, HD], F16))
                    load(nc, g)
                    attention0(nc, g)
                g.b_row0 = sb0("b_row0", [P, E0, 2 * F0])
                tables(nc, g)
                experts0(nc, g)
            g.XT_hi, g.XT_lo = sb2("XT_hi", [P, NB, P], F16), sb2("XT_lo", [P, NB, P], F16)
            g.W1_hi, g.W1_lo = sb2("W1_hi", [P, 2 * NFT * P], F16), sb2("W1_lo", [P, 2 * NFT * P], F16)
            g.CWT = sb2("CWT", [P, NB, P], F16)
            g.sel = sb2("sel", [P, NFT * P], F16)
            attention1(nc, g)
            experts1(nc, g)


def kernel(**inputs):
    import numpy as np
    import concourse.bacc as bacc
    from concourse.bass_utils import run_bass_kernel_spmd

    a = {k: np.asarray(v) for k, v in inputs.items()}
    c = np.zeros((P, C_END), np.float32)
    i, e = np.arange(P), np.arange(E0)
    c[:, C_ID:C_ID + P] = np.eye(P)
    c[:, C_TRI:C_TRI + P] = np.triu(np.ones((P, P)), 1)
    c[:, C_ONE:C_ONE + P] = 1
    c[:, C_MASK:C_MASK + HG] = (i[:, None] // HD) % HG == np.arange(HG)
    c[:, C_LT:C_LT + E0 * E0] = (e[None, :] < e[:, None]).reshape(-1)
    c[:, C_K:C_K + 2 * E0] = np.repeat([0, 1], E0)
    c[:, C_RUN:C_RUN + E0] = e * REGION
    c[:, C_P] = i
    c[:, C_J:C_J + NT] = np.arange(NT)
    sel = np.zeros((P, NFT * P), np.float16)
    spread = np.arange(E1)[:, None] == np.arange(NFT * P) // F1
    sel[:E1], sel[E1:] = spread * H_SCALE, spread * H_SCALE / 2048
    d = {
        "x": a["x"], "ctx": a["ctx_1024"], "consts": c, "sel": sel, "ident16": np.eye(P, dtype=np.float16),
        "cols": np.stack([a[n] for n in ("L0_xattn_gq", "L0_xattn_betq", "L0_xattn_gk", "L0_xattn_betk", "L0_xattn_gv", "L0_xattn_betv",
                                         "L1_xattn_bq", "L1_xattn_bk")], 1),
        "rows": np.concatenate([a[n] for n in ("L0_xattn_bq", "L0_xattn_bk", "L0_xattn_bv", "L1_xattn_bv", "L0_xattn_bo",
                                               "L1_ffn_expert_biases", "L1_xattn_bo", "L0_xattn_gq", "L0_xattn_gk",
                                               "L0_xattn_betq", "L0_xattn_betk")]),
        "w_ctx": np.concatenate([a["L0_xattn_Wq"], a["L0_xattn_Wk"], a["L0_xattn_Wv"], a["L1_xattn_Wv"].T], 1),
        "w_small": np.concatenate([a["L0_xattn_Wo"], a["L0_ffn_router_w"].T, a["L1_xattn_Wo"].T, a["L1_ffn_centroids"].T,
                                   a["L1_xattn_Wq"].T, a["L1_xattn_Wk"].T], 1),
        "w_up0": np.concatenate([a["L0_ffn_wg_w"], a["L0_ffn_w1_w"]], 1).transpose(2, 0, 1),
        "w_down0": a["L0_ffn_w2_w"].reshape(E0, P, FC, P).transpose(3, 0, 2, 1).reshape(P, E0, FC * P),
        "b_row0": np.concatenate([a["L0_ffn_wg_b"], a["L0_ffn_w1_b"]], 1).reshape(-1),
        "b_down0": a["L0_ffn_w2_b"].reshape(-1),
        "w1": np.concatenate([a["L1_ffn_W_up"].transpose(1, 0, 2).reshape(P, E1 * F1),
                              a["L1_ffn_W_down"].reshape(NFT, P, P).transpose(1, 0, 2).reshape(P, NFT * P)], 1),
        "ws_up": a["L1_ffn_Ws_up"], "ws_down": a["L1_ffn_Ws_down"],
    }
    nc = bacc.Bacc("TRN2", target_bir_lowering=False, num_devices=1)
    arrays, args = {}, []
    for name, v in d.items():
        v = np.ascontiguousarray(v)
        arrays["in_" + name] = v
        args.append(nc.dram_tensor("in_" + name, v.shape, mybir.dt.from_np(v.dtype), kind="ExternalInput").ap())
    out = nc.dram_tensor("out_x", (NB, P, P), F32, kind="ExternalOutput").ap()
    program(nc, args, out)
    r = run_bass_kernel_spmd(nc, [arrays], core_ids=[0])
    return r.results[0]["out_x"]
```
